# Optimizing a Trainium2 kernel written in Bass

```python
import numpy as np
import jax
import jax.numpy as jnp

def _softmax(x, axis=-1):
    return jax.nn.softmax(x, axis=axis)

def _gelu(x):
    return jax.nn.gelu(x, approximate=True)

def _silu(x):
    return jax.nn.silu(x)

def _sigmoid(x):
    return jax.nn.sigmoid(x)

def _layernorm(x, axis=-1, eps=1e-05):
    m = jnp.mean(x, axis=axis, keepdims=True)
    v = jnp.var(x, axis=axis, keepdims=True)
    return (x - m) / jnp.sqrt(v + eps)

def _scatter_add(tgt, idx, src, axis=0):
    return tgt.at[idx].add(src)

def _segment_sum(src, seg, n):
    return jax.ops.segment_sum(src, seg, n)
kernel_name = 'mk_gnn_resnorm_d4_gnn_r64_7b1b7d'

def setup_inputs(seed: int=0):
    np.random.seed(seed)
    _w = jnp.asarray

    def _rec_inputs():
        import jax
        import jax.numpy as jnp
        _gk = jax.random.key(seed)
        x = -0.000202 + 1 * jax.random.normal(jax.random.fold_in(_gk, 1), (50000, 128), jnp.float32)
        src = jax.random.randint(jax.random.fold_in(_gk, 2), (12500,), 0, 50000, jnp.int32)
        dst = jnp.minimum((50000 * jax.random.uniform(jax.random.fold_in(_gk, 3), (12500,)) ** 2.0).astype(jnp.int32), 49999)
        _o = jnp.argsort(dst, stable=True)
        src = src[_o]
        dst = dst[_o]
        edge_attr_128 = 2.93046e-05 + 1.00006 * jax.random.normal(jax.random.fold_in(_gk, 13), (12500, 128), jnp.float32)
        edge_weight = jax.random.uniform(jax.random.fold_in(_gk, 15), (12500,), jnp.float32, 0.0, 0.999998)
        return (x, src, dst, edge_attr_128, edge_weight)
    x, src, dst, edge_attr_128, edge_weight = _rec_inputs()

    def _L0_gnn_setup():
        import jax, jax.numpy as jnp
        import numpy as np
        N_NODES = 50000
        N_EDGES = 12500
        D = 128

        def _graphconv_both(x, src, dst, W, b, n_nodes):
            ones = jnp.ones_like(src, dtype=x.dtype)
            deg_out = jax.ops.segment_sum(ones, src, num_segments=n_nodes)
            deg_in = jax.ops.segment_sum(ones, dst, num_segments=n_nodes)
            norm_src = jax.lax.rsqrt(jnp.maximum(deg_out, 1.0))
            norm_dst = jax.lax.rsqrt(jnp.maximum(deg_in, 1.0))
            h = x * norm_src[:, None] @ W
            msgs = h[src]
            agg = jax.ops.segment_sum(msgs, dst, num_segments=n_nodes)
            return agg * norm_dst[:, None] + b
        key = jax.random.key(seed)
        k1, k2, k3, k4, k5, k6, k7, k8 = jax.random.split(key, 8)
        features = jax.random.normal(k1, (N_NODES, D), dtype=jnp.float32)
        src = jax.random.randint(k2, (N_EDGES,), 0, N_NODES)
        dst = jax.random.randint(k3, (N_EDGES,), 0, N_NODES)
        s = 1.0 / np.sqrt(D)
        W_conv = jax.random.uniform(k4, (D, D), jnp.float32, -s, s)
        b_conv = jnp.zeros((D,), jnp.float32)
        s2 = 1.0 / np.sqrt(2 * D)
        W_aggr = jax.random.uniform(k5, (2 * D, D), jnp.float32, -s2, s2)
        b_aggr = jax.random.uniform(k6, (D,), jnp.float32, -s2, s2)
        return {'features': features, 'src': src, 'dst': dst, 'W_conv': W_conv, 'b_conv': b_conv, 'W_aggr': W_aggr, 'b_aggr': b_aggr}
    _L0_gnn_all = _L0_gnn_setup()
    _L0_gnn_in = {k: v for k, v in _L0_gnn_all.items() if k in ('W_conv', 'b_conv', 'W_aggr', 'b_aggr')}
    del _L0_gnn_all

    def _L1_gnn_setup():
        import jax, jax.numpy as jnp
        import numpy as np
        N_NODES = 100000
        N_EDGES = 25000
        IN_FEATS = 128
        N_HIDDEN = 128
        key = jax.random.key(seed)
        k1, k2, k3, k4 = jax.random.split(key, 4)
        features = jax.random.normal(k1, (N_NODES, IN_FEATS), dtype=jnp.float32)
        src = jax.random.randint(k2, (N_EDGES,), 0, N_NODES, dtype=jnp.int32)
        dst = jax.random.randint(k3, (N_EDGES,), 0, N_NODES, dtype=jnp.int32)
        weight = jax.random.normal(k4, (IN_FEATS, N_HIDDEN), dtype=jnp.float32) * (1.0 / np.sqrt(IN_FEATS))
        bias = jnp.zeros((N_HIDDEN,), dtype=jnp.float32)
        return {'features': features, 'src': src, 'dst': dst, 'weight': weight, 'bias': bias}
    _L1_gnn_all = _L1_gnn_setup()
    _L1_gnn_in = {k: v for k, v in _L1_gnn_all.items() if k in ('weight', 'bias')}
    del _L1_gnn_all

    def _L2_gnn_setup():
        import jax, jax.numpy as jnp
        import numpy as np
        N_NODES = 50000
        N_EDGES = 10000
        C = 128
        BN_EPS = 0.0001

        def elu(x):
            return jnp.where(x > 0, x, jnp.expm1(x))

        def batchnorm_train(x, gamma, beta):
            mean = jnp.mean(x, axis=0)
            var = jnp.mean((x - mean) ** 2, axis=0)
            return gamma * (x - mean) * jax.lax.rsqrt(var + BN_EPS) + beta
        key = jax.random.key(seed)
        ks = jax.random.split(key, 8)
        x = jax.random.normal(ks[0], (N_NODES, C), dtype=jnp.float32)
        edge_index = jax.random.randint(ks[1], (2, N_EDGES), 0, N_NODES, dtype=jnp.int32)
        edge_attr = jax.random.normal(ks[2], (N_EDGES, C), dtype=jnp.float32)
        u = jax.random.normal(ks[3], (1, C), dtype=jnp.float32)
        batch = jnp.zeros((N_NODES,), dtype=jnp.int32)
        s1 = 1.0 / np.sqrt(2 * C)
        W1 = jax.random.uniform(ks[4], (2 * C, C), jnp.float32, -s1, s1)
        b1 = jnp.zeros((C,), jnp.float32)
        g1 = jnp.ones((C,), jnp.float32)
        be1 = jnp.zeros((C,), jnp.float32)
        W2 = jax.random.uniform(ks[5], (2 * C, C), jnp.float32, -s1, s1)
        b2 = jnp.zeros((C,), jnp.float32)
        g2 = jnp.ones((C,), jnp.float32)
        be2 = jnp.zeros((C,), jnp.float32)
        return dict(x=x, edge_index=edge_index, edge_attr=edge_attr, u=u, batch=batch, W1=W1, b1=b1, g1=g1, be1=be1, W2=W2, b2=b2, g2=g2, be2=be2)
    _L2_gnn_all = _L2_gnn_setup()
    _L2_gnn_in = {k: v for k, v in _L2_gnn_all.items() if k in ('u', 'W1', 'b1', 'g1', 'be1', 'W2', 'b2', 'g2', 'be2')}
    del _L2_gnn_all

    def _L3_gnn_setup():
        import jax, jax.numpy as jnp
        import numpy as np
        N_NODES = 100000
        N_EDGES = 10000
        DIM = 128
        key = jax.random.key(seed)
        k1, k2, k3, k4, k5 = jax.random.split(key, 5)
        x = jax.random.normal(k1, (N_NODES, DIM), dtype=jnp.float32)
        edge_index = jax.random.randint(k2, (2, N_EDGES), 0, N_NODES, dtype=jnp.int64)
        edge_weight = jax.random.uniform(k3, (N_EDGES,), dtype=jnp.float32)
        W = jax.random.normal(k4, (DIM, DIM), dtype=jnp.float32) * (1.0 / np.sqrt(DIM))
        b = jax.random.normal(k5, (DIM,), dtype=jnp.float32) * 0.01
        return {'x': x, 'edge_index': edge_index, 'edge_weight': edge_weight, 'W': W, 'b': b}
    _L3_gnn_all = _L3_gnn_setup()
    _L3_gnn_in = {k: v for k, v in _L3_gnn_all.items() if k in ('W', 'b')}
    del _L3_gnn_all
    return {'x': x, 'src': src, 'dst': dst, 'edge_attr_128': edge_attr_128, 'edge_weight': edge_weight, 'L0_gnn_W_conv': _L0_gnn_in['W_conv'], 'L0_gnn_b_conv': _L0_gnn_in['b_conv'], 'L0_gnn_W_aggr': _L0_gnn_in['W_aggr'], 'L0_gnn_b_aggr': _L0_gnn_in['b_aggr'], 'L1_gnn_weight': _L1_gnn_in['weight'], 'L1_gnn_bias': _L1_gnn_in['bias'], 'L2_gnn_u': _L2_gnn_in['u'], 'L2_gnn_W1': _L2_gnn_in['W1'], 'L2_gnn_b1': _L2_gnn_in['b1'], 'L2_gnn_g1': _L2_gnn_in['g1'], 'L2_gnn_be1': _L2_gnn_in['be1'], 'L2_gnn_W2': _L2_gnn_in['W2'], 'L2_gnn_b2': _L2_gnn_in['b2'], 'L2_gnn_g2': _L2_gnn_in['g2'], 'L2_gnn_be2': _L2_gnn_in['be2'], 'L3_gnn_W': _L3_gnn_in['W'], 'L3_gnn_b': _L3_gnn_in['b']}

def reference(x, src, dst, edge_attr_128, edge_weight, L0_gnn_W_conv, L0_gnn_b_conv, L0_gnn_W_aggr, L0_gnn_b_aggr, L1_gnn_weight, L1_gnn_bias, L2_gnn_u, L2_gnn_W1, L2_gnn_b1, L2_gnn_g1, L2_gnn_be1, L2_gnn_W2, L2_gnn_b2, L2_gnn_g2, L2_gnn_be2, L3_gnn_W, L3_gnn_b):
    import jax
    import jax.numpy as jnp

    def _L0_gnn_ref(features, src, dst, W_conv, b_conv, W_aggr, b_aggr):
        import jax, jax.numpy as jnp
        import numpy as np
        N_NODES = 50000
        N_EDGES = 12500
        D = 128

        def _graphconv_both(x, src, dst, W, b, n_nodes):
            ones = jnp.ones_like(src, dtype=x.dtype)
            deg_out = jax.ops.segment_sum(ones, src, num_segments=n_nodes)
            deg_in = jax.ops.segment_sum(ones, dst, num_segments=n_nodes)
            norm_src = jax.lax.rsqrt(jnp.maximum(deg_out, 1.0))
            norm_dst = jax.lax.rsqrt(jnp.maximum(deg_in, 1.0))
            h = x * norm_src[:, None] @ W
            msgs = h[src]
            agg = jax.ops.segment_sum(msgs, dst, num_segments=n_nodes)
            return agg * norm_dst[:, None] + b
        x = _graphconv_both(features, src, dst, W_conv, b_conv, N_NODES)
        x = jnp.concatenate([x, features], axis=1)
        return x @ W_aggr + b_aggr

    def _L1_gnn_ref(features, src, dst, weight, bias):
        import jax, jax.numpy as jnp
        import numpy as np
        N_NODES = 100000
        N_EDGES = 25000
        IN_FEATS = 128
        N_HIDDEN = 128
        "DGL GraphConv with norm='both' + relu activation.\n            out = relu( D_dst^{-1/2} * segment_sum( (D_src^{-1/2} x)[src] -> dst ) @ W + b )\n            "
        n = features.shape[0]
        ones_e = jnp.ones(src.shape[0], dtype=features.dtype)
        deg_out = jnp.clip(jax.ops.segment_sum(ones_e, src, num_segments=n), 1.0)
        deg_in = jnp.clip(jax.ops.segment_sum(ones_e, dst, num_segments=n), 1.0)
        h = features * jax.lax.rsqrt(deg_out)[:, None]
        agg = jax.ops.segment_sum(h[src], dst, num_segments=n)
        agg = agg * jax.lax.rsqrt(deg_in)[:, None]
        out = agg @ weight + bias
        return jax.nn.relu(out)

    def _L2_gnn_ref(x, edge_index, edge_attr, u, batch, W1, b1, g1, be1, W2, b2, g2, be2):
        import jax, jax.numpy as jnp
        import numpy as np
        N_NODES = 50000
        N_EDGES = 10000
        C = 128
        BN_EPS = 0.0001

        def elu(x):
            return jnp.where(x > 0, x, jnp.expm1(x))

        def batchnorm_train(x, gamma, beta):
            mean = jnp.mean(x, axis=0)
            var = jnp.mean((x - mean) ** 2, axis=0)
            return gamma * (x - mean) * jax.lax.rsqrt(var + BN_EPS) + beta
        row, col = (edge_index[0], edge_index[1])
        h = jnp.concatenate([x[row], edge_attr], axis=1)
        h = elu(batchnorm_train(h @ W1 + b1, g1, be1))
        sums = jax.ops.segment_sum(h, col, num_segments=x.shape[0])
        cnt = jax.ops.segment_sum(jnp.ones((h.shape[0],), h.dtype), col, num_segments=x.shape[0])
        agg = sums / jnp.maximum(cnt, 1.0)[:, None]
        z = jnp.concatenate([x, agg], axis=1)
        return elu(batchnorm_train(z @ W2 + b2, g2, be2))

    def _L3_gnn_ref(x, edge_index, edge_weight, W, b):
        import jax, jax.numpy as jnp
        import numpy as np
        N_NODES = 100000
        N_EDGES = 10000
        DIM = 128
        row, col = (edge_index[0], edge_index[1])
        msgs = edge_weight[:, None] * x[row]
        agg = jax.ops.segment_sum(msgs, col, num_segments=x.shape[0])
        return agg @ W.T + b
    edge_index = jnp.stack([src, dst])
    batch0 = jnp.zeros((50000,), jnp.int32)
    x = _layernorm(x + _L0_gnn_ref(x, src, dst, L0_gnn_W_conv, L0_gnn_b_conv, L0_gnn_W_aggr, L0_gnn_b_aggr), axis=-1)
    x = _layernorm(x + _L1_gnn_ref(x, src, dst, L1_gnn_weight, L1_gnn_bias), axis=-1)
    x = _layernorm(x + _L2_gnn_ref(x, edge_index, edge_attr_128, L2_gnn_u, batch0, L2_gnn_W1, L2_gnn_b1, L2_gnn_g1, L2_gnn_be1, L2_gnn_W2, L2_gnn_b2, L2_gnn_g2, L2_gnn_be2), axis=-1)
    x = _layernorm(x + _L3_gnn_ref(x, edge_index, edge_weight, L3_gnn_W, L3_gnn_b), axis=-1)
    return x

_drawn_inputs = setup_inputs


def setup_inputs(seed=0):
    import zlib

    import numpy as np

    out = dict(_drawn_inputs(seed))
    spreads = {'L0_gnn_b_conv': (0.0, 0.1),
     'L1_gnn_bias': (0.0, 0.1),
     'L2_gnn_b1': (0.0, 0.8),
     'L2_gnn_g1': (1.0, 0.2),
     'L2_gnn_be1': (0.0, 0.437),
     'L2_gnn_b2': (0.0, 0.8),
     'L2_gnn_g2': (1.0, 0.2),
     'L2_gnn_be2': (0.0, 0.1)}
    factors = {'L3_gnn_b': 5.705}
    for name, (base, spread) in spreads.items():
        noise = np.random.default_rng([zlib.crc32(name.encode()), seed]).standard_normal(out[name].shape)
        drawn = base * np.exp(spread * noise) if base else spread * noise
        out[name] = jnp.asarray(drawn.astype(out[name].dtype))
    for name, factor in factors.items():
        out[name] = (out[name] * factor).astype(out[name].dtype)
    return out
```

```python
import numpy as np
import concourse.bass as bass
from concourse import mybir
from contextlib import ExitStack

P = 128
D = 128
G = 7
NODES, EDGES = 50000, 12500
NT = 392
NG = NT // G
NPAD = P * NT
ET = 98
EG = ET // G
EPAD = ET * P
LASTROWS = EDGES - (ET - 1) * P
CW = 132
ZERO_ROW = EPAD - 1
NOWHERE = 100000.0
LN_EPS, BN_EPS = 1e-5, 1e-4
SEED = float(0x5F3759DF)
NEWTON = 3
ROUND = float(3 << 22)


class Step:

    def __init__(self, sem, lead=0, base=0):
        self.sem, self.lead, self.base = sem, lead, base

    def done(self, q):
        return q + (1 + self.lead + self.base)

    def prev(self, q):
        return q + (self.lead + self.base)

    def prev2(self, q):
        return q + (self.lead + self.base - 1)


class Mark:

    def __init__(self, sem, at):
        self.sem, self.at = sem, at

    def passed(self, eng):
        eng.wait_ge(self.sem, self.at)


class Chain:

    def __init__(self, sem, per, base=0):
        self.sem, self.per, self.base = sem, per, base

    def at(self, q, j):
        return q * self.per + (self.base * self.per + j)

    def done(self, q):
        return self.at(q, self.per)

    def prev(self, q):
        return self.at(q, 0)


def build(nc, x, xT, edge_attr, dst1, src, weight, W_conv_T, b_conv, W_aggr, b_aggr, W_l1, b_l1,
          W1, b1, g1, be1, W2, b2, g2, be2, W3_T, b3, out):
    f32, i32, f16, bf16 = mybir.dt.float32, mybir.dt.int32, mybir.dt.float16, mybir.dt.bfloat16
    ALU = mybir.AluOpType
    ACT = mybir.ActivationFunctionType
    AX = mybir.AxisListType

    ctx = ExitStack()
    with ctx:
        def sb(name, shape, dt=f32):
            return ctx.enter_context(nc.sbuf_tensor(name, shape, dt))

        def sem(name):
            return ctx.enter_context(nc.semaphore(name))

        def step(name, lead=0):
            return Step(sem(name), lead)

        def dram(name, shape, dt=f32):
            return nc.dram_tensor(name, shape, dt, kind="Internal").ap()

        def scratch(i):
            return WK[:, i, :].rearrange("p (k f) -> p k f", k=G)

        x2_dram = dram("x2_dram", (NG + 1, P, G * D))
        lookup_dram = dram("lookup_dram", (NPAD, 2))
        table = [dram("sums0", (EPAD, CW))] + [dram(f"sums{n}", (EPAD, D)) for n in (1, 2, 3)]
        xd_dram = dram("xd_dram", (EG, P, G * D))
        zd_dram = dram("zd_dram", (EG, P, G * D))

        YS = sb("YS", [P, ET, D])
        Z = sb("Z", [P, ET, D])
        EQ = sb("EQ", [P, ET, P], bf16)
        WK = sb("WK", [P, 12, G * D])
        XM = sb("XM", [P, G, CW])
        PT = sb("PT", [P, 2, G, CW])
        GS = sb("GS", [P, 2, G, CW])
        ident = sb("ident", [P, P])
        ones = sb("ones", [P, P])
        wM = sb("wM", [P, D]); wA = sb("wA", [P, D]); wL = sb("wL", [P, D])
        w1a = sb("w1a", [P, D]); w1b = sb("w1b", [P, D])
        w2a = sb("w2a", [P, D]); w2b = sb("w2b", [P, D]); w2s = sb("w2s", [P, D])
        w3 = sb("w3", [P, D])
        blB = sb("blB", [P, D]); cB = sb("cB", [P, D]); b3B = sb("b3B", [P, D])
        bn1B = sb("bn1B", [P, 2, D]); bn2B = sb("bn2B", [P, 2, D])
        b0row = sb("b0row", [1, D])
        rows = sb("rows", [1, 7, D])
        bnrow = sb("bnrow", [1, 2, D])
        bconv = sb("bconv", [P, 1])
        eps_ln = sb("eps_ln", [P, 1])
        KD = sb("KD", [P, ET]); WE = sb("WE", [P, ET])
        NS = sb("NS", [P, ET]); ND = sb("ND", [P, ET]); RC = sb("RC", [P, ET]); RCD = sb("RCD", [P, ET])
        REP = sb("REP", [P, ET]); REAL = sb("REAL", [P, ET])
        SRCI = sb("SRCI", [P, ET], i32); DSTI = sb("DSTI", [P, ET], i32)
        POSI = sb("POSI", [P, ET], i32); OUTI = sb("OUTI", [P, ET], i32)
        IX = sb("IX", [P, 2, G], i32)
        MASK = sb("MASK", [P, NT])
        Cmat = sb("Cmat", [P, ET])
        REPI = sb("REPI", [P, 1], i32)
        FR = sb("FR", [P, CW]); LR = sb("LR", [P, CW])
        ZH = sb("ZH", [P, 512], f16)
        sc = sb("sc", [P, 8])
        small = sb("small", [P, 26, G])
        SS1, SD1, R1, SS2, SD2, R2, RM, SS3, SD3, R3, NDD, EM, CS, RW = (small[:, n, :] for n in range(14))
        RV, RS, RT = ([small[:, m + n, :] for n in range(4)] for m in (14, 18, 22))
        ST = sb("ST", [P, 4, G, 6])
        MV = sb("MV", [P, 4, G, 2])
        MVS, MV2, MV3, MVD = (MV[:, n, :, :] for n in range(4))
        acc = ctx.enter_context(nc.psum_tensor("acc", [P, 2, 512], f32))
        pX = ctx.enter_context(nc.psum_tensor("pX", [P, 1024], f32))
        pY = ctx.enter_context(nc.psum_tensor("pY", [P, 1024], f32))
        pZ = ctx.enter_context(nc.psum_tensor("pZ", [P, 1024], f32))
        pW = acc[:, :, :].rearrange("p a c -> p (a c)")

        EQF, M, WAT, AT2 = 6, 7, 8, 9

        def tiles(t):
            return t[:, 0:G * D].rearrange("p (k f) -> p k f", k=G)

        pXt, pYt, pZt, pWt = tiles(pX), tiles(pY), tiles(pZ), tiles(pW)

        kt = WK[0:ET, 0, 0:4 * P].rearrange("t (a e) -> t a e", a=4)
        kti = WK[0:ET, 1, 0:4 * P].bitcast(i32).rearrange("t (a e) -> t a e", a=4)
        wk_a, wk_b = WK[:, 2, :], WK[:, 3, :]
        PD, TD, PS_, TS_ = (WK[:, 4, n * ET:(n + 1) * ET] for n in range(4))
        KP, KS = WK[:, 3, 256:256 + ET], WK[:, 3, 384:384 + ET]
        RR = RCD[:, :]
        LK = WK[:, 6, 0:2 * ET].rearrange("p (t c) -> p t c", c=2)
        ones_t = WK[:, 6, 2 * ET:2 * ET + NT]
        rt = WK[0:1, 6, 0:6 * D].rearrange("a (r f) -> a r f", r=6)
        GM, GP = WK[:, 7, 0:D + 1], WK[:, 7, 256:256 + D]
        iota_i = WK[:, 5, 0:NT].bitcast(i32)
        iota_h = WK[:, 5, NT:NT + NT // 2].bitcast(f16)
        OHP = WK[:, 10, :].bitcast(f16)[:, 0:4 * P].rearrange("p (a b c) -> p a b c", a=2, b=2)
        OHT = WK[:, 11, :].bitcast(f16)[:, 0:4 * NT].rearrange("p (a b c) -> p a b c", a=2, b=2)
        deg = WK[:, 7, 0:NT]; degout = WK[:, 8, 0:NT]
        cum = WK[:, 7, NT:2 * NT]; posn = WK[:, 8, NT:2 * NT]
        tabs = WK[:, 9, 0:2 * NT].rearrange("p (t c) -> p t c", c=2)
        tri = WK[:, 6, 0:P]

        carried = sem("waits_carried")
        consts = sem("constants_made")
        s_keys, s_wts, s_w32 = sem("keys_loaded"), sem("weights_loaded"), sem("previous_keys_loaded")
        vlink, glink = sem("vector_link"), sem("gpsimd_link")

        def marks(name, n):
            s_ = sem(name)
            return [Mark(s_, m + 1) for m in range(n)]

        (zeros, keys_f, idx_ready, comp_ready, lk_diag, cmask0, hist_out, rowtot, tab_ready, ns_in, ns_ready,
         bn_v1, bn_t1, bn_done1, gr, gr_p, bn_v2, bn_t2, bn_done2) = marks("vector_events", 19)
        (comp_mm, keys_T, lk_mm, rowoff, bn_b1, gr_mm, gr_q, bn_b2) = marks("tensor_events", 8)
        (ns_sq, bn_a1, bn_a2) = marks("scalar_events", 3)
        (cmask, mask1) = marks("gpsimd_events", 2)
        oh, ohmm = step("onehots_built"), step("onehots_counted", 1)
        zgroup = sem("zero_group_stored")
        tab_stored = sem("lookup_stored")
        rk_l, eq_built = [sem("rowkeys0"), sem("rowkeys1")], step("eq_built", 1)
        p1 = {k: step("p1_" + k, 1 if k in ("mm", "xm") else 0) for k in
              ("mm", "sq", "sqrt", "r", "s", "sq2", "sqrt2", "r2", "rm", "x2", "xm", "gram")}
        p1_x, p1_st = [sem("nodes_x0"), sem("nodes_x1")], [sem("p1_stored0"), sem("p1_stored1")]
        ag = {k: step("agg_" + k) for k in ("eqf", "m", "mmT", "aT", "mmP", "p", "cnt")}
        ag_st = [sem("agg_stored0"), sem("agg_stored1")]
        bd_l, bd_mm, bd_r, bd_sc = sem("boundary_rows_loaded"), sem("boundary_product"), sem("boundary_rows_ready"), sem("boundary_scattered")
        edge_sems, counted = {}, {}

        def edge_steps(*names):
            out_ = {}
            for k in names:
                if k not in edge_sems:
                    edge_sems[k], counted[k] = sem("edges_" + k), 0
                out_[k] = Step(edge_sems[k], 1 if k in ("raw", "y", "s", "eaT", "T", "z") else 0, counted[k])
                counted[k] += EG
            return out_

        xs = edge_steps("ix", "T", "aT", "mm", "raw", "ys")
        lk = edge_steps("ix")
        s1 = edge_steps("ix", "c", "rc", "nd", "y", "sq", "sqrt", "r", "x1")
        s2 = edge_steps("ix", "a", "a2", "s", "bn", "ag", "sqrt", "r", "x2", "keep", "eaT", "eaTc", "xT", "xTc", "z1", "zc", "sq", "stat", "em")
        d1 = edge_steps("ix", "T", "aT", "mm", "c", "rc", "nd", "y", "sq", "sqrt", "r", "x1", "a", "s", "bn", "ag", "sqrt2", "r2", "x2")
        s4 = edge_steps("ix", "cp", "T", "aT", "mm", "z")
        h1 = edge_steps("v1", "v", "exp", "t", "s1")
        s5 = edge_steps("v1", "v", "exp", "t", "s1", "s", "bn", "ag", "rw")
        d3 = edge_steps("v1", "v", "exp", "t", "s", "bn", "ag", "u", "u2", "bn2", "ag2", "o")
        lk_use = step("lookup_used", 1)
        gathered = [sem("gathered0"), sem("gathered1")]
        s2_ea = [sem("edge_features0"), sem("edge_features1")]
        bn_v, bn_t, bn_done, bn_b, bn_a = (bn_v1, bn_v2), (bn_t1, bn_t2), (bn_done1, bn_done2), (bn_b1, bn_b2), (bn_a1, bn_a2)
        d1_p, d1_st = sem("d1_sums"), sem("d1_stored")
        d2 = {k: step("d2_" + k, 1 if k in ("z", "T") else 0) for k in ("T", "aT", "mm", "z", "sq", "stat", "em")}
        d2_x, d2_p, d2_st = [sem("d2_x0"), sem("d2_x1")], [sem("d2_p0"), sem("d2_p1")], [sem("d2_stored0"), sem("d2_stored1")]
        p2 = {k: step("p2_" + k, 1 if k == "t" else 0) for k in ("T", "xT", "exp", "t", "bn", "ag", "u", "bn2", "ag2", "o")}
        for k in ("mm", "s"):
            p2[k] = Step(p1[k].sem, p1[k].lead, NG + 1)
        seed_sems = [sem(f"rsqrt_seed{n}") for n in range(4)]
        newton_sems = [sem(f"rsqrt_newton{n}") for n in range(4)]

        def rsqrt_steps(n, base=0):
            return Chain(seed_sems[n], 3, base), Chain(newton_sems[n], 4 * NEWTON, base)

        s5["seed"], s5["r"] = rsqrt_steps(0)
        d3["seed"], d3["r"] = rsqrt_steps(0, EG)
        p2["seed"], p2["r"] = rsqrt_steps(1)
        p2["seed2"], p2["r2"] = rsqrt_steps(2)
        d3["seed2"], d3["r2"] = rsqrt_steps(3)
        p2_x, p2_st = [sem("p2_x0"), sem("p2_x1")], [sem("p2_stored0"), sem("p2_stored1")]
        d3_l = sem("d3_loaded")
        fin = sem("outputs_scattered")

        block = ctx.enter_context(nc.Block())

        def wait(eng, st, value):
            eng.wait_ge(st.sem if isinstance(st, (Step, Chain)) else st, value)

        def hold(eng):
            eng.sem_inc(carried, 1)

        def span(q):
            return bass.ds(q * G, G)

        @block.sync
        def _(sp):
            sp.dma_start(kti[:, 0, :], dst1[1:1 + EPAD].rearrange("(t p) -> t p", p=P)).then_inc(s_keys, 16)
            sp.dma_start(kti[:, 1, :], dst1[0:EPAD].rearrange("(t p) -> t p", p=P)).then_inc(s_keys, 16)
            sp.dma_start(kti[:, 2, :], src.rearrange("(t p) -> t p", p=P)).then_inc(s_keys, 16)
            sp.dma_start(kt[:, 3, :], weight.rearrange("(t p) -> t p", p=P)).then_inc(s_keys, 16)
            for to, of in ((wk_a[:, 0:D], W_conv_T), (wk_a[:, D:2 * D], W_aggr[0:D, :]), (wM, W_aggr[D:2 * D, :]),
                           (wL, W_l1), (w1a, W1[0:D, :]), (w1b, W1[D:2 * D, :]), (w2a, W2[0:D, :]),
                           (w2b, W2[D:2 * D, :]), (w3, W3_T)):
                sp.dma_start(to[:, :] if to.shape[1] == D else to, of).then_inc(s_wts, 16)
            sp.dma_start(blB[:, :], b_l1.rearrange("(a n) -> a n", a=1).broadcast_to([P, D])).then_inc(s_wts, 16)
            sp.dma_start(b3B[:, :], b3.rearrange("(a n) -> a n", a=1).broadcast_to([P, D])).then_inc(s_wts, 16)
            for n, r in enumerate((b1, g1, be1, b2, g2, be2, b_aggr)):
                sp.dma_start(rows[:, n, :], r.rearrange("(a n) -> a n", a=1)).then_inc(s_wts, 16)
            sp.dma_start(bconv[:, :], b_conv.rearrange("(n a) -> n a", a=1)).then_inc(s_wts, 16)

            def p1_load(q, u):
                wait(sp, p1["mm"], p1["mm"].prev2(q))
                sp.dma_start(WK[:, u, :], xT[bass.ds(q, 1), :, :].rearrange("a p c -> p (a c)")).then_inc(p1_x[u], 16)

            def p1_store(q, u):
                wait(sp, p1["x2"], p1["x2"].done(q))
                sp.dma_start(x2_dram[bass.ds(q, 1), :, :].rearrange("a p c -> p (a c)"), WK[:, 4 + u, :]).then_inc(p1_st[u], 16)

            def table_view(n, q, width):
                return table[n].rearrange("(t p) w -> p t w", p=P)[:, span(q), 0:width]

            def agg_store(n, q, i, u, width):
                a = n * EG + q
                wait(sp, ag["p"], ag["p"].done(a))
                sp.dma_start(table_view(n, q, width), PT[:, u, :, 0:width]).then_inc(ag_st[u], 16)

            def boundary(n, width):
                half = (n + 1) * EG // 2 * 16
                sp.wait_ge(ag_st[0], half)
                sp.wait_ge(ag_st[1], half)
                if n:
                    sp.wait_ge(bd_sc, 16 * n)
                t = table[n].rearrange("(t p) w -> t p w", p=P)
                sp.dma_start(FR[0:ET, 0:width], t[:, 0, :]).then_inc(bd_l, 16)
                sp.dma_start(LR[0:ET, 0:width], t[:, P - 1, :]).then_inc(bd_l, 16)

            zeros.passed(sp)
            sp.dma_start(x2_dram[NG, :, :].rearrange("p (k f) -> p k f", k=G), XM[:, :, 0:D]).then_inc(zgroup, 16)
            sp.wait_ge(zgroup, 16)
            tab_ready.passed(sp)
            sp.dma_start(lookup_dram.rearrange("(p t) c -> p t c", p=P), tabs).then_inc(tab_stored, 16)
            sp.wait_ge(tab_stored, 16)
            p1_load(0, 0)
            with sp.Fori(0, EG // 2) as i:
                for u in (0, 1):
                    q = i * 2 + u
                    wait(sp, eq_built, eq_built.prev2(q))
                    sp.dma_start(WK[:, 10 + u, :].bitcast(i32),
                                 dst1[bass.ds(q * (G * P) + 1, G * P)].rearrange("(a n) -> a n", a=1).broadcast_to([P, G * P]))\
                        .then_inc(rk_l[u], 16)
                    p1_load(q + 1, 1 - u)
                    p1_store(q, u)
            with sp.Fori(0, EG // 2) as i:
                for u in (0, 1):
                    q = i * 2 + u
                    p1_load(q + (EG + 1), 1 - u)
                    p1_store(q + EG, u)
                    agg_store(0, q, i, u, CW)
            boundary(0, CW)
            with sp.Fori(0, EG // 2) as i:
                for u in (0, 1):
                    q = i * 2 + u
                    p1_load(q + (2 * EG + 1), 1 - u)
                    p1_store(q + 2 * EG, u)
                    agg_store(1, q, i, u, D)
            boundary(1, D)
            with sp.Fori(0, EG // 2) as i:
                for u in (0, 1):
                    q = i * 2 + u
                    wait(sp, s2["eaT"], s2["eaT"].prev2(q))
                    sp.dma_start(scratch(10 + u), edge_attr.rearrange("(t p) f -> p t f", p=P)[:, span(q), :]).then_inc(s2_ea[u], 16)
                    p1_load(q + (3 * EG + 1), 1 - u)
                    p1_store(q + 3 * EG, u)
            sp.wait_ge(bd_sc, 32)
            wait(sp, p1["gram"], p1["gram"].prev(NG))
            with sp.Fori(0, EG // 2) as i:
                for u in (0, 1):
                    q = i * 2 + u
                    wait(sp, d1["s"], d1["s"].prev(q))
                    sp.dma_start(XM[:, :, :], table_view(0, q, CW)).then_inc(d1_p, 16)
                    sp.dma_start(scratch(1), table_view(1, q, D)).then_inc(d1_p, 16)
                    agg_store(2, q, i, u, D)
                    wait(sp, d1["x2"], d1["x2"].done(q))
                    sp.dma_start(xd_dram[bass.ds(q, 1), :, :].rearrange("a p c -> p (a c)"), WK[:, 3, :]).then_inc(d1_st, 16)
            boundary(2, D)
            sp.wait_ge(d1_st, 16 * EG)
            sp.wait_ge(bd_sc, 48)
            with sp.Fori(0, EG // 2) as i:
                for u in (0, 1):
                    q = i * 2 + u
                    wait(sp, d2["T"], d2["T"].prev2(q))
                    sp.dma_start(WK[:, u, :], xd_dram[bass.ds(q, 1), :, :].rearrange("a p c -> p (a c)")).then_inc(d2_x[u], 16)
                    wait(sp, d2["z"], d2["z"].prev2(q))
                    sp.dma_start(scratch(3 + u), table_view(2, q, D)).then_inc(d2_p[u], 16)
                    wait(sp, d2["z"], d2["z"].done(q))
                    sp.dma_start(zd_dram[bass.ds(q, 1), :, :].rearrange("a p c -> p (a c)"), WK[:, 5 if u == 0 else 10, :]).then_inc(d2_st[u], 16)

            def p2_load(q, u):
                wait(sp, p2["t"], p2["t"].prev2(q))
                sp.dma_start(WK[:, u, :], x2_dram[bass.ds(q, 1), :, :].rearrange("a p c -> p (a c)")).then_inc(p2_x[u], 16)

            def p2_store(q, u):
                wait(sp, p2["o"], p2["o"].done(q))
                sp.dma_start(out.rearrange("(p t) f -> p t f", p=P)[:, span(q), :], GS[:, u, :, 0:D]).then_inc(p2_st[u], 16)

            sp.wait_ge(p1_st[0], 16 * NG // 2)
            sp.wait_ge(p1_st[1], 16 * NG // 2)
            sp.wait_ge(d2_st[0], 16 * EG // 2)
            sp.wait_ge(d2_st[1], 16 * EG // 2)
            wait(sp, d2["stat"], d2["stat"].prev(EG))
            p2_load(0, 0)
            with sp.Fori(0, EG // 2) as i:
                for u in (0, 1):
                    q = i * 2 + u
                    p2_load(q + 1, 1 - u)
                    agg_store(3, q, i, u, D)
                    p2_store(q, u)
            boundary(3, D)
            sp.wait_ge(bd_sc, 64)
            with sp.Fori(0, EG // 2) as i:
                for u in (0, 1):
                    q = i * 2 + u
                    wait(sp, d3["u2"], d3["u2"].prev(q))
                    sp.dma_start(WK[:, 6, :], xd_dram[bass.ds(q, 1), :, :].rearrange("a p c -> p (a c)")).then_inc(d3_l, 16)
                    sp.dma_start(WK[:, 7, :], zd_dram[bass.ds(q, 1), :, :].rearrange("a p c -> p (a c)")).then_inc(d3_l, 16)
                    sp.dma_start(scratch(8), table_view(3, q, D)).then_inc(d3_l, 16)
                    for n in range(3):
                        r = q * 3 + (EG + n)
                        v = (u + n) % 2
                        p2_load(r + 1, 1 - v)
                        p2_store(r, v)
            sp.wait_ge(p2_st[0], 16 * NG // 2)
            sp.wait_ge(p2_st[1], 16 * NG // 2)
            sp.wait_ge(p2_x[0], 16 * (NG // 2 + 1))
            sp.wait_ge(fin, 16 * ET)

        @block.gpsimd
        def _(pool):
            pool.memset(ident[:, :], 0.0).then_inc(glink, 1)
            pool.memset(tri, 1.0).then_inc(glink, 1)
            pool.iota(iota_i, [[1, NT]], base=0, channel_multiplier=0).then_inc(consts, 1)
            pool.iota(sc[:, 0:1].bitcast(i32), [[0, 1]], base=P, channel_multiplier=P).then_inc(consts, 1)
            pool.wait_ge(glink, 2)
            pool.affine_select(out=ident[:, :], in_=ident[:, :], compare_op=ALU.not_equal, fill=1.0,
                               base=0, pattern=[[-1, P]], channel_multiplier=1).then_inc(consts, 1)
            pool.affine_select(out=tri, in_=tri, compare_op=ALU.is_gt, fill=0.0,
                               base=0, pattern=[[1, P]], channel_multiplier=-1).then_inc(consts, 1)

            def gather_group(q, u, ix, index, rows_of, width):
                hold(pool)
                pool.tensor_copy(IX[:, u, :], index[:, span(q)]).then_inc(ix.sem, 1)
                wait(pool, ix, ix.done(q))
                hold(pool)
                for k in range(G):
                    pool.indirect_dma_start(GS[:, u, k, 0:width], None, rows_of,
                                            bass.IndirectOffsetOnAxis(ap=IX[:, u, k:k + 1], axis=0)).then_inc(gathered[u], 16)

            idx_ready.passed(pool)
            with pool.Fori(0, EG // 2) as i:
                for u in (0, 1):
                    q = i * 2 + u
                    wait(pool, xs["raw"], xs["raw"].prev2(q))
                    gather_group(q, u, xs["ix"], SRCI, x, D)
            cmask0.passed(pool)
            pool.affine_select(out=Cmat[0:ET, :], in_=Cmat[0:ET, :], compare_op=ALU.is_gt, fill=0.0,
                               base=0, pattern=[[-1, ET]], channel_multiplier=1).then_inc(cmask.sem, 1)
            tab_ready.passed(pool)
            pool.affine_select(out=MASK[:, :], in_=MASK[:, :], compare_op=ALU.is_gt, fill=0.0,
                               base=NODES, pattern=[[-1, NT]], channel_multiplier=-NT).then_inc(mask1.sem, 1)
            pool.wait_ge(tab_stored, 16)
            with pool.Fori(0, EG // 2) as i:
                for u in (0, 1):
                    q = i * 2 + u
                    wait(pool, lk_use, lk_use.prev2(q))
                    gather_group(q, u, lk["ix"], SRCI, lookup_dram, 2)

            def scatter_boundary(n, width):
                pool.wait_ge(bd_r, n + 1)
                pool.indirect_dma_start(table[n], bass.IndirectOffsetOnAxis(ap=REPI[0:ET, 0:1], axis=0), LR[0:ET, 0:width], None,
                                        bounds_check=EPAD - 1, oob_is_err=False).then_inc(bd_sc, 16)
                pool.wait_ge(bd_sc, 16 * (n + 1))

            ns_ready.passed(pool)
            scatter_boundary(0, CW)
            with pool.Fori(0, EG // 2) as i:
                for u in (0, 1):
                    q = i * 2 + u
                    wait(pool, s1["y"], s1["y"].prev2(q))
                    gather_group(q, u, s1["ix"], POSI, table[0], CW)
            scatter_boundary(1, D)
            with pool.Fori(0, EG // 2) as i:
                for u in (0, 1):
                    q = i * 2 + u
                    wait(pool, s2["s"], s2["s"].prev2(q))
                    gather_group(q, u, s2["ix"], POSI, table[1], D)
            wait(pool, s2["s"], s2["s"].prev(EG))
            with pool.Fori(0, EG // 2) as i:
                for u in (0, 1):
                    q = i * 2 + u
                    wait(pool, d1["T"], d1["T"].prev2(q))
                    gather_group(q, u, d1["ix"], DSTI, x, D)
            scatter_boundary(2, D)
            wait(pool, d1["T"], d1["T"].prev(EG))
            with pool.Fori(0, EG // 2) as i:
                for u in (0, 1):
                    q = i * 2 + u
                    wait(pool, s4["z"], s4["z"].prev2(q))
                    gather_group(q, u, s4["ix"], POSI, table[2], D)

            def rsqrt(seed, st, q, n):
                y, v, t = RS[n], RV[n], RT[n]
                wait(pool, seed, seed.done(q))
                hold(pool)
                for j in range(NEWTON):
                    if j:
                        wait(pool, st, st.at(q, 4 * j))
                    pool.tensor_tensor(t, y, y, ALU.mult).then_inc(st.sem, 1)
                    wait(pool, st, st.at(q, 4 * j + 1))
                    pool.tensor_tensor(t, t, v, ALU.mult).then_inc(st.sem, 1)
                    wait(pool, st, st.at(q, 4 * j + 2))
                    hold(pool)
                    pool.tensor_scalar(t, t, -0.5, 1.5, ALU.mult, ALU.add).then_inc(st.sem, 1)
                    wait(pool, st, st.at(q, 4 * j + 3))
                    pool.tensor_tensor(y, y, t, ALU.mult).then_inc(st.sem, 1)

            def p2_first(q):
                rsqrt(p2["seed"], p2["r"], q, 1)

            def p2_last(q, h, u):
                rsqrt(p2["seed2"], p2["r2"], q, 2)
                wait(pool, p2_st[u], h * 16)
                wait(pool, p2["r2"], p2["r2"].done(q))
                hold(pool)
                for k in range(G):
                    last = pool.tensor_scalar(GS[:, u, k, 0:D], scratch(10 + u)[:, k, :], MV3[:, k, 0:1], RS[2][:, k:k + 1],
                                              ALU.subtract, ALU.mult)
                last.then_inc(p2["o"].sem, 1)

            wait(pool, s4["z"], s4["z"].prev(EG))
            p2_first(0)
            with pool.Fori(0, EG // 2) as i:
                for u in (0, 1):
                    q = i * 2 + u
                    rsqrt(s5["seed"], s5["r"], q, 0)
                    p2_first(q + 1)
                    p2_last(q, i, u)
            scatter_boundary(3, D)
            with pool.Fori(0, EG // 2) as i:
                for u in (0, 1):
                    q = i * 2 + u
                    rsqrt(d3["seed"], d3["r"], q, 0)
                    for n in range(3):
                        r = (q * 3) + (EG + n)
                        p2_first(r + 1)
                        if n == 1:
                            rsqrt(d3["seed2"], d3["r2"], q, 3)
                        p2_last(r, i * 3 + (EG // 2 + (3 * u + n) // 2), (u + n) % 2)
            pool.wait_ge(p2_st[0], 16 * NG // 2)
            pool.wait_ge(p2_st[1], 16 * NG // 2)
            wait(pool, d3["o"], d3["o"].prev(EG))
            for t in range(ET):
                pool.indirect_dma_start(out, bass.IndirectOffsetOnAxis(ap=OUTI[:, t:t + 1], axis=0), YS[:, t, :], None,
                                        bounds_check=NODES - 1, oob_is_err=False).then_inc(fin, 16)
            pool.wait_ge(fin, 16 * ET)

        @block.tensor
        def _(pe):
            mm = pe.matmul
            for st in (ohmm, p1["mm"], s2["eaT"], xs["T"], d2["T"]):
                pe.sem_inc(st.sem, 1)
            pe.wait_ge(s_wts, 16 * 19)
            mm(pX[:, 0:D], wk_a[:, 0:D], wk_a[:, D:2 * D], start=True, stop=True)
            mm(pY[0:1, 0:D], bconv[:, 0:1], wk_a[:, D:2 * D], start=True, stop=True).then_inc(comp_mm.sem, 1)
            pe.wait_ge(consts, 4)
            keys_f.passed(pe)
            for a in range(4):
                last = pe.transpose(pZ[:, a * ET:(a + 1) * ET], kt[:, a, :], ident[0:ET, 0:ET])
            last.then_inc(keys_T.sem, 1)
            lk_diag.passed(pe)
            mm(pY[0:ET, 512:512 + ET], ones[0:ET, 0:ET], wk_b[0:ET, 0:ET], start=True, stop=True).then_inc(lk_mm.sem, 1)

            comp_ready.passed(pe)
            zeros.passed(pe)
            for a in (0, 1):
                mm(acc[:, a, 0:NT], ZH[:, 0:P], ZH[:, 0:NT], start=True, stop=False, skip_group_check=True)
            with pe.Fori(0, EG // 2) as i:
                for u in (0, 1):
                    q = i * 2 + u
                    for k in range(G):
                        t = q * G + k
                        v = (u * G + k) % 2
                        wait(pe, oh, oh.done(t))
                        mm(acc[:, 0, 0:NT], OHP[:, v, 0, :], OHT[:, v, 0, :], start=False, stop=False, skip_group_check=True)
                        mm(acc[:, 1, 0:NT], OHP[:, v, 1, :], OHT[:, v, 1, :], start=False, stop=False, skip_group_check=True)\
                            .then_inc(ohmm.sem, 1)
                    wait(pe, gathered[u], i * (16 * G) + (0 * 8 * G * EG + 16 * G))
                    wait(pe, xs["aT"], xs["aT"].prev(q))
                    for k in range(G):
                        last = pe.transpose(pYt[:, k, :], GS[:, u, k, 0:D], ident[:, :])
                    last.then_inc(xs["T"].sem, 1)
                    wait(pe, xs["ys"], xs["ys"].prev(q))
                    wait(pe, xs["aT"], xs["aT"].done(q))
                    for k in range(G):
                        mm(pZt[:, k, :], scratch(WAT)[:, k, :], wM[:, :], start=True, stop=False)
                        last = mm(pZt[:, k, :], ones[0:1, :], b0row[0:1, :], start=False, stop=True)
                    last.then_inc(xs["mm"].sem, 1)
            for a in (0, 1):
                last = mm(acc[:, a, 0:NT], ZH[:, 0:P], ZH[:, 0:NT], start=False, stop=True, skip_group_check=True)
            last.then_inc(ohmm.sem, 1)
            rowtot.passed(pe)
            mm(pY[:, 0:1], tri, cum[:, NT - 1:NT], start=True, stop=True).then_inc(rowoff.sem, 1)

            def p1_mm(q, h, u):
                wait(pe, p1_x[u], h * 16 + 16)
                wait(pe, p1["s"], p1["s"].prev(q))
                for k in range(G):
                    mm(pXt[:, k, :], WK[:, u, k * P:(k + 1) * P], wM[:, :], start=True, stop=False)
                    last = mm(pXt[:, k, :], ones[0:1, :], b0row[0:1, :], start=False, stop=True)
                last.then_inc(p1["mm"].sem, 1)

            def p1_gram(q):
                wait(pe, p1["xm"], p1["xm"].done(q))
                for k in range(G):
                    last = mm(acc[:, 0, 0:D + 1], XM[:, k, 0:D], XM[:, k, 0:D + 1], start=False, stop=False, skip_group_check=True)
                last.then_inc(p1["gram"].sem, 1)

            def p1_group(n, q, i, u):
                p1_mm(q + (n * EG + 1), i + (n * (EG // 2) + u), 1 - u)
                p1_gram(q + n * EG)

            def agg(n, q, w):
                a = q + n * EG
                wait(pe, ag["eqf"], ag["eqf"].done(a))
                wait(pe, ag["aT"], ag["aT"].prev(a))
                wait(pe, ag["m"], ag["m"].done(a))
                for k in range(G):
                    last = mm(pYt[:, k, :], scratch(M)[:, k, :], scratch(EQF)[:, k, :], start=True, stop=True)
                last.then_inc(ag["mmT"].sem, 1)
                wait(pe, ag["p"], ag["p"].prev(a))
                wait(pe, ag["aT"], ag["aT"].done(a))
                for k in range(G):
                    last = mm(pZt[:, k, :], scratch(WAT)[:, k, :], w[:, :], start=True, stop=True)
                last.then_inc(ag["mmP"].sem, 1)

            def boundary(n, width):
                pe.wait_ge(bd_l, 32 * (n + 1))
                if n == 0:
                    cmask.passed(pe)
                wait(pe, ag["p"], ag["p"].prev((n + 1) * EG))
                mm(pZ[0:ET, 0:width], Cmat[0:ET, :], FR[0:ET, 0:width], start=True, stop=True).then_inc(bd_mm, 1)

            hist_out.passed(pe)
            mm(acc[:, 0, 0:D + 1], ZH[:, 0:P], ZH[:, 0:D + 1], start=True, stop=False, skip_group_check=True)
            mm(acc[0:1, 1, 0:2 * D], ZH[:, 0:1], ZH[:, 0:2 * D], start=True, stop=False, skip_group_check=True)
            p1_mm(0, 0, 0)
            with pe.Fori(0, EG // 2) as i:
                for u in (0, 1):
                    p1_group(0, i * 2 + u, i, u)
            with pe.Fori(0, EG // 2) as i:
                for u in (0, 1):
                    q = i * 2 + u
                    p1_group(1, q, i, u)
                    agg(0, q, wA)
            boundary(0, CW)
            with pe.Fori(0, EG // 2) as i:
                for u in (0, 1):
                    q = i * 2 + u
                    p1_group(2, q, i, u)
                    agg(1, q, wL)
            boundary(1, D)
            with pe.Fori(0, EG // 2) as i:
                for u in (0, 1):
                    q = i * 2 + u
                    p1_group(3, q, i, u)
                    wait(pe, s2_ea[u], i * 16 + 16)
                    wait(pe, s2["xTc"], s2["xTc"].prev(q))
                    for k in range(G):
                        last = pe.transpose(pYt[:, k, :], scratch(10 + u)[:, k, :], ident[:, :])
                    last.then_inc(s2["eaT"].sem, 1)
                    wait(pe, s2["eaTc"], s2["eaTc"].done(q))
                    wait(pe, s2["x2"], s2["x2"].done(q))
                    for k in range(G):
                        last = pe.transpose(pYt[:, k, :], scratch(M)[:, k, :], ident[:, :])
                    last.then_inc(s2["xT"].sem, 1)
                    wait(pe, s2["sq"], s2["sq"].prev(q))
                    wait(pe, s2["xTc"], s2["xTc"].done(q))
                    for k in range(G):
                        mm(pZt[:, k, :], scratch(WAT)[:, k, :], w1a[:, :], start=True, stop=False)
                        last = mm(pZt[:, k, :], scratch(AT2)[:, k, :], w1b[:, :], start=False, stop=True)
                    last.then_inc(s2["z1"].sem, 1)
                    wait(pe, s2["em"], s2["em"].done(q))
                    wait(pe, s2["sq"], s2["sq"].done(q))
                    hold(pe)
                    for k in range(G):
                        mm(acc[0:1, 1, 0:D], EM[:, k:k + 1], Z[:, bass.ds(q * G + k, 1), :].rearrange("p a f -> p (a f)"), start=False, stop=False, skip_group_check=True)
                        last = mm(acc[0:1, 1, D:2 * D], EM[:, k:k + 1], scratch(EQF)[:, k, :], start=False, stop=False, skip_group_check=True)
                    last.then_inc(s2["stat"].sem, 1)
            bn_t[0].passed(pe)
            mm(pX[:, 0:2 * D], ones[0:1, :], bnrow[0:1, :, :].rearrange("a b c -> a (b c)"), start=True, stop=True).then_inc(bn_b[0].sem, 1)
            bn_done[0].passed(pe)
            mm(acc[0:1, 1, 0:2 * D], ZH[:, 0:1], ZH[:, 0:2 * D], start=True, stop=False, skip_group_check=True)
            with pe.Fori(0, EG // 2) as i:
                for u in (0, 1):
                    q = i * 2 + u
                    wait(pe, gathered[u], i * (16 * G) + (4 * 8 * G * EG + 16 * G))
                    wait(pe, d1["y"], d1["y"].prev(q))
                    for k in range(G):
                        last = pe.transpose(pXt[:, k, :], GS[:, u, k, 0:D], ident[:, :])
                    last.then_inc(d1["T"].sem, 1)
                    agg(2, q, w2b)
                    wait(pe, d1["aT"], d1["aT"].done(q))
                    for k in range(G):
                        mm(pXt[:, k, :], scratch(2)[:, k, :], wM[:, :], start=True, stop=False)
                        last = mm(pXt[:, k, :], ones[0:1, :], b0row[0:1, :], start=False, stop=True)
                    last.then_inc(d1["mm"].sem, 1)
            boundary(2, D)
            pe.wait_ge(bd_r, 3)
            with pe.Fori(0, EG // 2) as i:
                for u in (0, 1):
                    q = i * 2 + u
                    wait(pe, d2_x[u], i * 16 + 16)
                    wait(pe, d2["z"], d2["z"].prev(q))
                    for k in range(G):
                        last = pe.transpose(pXt[:, k, :], scratch(u)[:, k, :], ident[:, :])
                    last.then_inc(d2["T"].sem, 1)
                    wait(pe, s4["aT"], s4["aT"].prev(q))
                    wait(pe, s4["cp"], s4["cp"].done(q))
                    for k in range(G):
                        last = pe.transpose(pYt[:, k, :], scratch(M)[:, k, :], ident[:, :])
                    last.then_inc(s4["T"].sem, 1)
                    wait(pe, d2["aT"], d2["aT"].done(q))
                    for k in range(G):
                        last = mm(pXt[:, k, :], scratch(2)[:, k, :], w2a[:, :], start=True, stop=True)
                    last.then_inc(d2["mm"].sem, 1)
                    wait(pe, s4["z"], s4["z"].prev(q))
                    wait(pe, s4["aT"], s4["aT"].done(q))
                    for k in range(G):
                        last = mm(pZt[:, k, :], scratch(WAT)[:, k, :], w2a[:, :], start=True, stop=True)
                    last.then_inc(s4["mm"].sem, 1)
                    wait(pe, d2["em"], d2["em"].done(q))
                    wait(pe, d2["sq"], d2["sq"].done(q))
                    for k in range(G):
                        mm(acc[0:1, 1, 0:D], EM[:, k:k + 1], scratch(5 if u == 0 else 10)[:, k, :], start=False, stop=False, skip_group_check=True)
                        last = mm(acc[0:1, 1, D:2 * D], EM[:, k:k + 1], scratch(EQF)[:, k, :], start=False, stop=False, skip_group_check=True)
                    last.then_inc(d2["stat"].sem, 1)
            gr.passed(pe)
            mm(pX[:, 0:D], GM[:, 0:D], w2a[:, :], start=True, stop=True)
            mm(pX[0:1, 512:512 + D], GM[:, D:D + 1], w2a[:, :], start=True, stop=True).then_inc(gr_mm.sem, 1)
            gr_p.passed(pe)
            mm(pY[0:1, 0:D], ones[:, 0:1], GP, start=True, stop=True).then_inc(gr_q.sem, 1)
            bn_t[1].passed(pe)
            mm(pX[:, 0:2 * D], ones[0:1, :], bnrow[0:1, :, :].rearrange("a b c -> a (b c)"), start=True, stop=True).then_inc(bn_b[0].sem, 1)
            bn_done[1].passed(pe)

            def p2_mm(q, h, u):
                wait(pe, p2_x[u], h * 16 + 16)
                wait(pe, p2["xT"], p2["xT"].prev(q))
                for k in range(G):
                    last = pe.transpose(pXt[:, k, :], scratch(u)[:, k, :], ident[:, :])
                last.then_inc(p2["T"].sem, 1)
                wait(pe, p2["s"], p2["s"].prev(q))
                wait(pe, p2["xT"], p2["xT"].done(q))
                for k in range(G):
                    mm(pWt[:, k, :], scratch(2)[:, k, :], w2s[:, :], start=True, stop=False)
                    last = mm(pWt[:, k, :], ones[0:1, :], bnrow[0:1, 1, :], start=False, stop=True)
                last.then_inc(p2["mm"].sem, 1)

            p2_mm(0, 0, 0)
            with pe.Fori(0, EG // 2) as i:
                for u in (0, 1):
                    q = i * 2 + u
                    p2_mm(q + 1, i if u == 0 else i + 1, 1 - u)
                    agg(3, q, w3)
            boundary(3, D)
            with pe.Fori(0, EG // 2) as i:
                for u in (0, 1):
                    q = i * 2 + u
                    for n in range(3):
                        r = (q * 3) + (EG + n + 1)
                        p2_mm(r, i * 3 + (EG // 2 + (3 * u + n + 1) // 2), (u + n + 1) % 2)

        @block.scalar
        def _(act):
            A = act.activation

            def square_sums(src_t, junk, ss, st):
                for k in range(G):
                    last = A(junk[:, k, 0:D], src_t[:, k, :], ACT.Square, accum_out=ss[:, k:k + 1])
                last.then_inc(st.sem, 1)

            def p1_first(q, u):
                wait(act, p1["xm"], p1["xm"].prev2(q))
                wait(act, p1["mm"], p1["mm"].done(q))
                hold(act)
                square_sums(pXt, scratch(2 + u), SS1, p1["sq"])
                wait(act, p1["sq"], p1["sq"].done(q))
                wait(act, p1["r"], p1["r"].prev(q))
                hold(act)
                A(SD1, SS1, ACT.Sqrt, bias=eps_ln[:, 0:1], scale=1.0 / D).then_inc(p1["sqrt"].sem, 1)

            def p1_second(q, u):
                wait(act, p1["gram"], p1["gram"].prev(q))
                wait(act, p1["s"], p1["s"].done(q))
                hold(act)
                square_sums(scratch(2 + u), XM, SS2, p1["sq2"])
                wait(act, p1["sq2"], p1["sq2"].done(q))
                wait(act, p1["r2"], p1["r2"].prev(q))
                hold(act)
                A(SD2, SS2, ACT.Sqrt, bias=eps_ln[:, 0:1], scale=1.0 / D).then_inc(p1["sqrt2"].sem, 1)

            def p1_group(n, q, u):
                p1_first(q + (n * EG + 1), 1 - u)
                p1_second(q + n * EG, u)

            def agg_eq(n, q):
                a = q + n * EG
                wait(act, ag["mmT"], ag["mmT"].prev(a))
                hold(act)
                A(scratch(EQF), EQ[:, span(q), :], ACT.Copy).then_inc(ag["eqf"].sem, 1)

            def agg(n, q, i, u):
                a = q + n * EG
                wait(act, ag["mmP"], ag["mmP"].prev(a))
                wait(act, ag["mmT"], ag["mmT"].done(a))
                hold(act)
                A(scratch(WAT), pYt, ACT.Copy).then_inc(ag["aT"].sem, 1)
                wait(act, ag_st[u], (i + n * (EG // 2)) * 16)
                wait(act, ag["mmP"], ag["mmP"].done(a))
                if n == 0:
                    wait(act, ag["cnt"], ag["cnt"].done(a))
                hold(act)
                A(PT[:, u, :, 0:D], pZt, ACT.Copy).then_inc(ag["p"].sem, 1)

            act.sem_inc(xs["raw"].sem, 1)
            with act.Fori(0, EG // 2) as i:
                for u in (0, 1):
                    q = i * 2 + u
                    wait(act, xs["mm"], xs["mm"].prev(q))
                    wait(act, xs["T"], xs["T"].done(q))
                    hold(act)
                    A(scratch(WAT), pYt, ACT.Copy).then_inc(xs["aT"].sem, 1)
                    wait(act, gathered[u], i * (16 * G) + (0 * 8 * G * EG + 16 * G))
                    hold(act)
                    A(Z[:, span(q), :], GS[:, u, :, 0:D], ACT.Copy).then_inc(xs["raw"].sem, 1)
                    wait(act, xs["mm"], xs["mm"].done(q))
                    hold(act)
                    A(YS[:, span(q), :], pZt, ACT.Copy).then_inc(xs["ys"].sem, 1)
            comp_ready.passed(act)
            act.wait_ge(tab_stored, 16)
            p1_first(0, 0)
            with act.Fori(0, EG // 2) as i:
                for u in (0, 1):
                    p1_group(0, i * 2 + u, u)
            ns_in.passed(act)
            A(NS[:, :], RR, ACT.Sqrt).then_inc(ns_sq.sem, 1)
            ns_ready.passed(act)
            with act.Fori(0, EG // 2) as i:
                for u in (0, 1):
                    q = i * 2 + u
                    agg_eq(0, q)
                    p1_group(1, q, u)
                    agg(0, q, i, u)
            with act.Fori(0, EG // 2) as i:
                for u in (0, 1):
                    q = i * 2 + u
                    agg_eq(1, q)
                    wait(act, s1["y"], s1["y"].prev(q))
                    wait(act, s1["rc"], s1["rc"].done(q))
                    hold(act)
                    A(ND[:, span(q)], RC[:, span(q)], ACT.Sqrt).then_inc(s1["nd"].sem, 1)
                    wait(act, ag["mmT"], ag["mmT"].prev(q + EG))
                    wait(act, s1["y"], s1["y"].done(q))
                    hold(act)
                    for k in range(G):
                        last = A(scratch(M)[:, k, :], YS[:, bass.ds(q * G + k, 1), :].rearrange("p a f -> p (a f)"), ACT.Square, accum_out=SS3[:, k:k + 1])
                    last.then_inc(s1["sq"].sem, 1)
                    wait(act, s1["r"], s1["r"].prev(q))
                    wait(act, s1["sq"], s1["sq"].done(q))
                    hold(act)
                    A(SD3, SS3, ACT.Sqrt, bias=eps_ln[:, 0:1], scale=1.0 / D).then_inc(s1["sqrt"].sem, 1)
                    p1_group(2, q, u)
                    agg(1, q, i, u)
            with act.Fori(0, EG // 2) as i:
                for u in (0, 1):
                    q = i * 2 + u
                    wait(act, s2["r"], s2["r"].prev(q))
                    wait(act, s2["ag"], s2["ag"].done(q))
                    hold(act)
                    A(SD3, MVS[:, :, 1], ACT.Sqrt, bias=eps_ln[:, 0:1], scale=1.0).then_inc(s2["sqrt"].sem, 1)
                    p1_group(3, q, u)
                    wait(act, s2["z1"], s2["z1"].prev(q))
                    wait(act, s2["eaT"], s2["eaT"].done(q))
                    hold(act)
                    A(scratch(AT2), pYt, ACT.Copy).then_inc(s2["eaTc"].sem, 1)
                    wait(act, s2["x2"], s2["x2"].done(q))
                    hold(act)
                    A(YS[:, span(q), :], scratch(M), ACT.Copy).then_inc(s2["keep"].sem, 1)
                    wait(act, s2["xT"], s2["xT"].done(q))
                    hold(act)
                    A(scratch(WAT), pYt, ACT.Copy).then_inc(s2["xTc"].sem, 1)
                    wait(act, s2["z1"], s2["z1"].done(q))
                    wait(act, s2["stat"], s2["stat"].prev(q))
                    hold(act)
                    A(Z[:, span(q), :], pZt, ACT.Copy).then_inc(s2["zc"].sem, 1)
                    A(scratch(EQF), pZt, ACT.Square).then_inc(s2["sq"].sem, 1)
            bn_v[0].passed(act)
            A(rt[:, 3, :], rt[:, 2, :], ACT.Sqrt).then_inc(bn_a[0].sem, 1)
            bn_done[0].passed(act)
            with act.Fori(0, EG // 2) as i:
                for u in (0, 1):
                    q = i * 2 + u
                    agg_eq(2, q)
                    wait(act, h1["s1"], h1["s1"].prev(q))
                    wait(act, h1["v"], h1["v"].done(q))
                    hold(act)
                    A(scratch(10), scratch(9), ACT.Exp).then_inc(h1["exp"].sem, 1)
                    wait(act, d1["mm"], d1["mm"].prev(q))
                    wait(act, d1["T"], d1["T"].done(q))
                    hold(act)
                    A(scratch(2), pXt, ACT.Copy).then_inc(d1["aT"].sem, 1)
                    agg(2, q, i, u)
                    wait(act, d1["x1"], d1["x1"].prev(q))
                    wait(act, d1["rc"], d1["rc"].done(q))
                    hold(act)
                    A(NDD, RCD[:, span(q)], ACT.Sqrt).then_inc(d1["nd"].sem, 1)
                    wait(act, d1["y"], d1["y"].done(q))
                    hold(act)
                    square_sums(scratch(4), scratch(5), SS3, d1["sq"])
                    wait(act, d1["sq"], d1["sq"].done(q))
                    hold(act)
                    A(SD3, SS3, ACT.Sqrt, bias=eps_ln[:, 0:1], scale=1.0 / D).then_inc(d1["sqrt"].sem, 1)
                    wait(act, d1["r2"], d1["r2"].prev(q))
                    wait(act, d1["ag"], d1["ag"].done(q))
                    hold(act)
                    A(SD2, MVS[:, :, 1], ACT.Sqrt, bias=eps_ln[:, 0:1], scale=1.0).then_inc(d1["sqrt2"].sem, 1)
            with act.Fori(0, EG // 2) as i:
                for u in (0, 1):
                    q = i * 2 + u
                    wait(act, s4["T"], s4["T"].prev(q))
                    hold(act)
                    A(scratch(M), YS[:, span(q), :], ACT.Copy).then_inc(s4["cp"].sem, 1)
                    wait(act, d2["mm"], d2["mm"].prev(q))
                    wait(act, d2["T"], d2["T"].done(q))
                    hold(act)
                    A(scratch(2), pXt, ACT.Copy).then_inc(d2["aT"].sem, 1)
                    wait(act, s4["mm"], s4["mm"].prev(q))
                    wait(act, s4["T"], s4["T"].done(q))
                    hold(act)
                    A(scratch(WAT), pYt, ACT.Copy).then_inc(s4["aT"].sem, 1)
                    wait(act, d2["stat"], d2["stat"].prev(q))
                    wait(act, d2["z"], d2["z"].done(q))
                    hold(act)
                    A(scratch(EQF), scratch(5 if u == 0 else 10), ACT.Square).then_inc(d2["sq"].sem, 1)
            bn_v[1].passed(act)
            A(rt[:, 3, :], rt[:, 2, :], ACT.Sqrt).then_inc(bn_a[0].sem, 1)
            bn_done[1].passed(act)

            def p2_first(q):
                wait(act, p2["mm"], p2["mm"].prev(q))
                wait(act, p2["T"], p2["T"].done(q))
                hold(act)
                A(scratch(2), pXt, ACT.Copy).then_inc(p2["xT"].sem, 1)
                wait(act, p2["t"], p2["t"].prev(q))
                wait(act, p2["mm"], p2["mm"].done(q))
                hold(act)
                A(scratch(3), pWt, ACT.Exp).then_inc(p2["exp"].sem, 1)

            p2_first(0)
            with act.Fori(0, EG // 2) as i:
                for u in (0, 1):
                    q = i * 2 + u
                    agg_eq(3, q)
                    wait(act, s5["s"], s5["s"].prev(q))
                    wait(act, s5["v"], s5["v"].done(q))
                    hold(act)
                    A(XM[:, :, 0:D], scratch(9), ACT.Exp).then_inc(s5["exp"].sem, 1)
                    p2_first(q + 1)
                    agg(3, q, i, u)
            with act.Fori(0, EG // 2) as i:
                for u in (0, 1):
                    q = i * 2 + u
                    wait(act, d3["u"], d3["u"].prev(q))
                    wait(act, d3["v"], d3["v"].done(q))
                    hold(act)
                    A(scratch(9), scratch(7), ACT.Exp).then_inc(d3["exp"].sem, 1)
                    for n in range(3):
                        p2_first((q * 3) + (EG + n + 1))

        @block.vector
        def _(dve):
            chain = [0]

            def link(ins):
                chain[0] += 1
                ins.then_inc(vlink, 1)
                dve.wait_ge(vlink, chain[0])

            ts, tt, stt = dve.tensor_scalar, dve.tensor_tensor, dve.scalar_tensor_tensor

            def row(t, q, k):
                return t[:, bass.ds(q * G + k, 1), :].rearrange("p a f -> p (a f)")

            def col(t, q, k):
                return t[:, bass.ds(q * G + k, 1)]

            def over(t):
                return t.unsqueeze(1).broadcast_to([P, G, D])

            for st in (lk_use, eq_built, p1["xm"], s1["y"], s2["s"], s4["z"], d2["z"], p2["t"]):
                dve.sem_inc(st.sem, 1)
            dve.memset(ones[:, :], 1.0)
            dve.memset(eps_ln[:, :], LN_EPS)
            dve.memset(ZH[:, :], 0.0)
            dve.memset(PT[:, :, :, :], 0.0)
            dve.memset(ones_t, 1.0)
            dve.memset(Cmat[:, :], 0.0)
            dve.memset(XM[:, :, :], 0.0).then_inc(zeros.sem, 1)
            zeros.passed(dve)
            dve.wait_ge(s_keys, 64)
            dve.tensor_copy(kt[:, 0:3, :], kti[:, 0:3, :]).then_inc(keys_f.sem, 1)
            dve.wait_ge(consts, 4)
            dve.tensor_copy(iota_h, iota_i)
            dve.tensor_copy(sc[:, 1:2], sc[:, 0:1].bitcast(i32))
            keys_T.passed(dve)
            dve.tensor_copy(KD[:, :], pZ[:, 0:ET])
            dve.tensor_copy(KP, pZ[:, ET:2 * ET])
            dve.tensor_copy(KS, pZ[:, 2 * ET:3 * ET])
            link(dve.tensor_copy(WE[:, :], pZ[:, 3 * ET:4 * ET]))
            dve.tensor_copy(SRCI[:, :], KS)
            dve.tensor_copy(DSTI[:, :], KD[:, :]).then_inc(idx_ready.sem, 1)
            for key, p_, t_ in ((KD[:, :], PD, TD), (KS, PS_, TS_)):
                link(ts(p_, key, -(NT - 1) / 2.0, 1.0 / NT, ALU.add, ALU.mult))
                link(ts(p_, p_, ROUND, None, ALU.add))
                link(ts(p_, p_, -ROUND, None, ALU.add))
                link(stt(out=t_, in0=p_, scalar=-float(NT), in1=key, op0=ALU.mult, op1=ALU.add))
            link(ts(REAL[:, :], KD[:, :], float(NODES), None, ALU.is_lt))
            link(tt(REP[:, :], KD[:, :], KP, ALU.not_equal))
            link(tt(REP[:, :], REP[:, :], REAL[:, :], ALU.mult))
            link(ts(RC[:, :], REP[:, :], -NOWHERE, NOWHERE, ALU.mult, ALU.add))
            link(tt(RC[:, :], RC[:, :], KD[:, :], ALU.add))
            dve.tensor_copy(OUTI[:, :], RC[:, :])
            dve.wait_ge(s_wts, 16 * 19)

            def centre(w, rows_, scratch_col):
                link(dve.tensor_reduce(scratch_col, w, axis=AX.X, op=ALU.add))
                link(ts(scratch_col, scratch_col, 1.0 / D, None, ALU.mult))
                link(ts(w, w, scratch_col, None, ALU.subtract))

            link(tt(wM[:, :], wM[:, :], ident[:, :], ALU.add))
            centre(wM[:, :], P, sc[:, 2:3])
            comp_mm.passed(dve)
            link(dve.tensor_copy(wA[:, :], pX[:, 0:D]))
            centre(wA[:, :], P, sc[:, 2:3])
            link(tt(b0row[0:1, :], pY[0:1, 0:D], rows[:, 6, :], ALU.add))
            centre(b0row[0:1, :], 1, sc[0:1, 2:3])
            link(ts(cB[:, :], blB[:, :], 0.0, None, ALU.max))
            centre(cB[:, :], P, sc[:, 2:3])
            dve.sem_inc(comp_ready.sem, 1)
            link(ts(wk_b[0:ET, 0:ET], ident[0:ET, 0:ET], kt[:, 0, P - 1:P], None, ALU.mult))
            dve.sem_inc(lk_diag.sem, 1)
            lk_mm.passed(dve)
            ts(Cmat[0:ET, :], pY[0:ET, 512:512 + ET], kt[:, 0, 0:1], None, ALU.is_equal).then_inc(cmask0.sem, 1)
            link(ts(wk_a[0:ET, 0:P], kt[:, 0, :], kt[:, 0, P - 1:P], None, ALU.is_equal))
            link(dve.tensor_reduce(sc[0:ET, 2:3], wk_a[0:ET, 0:P], axis=AX.X, op=ALU.add))
            link(ts(sc[0:ET, 3:4], sc[0:ET, 2:3], float(P), None, ALU.is_ge))
            link(ts(sc[0:ET, 4:5], kt[:, 1, 0:1], kt[:, 0, P - 1:P], None, ALU.is_equal))
            link(tt(sc[0:ET, 3:4], sc[0:ET, 3:4], sc[0:ET, 4:5], ALU.mult))
            link(tt(sc[0:ET, 1:2], sc[0:ET, 1:2], sc[0:ET, 2:3], ALU.subtract))
            link(stt(out=sc[0:ET, 1:2], in0=sc[0:ET, 3:4], scalar=NOWHERE, in1=sc[0:ET, 1:2], op0=ALU.mult, op1=ALU.add))
            link(dve.tensor_copy(REPI[0:ET, :], sc[0:ET, 1:2]))

            with dve.Fori(0, EG // 2) as i:
                for u in (0, 1):
                    q = i * 2 + u
                    for k in range(G):
                        t = q * G + k
                        v = (u * G + k) % 2
                        wait(dve, ohmm, ohmm.prev2(t))
                        ts(OHP[:, v, 0, :], iota_h[:, 0:P], PD[:, bass.ds(t, 1)], None, ALU.is_equal)
                        ts(OHT[:, v, 0, :], iota_h[:, 0:NT], TD[:, bass.ds(t, 1)], None, ALU.is_equal)
                        ts(OHP[:, v, 1, :], iota_h[:, 0:P], PS_[:, bass.ds(t, 1)], None, ALU.is_equal)
                        ts(OHT[:, v, 1, :], iota_h[:, 0:NT], TS_[:, bass.ds(t, 1)], None, ALU.is_equal).then_inc(oh.sem, 1)
            wait(dve, ohmm, ohmm.prev(ET + 1))
            wait(dve, xs["ys"], xs["ys"].prev(EG))
            dve.tensor_copy(degout, acc[:, 1, 0:NT])
            link(dve.tensor_copy(deg, acc[:, 0, 0:NT]))
            dve.sem_inc(hist_out.sem, 1)
            link(dve.tensor_tensor_scan(cum, ones_t, deg, 0.0, ALU.mult, ALU.add))
            dve.sem_inc(rowtot.sem, 1)
            rowoff.passed(dve)
            link(dve.tensor_copy(sc[:, 5:6], pY[:, 0:1]))
            link(tt(posn, cum, deg, ALU.subtract))
            link(ts(posn, posn, sc[:, 5:6], None, ALU.add))
            link(ts(MASK[:, :], deg, 0.0, None, ALU.is_equal))
            link(ts(cum, posn, -1.0, float(ZERO_ROW), ALU.mult, ALU.add))
            link(tt(cum, cum, MASK[:, :], ALU.mult))
            dve.tensor_copy(tabs[:, :, 0], degout)
            link(tt(tabs[:, :, 1], posn, cum, ALU.add))
            dve.sem_inc(tab_ready.sem, 1)
            mask1.passed(dve)

            def invert(st, q, r, sd, after):
                wait(dve, after, after.done(q))
                dve.reciprocal(r, sd).then_inc(st.sem, 1)

            def p1_first(q, u):
                wait(dve, p1["s"], p1["s"].prev(q))
                invert(p1["r"], q, R1, SD1, p1["sqrt"])
                wait(dve, p1["r"], p1["r"].done(q))
                for k in range(G):
                    last = stt(out=scratch(2 + u)[:, k, :], in0=pXt[:, k, :], scalar=R1[:, k:k + 1], in1=cB[:, :],
                               op0=ALU.mult, op1=ALU.add)
                last.then_inc(p1["s"].sem, 1)

            def p1_second(q, h, u):
                wait(dve, p1["xm"], p1["xm"].prev(q))
                invert(p1["r2"], q, R2, SD2, p1["sqrt2"])
                wait(dve, p1_st[u], h * 16)
                wait(dve, p1["r2"], p1["r2"].done(q))
                tt(RM, R2, MASK[:, span(q)], ALU.mult).then_inc(p1["rm"].sem, 1)
                for k in range(G):
                    last = ts(scratch(4 + u)[:, k, :], scratch(2 + u)[:, k, :], R2[:, k:k + 1], None, ALU.mult)
                last.then_inc(p1["x2"].sem, 1)
                wait(dve, p1["rm"], p1["rm"].done(q))
                hold(dve)
                dve.tensor_copy(XM[:, :, D], MASK[:, span(q)])
                for k in range(G):
                    last = ts(XM[:, k, 0:D], scratch(2 + u)[:, k, :], RM[:, k:k + 1], None, ALU.mult)
                last.then_inc(p1["xm"].sem, 1)

            def p1_group(n, q, i, u):
                p1_first(q + (n * EG + 1), 1 - u)
                p1_second(q + n * EG, i + n * (EG // 2), u)

            def boundary(n, width):
                dve.wait_ge(bd_mm, n + 1)
                tt(LR[0:ET, 0:width], LR[0:ET, 0:width], pZ[0:ET, 0:width], ALU.add).then_inc(bd_r, 1)

            p1_first(0, 0)
            with dve.Fori(0, EG // 2) as i:
                for u in (0, 1):
                    q = i * 2 + u
                    wait(dve, gathered[u], i * (16 * G) + (1 * 8 * G * EG + 16 * G))
                    hold(dve)
                    dve.tensor_copy(LK[:, span(q), :], GS[:, u, :, 0:2]).then_inc(lk_use.sem, 1)
                    wait(dve, rk_l[u], i * 16 + 16)
                    for k in range(G):
                        last = ts(row(EQ, q, k), WK[:, 10 + u, k * P:(k + 1) * P].bitcast(i32), col(KD, q, k), None, ALU.is_equal)
                    last.then_inc(eq_built.sem, 1)
                    p1_group(0, q, i, u)
            wait(dve, eq_built, eq_built.prev(EG))
            wait(dve, lk_use, lk_use.prev(EG))
            dve.memset(EQ[:, ET - 1, LASTROWS:P], 0.0)
            dve.tensor_copy(POSI[:, :], LK[:, :, 1])
            link(ts(RR, LK[:, :, 0], 1.0, None, ALU.max))
            link(dve.reciprocal(RR, RR))
            dve.sem_inc(ns_in.sem, 1)
            ns_sq.passed(dve)
            dve.sem_inc(ns_ready.sem, 1)
            with dve.Fori(0, EG // 2) as i:
                for u in (0, 1):
                    q = i * 2 + u
                    wait(dve, ag["mmT"], ag["mmT"].prev(q))
                    for k in range(G):
                        last = ts(scratch(M)[:, k, :], row(Z, q, k), col(NS, q, k), None, ALU.mult)
                    last.then_inc(ag["m"].sem, 1)
                    wait(dve, ag_st[u], i * 16)
                    wait(dve, ag["eqf"], ag["eqf"].done(q))
                    dve.tensor_reduce(PT[:, u, :, D], scratch(EQF), axis=AX.X, op=ALU.add).then_inc(ag["cnt"].sem, 1)
                    p1_group(1, q, i, u)
            boundary(0, CW)
            with dve.Fori(0, EG // 2) as i:
                for u in (0, 1):
                    q = i * 2 + u
                    wait(dve, gathered[u], i * (16 * G) + (2 * 8 * G * EG + 16 * G))
                    ts(CS, GS[:, u, :, D], 1.0, None, ALU.max).then_inc(s1["c"].sem, 1)
                    wait(dve, s1["c"], s1["c"].done(q))
                    hold(dve)
                    dve.reciprocal(RC[:, span(q)], CS).then_inc(s1["rc"].sem, 1)
                    wait(dve, s1["nd"], s1["nd"].done(q))
                    for k in range(G):
                        last = stt(out=row(YS, q, k), in0=GS[:, u, k, 0:D], scalar=col(ND, q, k), in1=row(YS, q, k),
                                   op0=ALU.mult, op1=ALU.add)
                    last.then_inc(s1["y"].sem, 1)
                    wait(dve, ag["m"], ag["m"].prev(q + EG))
                    invert(s1["r"], q, R3, SD3, s1["sqrt"])
                    wait(dve, s1["r"], s1["r"].done(q))
                    for k in range(G):
                        last = ts(row(YS, q, k), row(YS, q, k), R3[:, k:k + 1], None, ALU.mult)
                    last.then_inc(s1["x1"].sem, 1)
                    wait(dve, s1["x1"], s1["x1"].done(q))
                    for k in range(G):
                        last = ts(scratch(M)[:, k, :], row(YS, q, k), col(NS, q, k), None, ALU.mult)
                    last.then_inc(ag["m"].sem, 1)
                    p1_group(2, q, i, u)
            boundary(1, D)

            def stats(st_bn, st_ag, q, rows_, n):
                for k in range(G):
                    last = dve.bn_stats(ST[:, n, k, :], rows_(k))
                last.then_inc(st_bn.sem, 1)
                wait(dve, st_bn, st_bn.done(q))
                hold(dve)
                for k in range(G):
                    last = dve.bn_aggr(MV[:, n, k, :], ST[:, n, k, :])
                last.then_inc(st_ag.sem, 1)

            def rsqrt_seed(seed, ag_, q, n):
                bits = RS[n].bitcast(i32)
                wait(dve, ag_, ag_.done(q))
                ts(RV[n], MV[:, n, :, 1], LN_EPS, None, ALU.add).then_inc(seed.sem, 1)
                wait(dve, seed, seed.at(q, 1))
                ts(bits, RV[n].bitcast(i32), 1, None, ALU.logical_shift_right).then_inc(seed.sem, 1)
                wait(dve, seed, seed.at(q, 2))
                ts(bits, bits, -1.0, SEED, ALU.mult, ALU.add).then_inc(seed.sem, 1)

            def norm(out_, rows_, mean, r, st):
                for k in range(G):
                    last = ts(out_[:, k, :], rows_(k), mean[:, k, 0:1], r[:, k:k + 1], ALU.subtract, ALU.mult)
                last.then_inc(st.sem, 1)

            with dve.Fori(0, EG // 2) as i:
                for u in (0, 1):
                    q = i * 2 + u
                    wait(dve, gathered[u], i * (16 * G) + (3 * 8 * G * EG + 16 * G))
                    for k in range(G):
                        last = stt(out=GS[:, u, k, 0:D], in0=GS[:, u, k, 0:D], scalar=col(ND, q, k), in1=blB[:, :],
                                   op0=ALU.mult, op1=ALU.add)
                    last.then_inc(s2["a"].sem, 1)
                    wait(dve, s2["a"], s2["a"].done(q))
                    stt(out=GS[:, u, :, 0:D], in0=GS[:, u, :, 0:D], scalar=0.0, in1=YS[:, span(q), :],
                        op0=ALU.max, op1=ALU.add).then_inc(s2["a2"].sem, 1)
                    wait(dve, s2["a2"], s2["a2"].done(q))
                    hold(dve)
                    stats(s2["bn"], s2["ag"], q, lambda k: GS[:, u, k, 0:D], 0)
                    invert(s2["r"], q, R3, SD3, s2["sqrt"])
                    wait(dve, s2["keep"], s2["keep"].prev(q))
                    wait(dve, s2["xT"], s2["xT"].prev(q))
                    wait(dve, s2["r"], s2["r"].done(q))
                    norm(scratch(M), lambda k: GS[:, u, k, 0:D], MVS, R3, s2["x2"])
                    wait(dve, s2["stat"], s2["stat"].prev(q))
                    wait(dve, s2["x2"], s2["x2"].done(q))
                    hold(dve)
                    dve.tensor_copy(EM, REAL[:, span(q)]).then_inc(s2["em"].sem, 1)
                    dve.sem_inc(s2["s"].sem, 1)
                    p1_group(3, q, i, u)

            def batch_norm(n, sums, count, b, gamma, beta, to):
                link(ts(rt[:, 0:2, :], sums, 1.0 / count, None, ALU.mult))
                link(tt(rt[:, 2, :], rt[:, 0, :], rt[:, 0, :], ALU.mult))
                link(tt(rt[:, 2, :], rt[:, 1, :], rt[:, 2, :], ALU.subtract))
                link(ts(rt[:, 2, :], rt[:, 2, :], 0.0, BN_EPS, ALU.max, ALU.add))
                dve.sem_inc(bn_v[0].sem, 1)
                bn_a[n - 1].passed(dve)
                link(dve.reciprocal(rt[:, 4, :], rt[:, 3, :]))
                link(tt(bnrow[:, 0, :], rt[:, 4, :], gamma, ALU.mult))
                link(tt(rt[:, 0, :], rt[:, 0, :], b, ALU.add))
                link(tt(rt[:, 0, :], b, rt[:, 0, :], ALU.subtract))
                link(tt(rt[:, 0, :], rt[:, 0, :], bnrow[:, 0, :], ALU.mult))
                link(tt(bnrow[:, 1, :], rt[:, 0, :], beta, ALU.add))
                dve.sem_inc(bn_t[0].sem, 1)
                bn_b[n - 1].passed(dve)
                link(dve.tensor_copy(to.rearrange("p a f -> p (a f)"), pX[:, 0:2 * D]))

            wait(dve, s2["stat"], s2["stat"].prev(EG))
            wait(dve, p1["s"], p1["s"].prev(NG + 1))
            batch_norm(1, acc[0:1, 1, 0:2 * D].rearrange("a (r f) -> a r f", r=2), EDGES, rows[:, 0, :], rows[:, 1, :], rows[:, 2, :], bn1B[:, :, :])
            dve.sem_inc(bn_done[0].sem, 1)
            with dve.Fori(0, EG // 2) as i:
                for u in (0, 1):
                    q = i * 2 + u
                    wait(dve, h1["s1"], h1["s1"].prev(q))
                    tt(scratch(9), Z[:, span(q), :], over(bn1B[:, 0, :]), ALU.mult).then_inc(h1["v1"].sem, 1)
                    wait(dve, h1["v1"], h1["v1"].done(q))
                    tt(scratch(9), scratch(9), over(bn1B[:, 1, :]), ALU.add).then_inc(h1["v"].sem, 1)
                    wait(dve, h1["exp"], h1["exp"].done(q))
                    ts(scratch(10), scratch(10), 1.0, -1.0, ALU.min, ALU.add).then_inc(h1["t"].sem, 1)
                    wait(dve, ag["mmT"], ag["mmT"].prev(q + 2 * EG))
                    wait(dve, h1["t"], h1["t"].done(q))
                    stt(out=scratch(M), in0=scratch(9), scalar=0.0, in1=scratch(10), op0=ALU.max, op1=ALU.add).then_inc(h1["s1"].sem, 1)
                    wait(dve, h1["s1"], h1["s1"].done(q))
                    dve.sem_inc(ag["m"].sem, 1)
                    wait(dve, d1_p, q * 32 + 32)
                    ts(CS, XM[:, :, D], 1.0, None, ALU.max).then_inc(d1["c"].sem, 1)
                    wait(dve, d1["c"], d1["c"].done(q))
                    hold(dve)
                    dve.reciprocal(RCD[:, span(q)], CS).then_inc(d1["rc"].sem, 1)
                    wait(dve, d1["nd"], d1["nd"].done(q))
                    wait(dve, d1["x2"], d1["x2"].prev(q))
                    wait(dve, d1["mm"], d1["mm"].done(q))
                    for k in range(G):
                        last = stt(out=scratch(4)[:, k, :], in0=XM[:, k, 0:D], scalar=NDD[:, k:k + 1], in1=pXt[:, k, :], op0=ALU.mult, op1=ALU.add)
                    last.then_inc(d1["y"].sem, 1)
                    for k in range(G):
                        last = stt(out=scratch(1)[:, k, :], in0=scratch(1)[:, k, :], scalar=NDD[:, k:k + 1], in1=blB[:, :], op0=ALU.mult, op1=ALU.add)
                    last.then_inc(d1["a"].sem, 1)
                    invert(d1["r"], q, R3, SD3, d1["sqrt"])
                    wait(dve, d1["r"], d1["r"].done(q))
                    for k in range(G):
                        last = ts(scratch(4)[:, k, :], scratch(4)[:, k, :], R3[:, k:k + 1], None, ALU.mult)
                    last.then_inc(d1["x1"].sem, 1)
                    wait(dve, d1["x1"], d1["x1"].done(q))
                    stt(out=scratch(4), in0=scratch(1), scalar=0.0, in1=scratch(4), op0=ALU.max, op1=ALU.add).then_inc(d1["s"].sem, 1)
                    wait(dve, d1["s"], d1["s"].done(q))
                    stats(d1["bn"], d1["ag"], q, lambda k: scratch(4)[:, k, :], 0)
                    invert(d1["r2"], q, R2, SD2, d1["sqrt2"])
                    wait(dve, d1_st, q * 16)
                    wait(dve, d1["r2"], d1["r2"].done(q))
                    norm(scratch(3), lambda k: scratch(4)[:, k, :], MVS, R2, d1["x2"])
            boundary(2, D)
            with dve.Fori(0, EG // 2) as i:
                for u in (0, 1):
                    q = i * 2 + u
                    zslot = scratch(5 if u == 0 else 10)
                    wait(dve, d2_p[u], i * 16 + 16)
                    wait(dve, d2_st[u], i * 16)
                    wait(dve, d2["mm"], d2["mm"].done(q))
                    for k in range(G):
                        last = stt(out=zslot[:, k, :], in0=scratch(3 + u)[:, k, :], scalar=col(RCD, q, k), in1=pXt[:, k, :], op0=ALU.mult, op1=ALU.add)
                    last.then_inc(d2["z"].sem, 1)
                    wait(dve, d2["stat"], d2["stat"].prev(q))
                    hold(dve)
                    dve.tensor_copy(EM, REP[:, span(q)]).then_inc(d2["em"].sem, 1)
                    wait(dve, gathered[u], i * (16 * G) + (5 * 8 * G * EG + 16 * G))
                    wait(dve, s4["mm"], s4["mm"].done(q))
                    for k in range(G):
                        last = stt(out=row(Z, q, k), in0=GS[:, u, k, 0:D], scalar=col(RC, q, k), in1=pZt[:, k, :], op0=ALU.mult, op1=ALU.add)
                    last.then_inc(s4["z"].sem, 1)
            wait(dve, p1["gram"], p1["gram"].prev(NG))
            wait(dve, s4["T"], s4["T"].prev(EG))
            link(dve.tensor_copy(GM, acc[:, 0, 0:D + 1]))
            dve.sem_inc(gr.sem, 1)
            gr_mm.passed(dve)
            link(tt(GP, pX[:, 0:D], w2a[:, :], ALU.mult))
            dve.sem_inc(gr_p.sem, 1)
            gr_q.passed(dve)
            wait(dve, d2["stat"], d2["stat"].prev(EG))
            link(dve.tensor_copy(rt[:, 0:2, :], acc[0:1, 1, 0:2 * D].rearrange("a (r f) -> a r f", r=2)))
            link(tt(rt[:, 0, :], rt[:, 0, :], pX[0:1, 512:512 + D], ALU.add))
            link(tt(rt[:, 1, :], rt[:, 1, :], pY[0:1, 0:D], ALU.add))
            batch_norm(2, rt[:, 0:2, :], NODES, rows[:, 3, :], rows[:, 4, :], rows[:, 5, :], bn2B[:, :, :])
            link(tt(w2s[:, :], w2a[:, :], bn2B[:, 0, :], ALU.mult))
            dve.sem_inc(bn_done[0].sem, 1)

            def p2_first(q, u):
                wait(dve, p2["exp"], p2["exp"].done(q))
                stt(out=scratch(3), in0=scratch(3), scalar=1.0, in1=scratch(u), op0=ALU.min, op1=ALU.add).then_inc(p2["t"].sem, 1)
                wait(dve, p2["t"], p2["t"].done(q))
                stt(out=scratch(4 + u), in0=pWt, scalar=0.0, in1=scratch(3), op0=ALU.max, op1=ALU.add).then_inc(p2["s"].sem, 1)
                wait(dve, p2["s"], p2["s"].done(q))
                stats(p2["bn"], p2["ag"], q, lambda k: scratch(4 + u)[:, k, :], 1)
                rsqrt_seed(p2["seed"], p2["ag"], q, 1)

            def p2_last(q, u):
                wait(dve, p2["o"], p2["o"].prev(q))
                wait(dve, p2["r"], p2["r"].done(q))
                for k in range(G):
                    last = stt(out=scratch(10 + u)[:, k, :], in0=scratch(4 + u)[:, k, :], scalar=RS[1][:, k:k + 1], in1=b3B[:, :],
                               op0=ALU.mult, op1=ALU.add)
                last.then_inc(p2["u"].sem, 1)
                wait(dve, p2["u"], p2["u"].done(q))
                stats(p2["bn2"], p2["ag2"], q, lambda k: scratch(10 + u)[:, k, :], 2)
                rsqrt_seed(p2["seed2"], p2["ag2"], q, 2)

            p2_first(0, 0)
            with dve.Fori(0, EG // 2) as i:
                for u in (0, 1):
                    q = i * 2 + u
                    wait(dve, s5["exp"], s5["exp"].prev(q))
                    tt(scratch(9), Z[:, span(q), :], over(bn2B[:, 0, :]), ALU.mult).then_inc(s5["v1"].sem, 1)
                    wait(dve, s5["v1"], s5["v1"].done(q))
                    tt(scratch(9), scratch(9), over(bn2B[:, 1, :]), ALU.add).then_inc(s5["v"].sem, 1)
                    p2_last(q, u)
                    wait(dve, s5["exp"], s5["exp"].done(q))
                    stt(out=XM[:, :, 0:D], in0=XM[:, :, 0:D], scalar=1.0, in1=YS[:, span(q), :], op0=ALU.min, op1=ALU.add).then_inc(s5["t"].sem, 1)
                    wait(dve, s5["t"], s5["t"].done(q))
                    stt(out=XM[:, :, 0:D], in0=scratch(9), scalar=0.0, in1=XM[:, :, 0:D], op0=ALU.max, op1=ALU.add).then_inc(s5["s1"].sem, 1)
                    wait(dve, s5["s1"], s5["s1"].done(q))
                    stats(s5["bn"], s5["ag"], q, lambda k: XM[:, k, 0:D], 0)
                    rsqrt_seed(s5["seed"], s5["ag"], q, 0)
                    p2_first(q + 1, 1 - u)
                    wait(dve, s5["r"], s5["r"].done(q))
                    tt(RW, RS[0], WE[:, span(q)], ALU.mult).then_inc(s5["rw"].sem, 1)
                    wait(dve, ag["mmT"], ag["mmT"].prev(q + 3 * EG))
                    wait(dve, s5["rw"], s5["rw"].done(q))
                    norm(scratch(M), lambda k: XM[:, k, 0:D], MVS, RW, ag["m"])
                    wait(dve, ag["m"], ag["m"].done(q + 3 * EG))
                    dve.sem_inc(s5["s"].sem, 1)
            boundary(3, D)
            with dve.Fori(0, EG // 2) as i:
                for u in (0, 1):
                    q = i * 2 + u
                    wait(dve, d3_l, q * 48 + 48)
                    tt(scratch(7), scratch(7), over(bn2B[:, 0, :]), ALU.mult).then_inc(d3["v1"].sem, 1)
                    wait(dve, d3["v1"], d3["v1"].done(q))
                    tt(scratch(7), scratch(7), over(bn2B[:, 1, :]), ALU.add).then_inc(d3["v"].sem, 1)
                    p2_last(q * 3 + EG, u)
                    p2_first(q * 3 + (EG + 1), 1 - u)
                    wait(dve, d3["exp"], d3["exp"].done(q))
                    stt(out=scratch(9), in0=scratch(9), scalar=1.0, in1=scratch(6), op0=ALU.min, op1=ALU.add).then_inc(d3["t"].sem, 1)
                    wait(dve, d3["t"], d3["t"].done(q))
                    stt(out=scratch(9), in0=scratch(7), scalar=0.0, in1=scratch(9), op0=ALU.max, op1=ALU.add).then_inc(d3["s"].sem, 1)
                    wait(dve, d3["s"], d3["s"].done(q))
                    stats(d3["bn"], d3["ag"], q, lambda k: scratch(9)[:, k, :], 0)
                    rsqrt_seed(d3["seed"], d3["ag"], q, 0)
                    p2_last(q * 3 + (EG + 1), 1 - u)
                    p2_first(q * 3 + (EG + 2), u)
                    wait(dve, d3["o"], d3["o"].prev(q))
                    wait(dve, d3["r"], d3["r"].done(q))
                    for k in range(G):
                        last = stt(out=XM[:, k, 0:D], in0=scratch(9)[:, k, :], scalar=RS[0][:, k:k + 1], in1=b3B[:, :], op0=ALU.mult, op1=ALU.add)
                    last.then_inc(d3["u"].sem, 1)
                    wait(dve, d3["u"], d3["u"].done(q))
                    tt(XM[:, :, 0:D], XM[:, :, 0:D], scratch(8), ALU.add).then_inc(d3["u2"].sem, 1)
                    wait(dve, d3["u2"], d3["u2"].done(q))
                    stats(d3["bn2"], d3["ag2"], q, lambda k: XM[:, k, 0:D], 3)
                    rsqrt_seed(d3["seed2"], d3["ag2"], q, 3)
                    p2_last(q * 3 + (EG + 2), u)
                    p2_first(q * 3 + (EG + 3), 1 - u)
                    wait(dve, d3["r2"], d3["r2"].done(q))
                    for k in range(G):
                        last = ts(row(YS, q, k), XM[:, k, 0:D], MVD[:, k, 0:1], RS[3][:, k:k + 1], ALU.subtract, ALU.mult)
                    last.then_inc(d3["o"].sem, 1)


def kernel(x, src, dst, edge_attr_128, edge_weight, L0_gnn_W_conv, L0_gnn_b_conv, L0_gnn_W_aggr, L0_gnn_b_aggr,
           L1_gnn_weight, L1_gnn_bias, L2_gnn_u, L2_gnn_W1, L2_gnn_b1, L2_gnn_g1, L2_gnn_be1, L2_gnn_W2, L2_gnn_b2,
           L2_gnn_g2, L2_gnn_be2, L3_gnn_W, L3_gnn_b):
    from concourse import bacc
    from concourse.bass_utils import run_bass_kernel_spmd

    x = np.asarray(x)
    src, dst, ea, w = (np.asarray(a) for a in (src, dst, edge_attr_128, edge_weight))
    xp = np.zeros((NPAD, D), x.dtype)
    xp[:NODES] = x
    xT = np.zeros((NG + 1, D, G * P), x.dtype)
    xT[:NG] = xp.reshape(P, NG, G, D).transpose(1, 3, 2, 0).reshape(NG, D, G * P)
    dst1 = np.full((EPAD + 1,), NPAD - 1, dst.dtype)
    dst1[0] = -1
    dst1[1:EDGES + 1] = dst
    srcp = np.full((EPAD,), NPAD - 1, src.dtype)
    srcp[:EDGES] = src
    wp = np.zeros((EPAD,), w.dtype)
    wp[:EDGES] = w
    eap = np.zeros((EPAD, D), ea.dtype)
    eap[:EDGES] = ea
    ins = dict(x=xp, xT=xT, edge_attr=eap, dst1=dst1, src=srcp, weight=wp,
               W_conv_T=np.ascontiguousarray(np.asarray(L0_gnn_W_conv).T), b_conv=L0_gnn_b_conv, W_aggr=L0_gnn_W_aggr,
               b_aggr=L0_gnn_b_aggr, W_l1=L1_gnn_weight, b_l1=L1_gnn_bias, W1=L2_gnn_W1, b1=L2_gnn_b1, g1=L2_gnn_g1,
               be1=L2_gnn_be1, W2=L2_gnn_W2, b2=L2_gnn_b2, g2=L2_gnn_g2, be2=L2_gnn_be2,
               W3_T=np.ascontiguousarray(np.asarray(L3_gnn_W).T), b3=L3_gnn_b)
    ins = {k: np.ascontiguousarray(np.asarray(v)) for k, v in ins.items()}
    nc = bacc.Bacc("TRN2", target_bir_lowering=False, num_devices=1)
    aps = {k: nc.dram_tensor("in_" + k, v.shape, mybir.dt.from_np(v.dtype), kind="ExternalInput").ap() for k, v in ins.items()}
    out = nc.dram_tensor("out", (NPAD, D), mybir.dt.float32, kind="ExternalOutput").ap()
    build(nc, out=out, **aps)
    r = run_bass_kernel_spmd(nc, [{"in_" + k: v for k, v in ins.items()}], core_ids=[0])
    return r.results[0]["out"][:NODES]
```

```python
import numpy as np
import concourse.bass as bass
from concourse import mybir
from contextlib import ExitStack

P = 128
D = 128
G = 7
NODES, EDGES = 50000, 12500
NT = 392
NG = NT // G
NPAD = P * NT
ET = 98
EG = ET // G
EPAD = ET * P
LASTROWS = EDGES - (ET - 1) * P
CW = 132
ZERO_ROW = EPAD - 1
NOWHERE = 100000.0
LN_EPS, BN_EPS = 1e-5, 1e-4
SEED = float(0x5F3759DF)
NEWTON = 3
ROUND = float(3 << 22)


class Step:

    def __init__(self, sem, lead=0, base=0):
        self.sem, self.lead, self.base = sem, lead, base

    def done(self, q):
        return q + (1 + self.lead + self.base)

    def prev(self, q):
        return q + (self.lead + self.base)

    def prev2(self, q):
        return q + (self.lead + self.base - 1)


class Mark:

    def __init__(self, sem, at):
        self.sem, self.at = sem, at

    def passed(self, eng):
        eng.wait_ge(self.sem, self.at)


class Chain:

    def __init__(self, sem, per, base=0):
        self.sem, self.per, self.base = sem, per, base

    def at(self, q, j):
        return q * self.per + (self.base * self.per + j)

    def done(self, q):
        return self.at(q, self.per)

    def prev(self, q):
        return self.at(q, 0)


def build(nc, x, xT, edge_attr, dst1, src, weight, W_conv_T, b_conv, W_aggr, b_aggr, W_l1, b_l1,
          W1, b1, g1, be1, W2, b2, g2, be2, W3_T, b3, out):
    f32, i32, f16, bf16 = mybir.dt.float32, mybir.dt.int32, mybir.dt.float16, mybir.dt.bfloat16
    ALU = mybir.AluOpType
    ACT = mybir.ActivationFunctionType
    AX = mybir.AxisListType

    ctx = ExitStack()
    with ctx:
        def sb(name, shape, dt=f32):
            return ctx.enter_context(nc.sbuf_tensor(name, shape, dt))

        def sem(name):
            return ctx.enter_context(nc.semaphore(name))

        def step(name, lead=0):
            return Step(sem(name), lead)

        def dram(name, shape, dt=f32):
            return nc.dram_tensor(name, shape, dt, kind="Internal").ap()

        def scratch(i):
            return WK[:, i, :].rearrange("p (k f) -> p k f", k=G)

        x2_dram = dram("x2_dram", (NG + 2, P, G * D))
        parts_dram = dram("parts_dram", (2, 3, D), bf16)
        lookup_dram = dram("lookup_dram", (NPAD, 2))
        table = [dram("sums0", (EPAD, CW))] + [dram(f"sums{n}", (EPAD, D)) for n in (1, 2, 3)]
        xd_dram = dram("xd_dram", (EG, P, G * D))
        zd_dram = dram("zd_dram", (EG, P, G * D))

        YS = sb("YS", [P, ET, D])
        Z = sb("Z", [P, ET, D])
        EQ = sb("EQ", [P, ET, P], bf16)
        WK = sb("WK", [P, 12, G * D])
        XM = sb("XM", [P, G, CW])
        PT = sb("PT", [P, 2, G, CW])
        GS = sb("GS", [P, 2, G, CW])
        ident = sb("ident", [P, P])
        ones = sb("ones", [P, P])
        wM = sb("wM", [P, D]); wA = sb("wA", [P, D]); wL = sb("wL", [P, D])
        w1a = sb("w1a", [P, D]); w1b = sb("w1b", [P, D])
        w2a = sb("w2a", [P, D]); w2b = sb("w2b", [P, D]); w2s = sb("w2s", [P, D])
        w3 = sb("w3", [P, D])
        blB = sb("blB", [P, D]); cB = sb("cB", [P, D]); b3B = sb("b3B", [P, D])
        bn1B = sb("bn1B", [P, 2, D]); bn2B = sb("bn2B", [P, 2, D])
        bias3 = sb("bias3", [3, D], bf16)
        ones3 = sb("ones3", [3, P], bf16)
        rows = sb("rows", [1, 7, D])
        bnrow = sb("bnrow", [1, 2, D])
        b0row = bnrow[:, 1, :]
        bconv = sb("bconv", [P, 1])
        eps_ln = sb("eps_ln", [P, 1])
        KD = sb("KD", [P, ET]); WE = sb("WE", [P, ET])
        NS = sb("NS", [P, ET]); ND = sb("ND", [P, ET]); RC = sb("RC", [P, ET]); RCD = sb("RCD", [P, ET])
        REP = sb("REP", [P, ET]); REAL = sb("REAL", [P, ET])
        SRCI = sb("SRCI", [P, ET], i32); DSTI = sb("DSTI", [P, ET], i32)
        POSI = sb("POSI", [P, ET], i32); OUTI = sb("OUTI", [P, ET], i32)
        IX = sb("IX", [P, 2, G], i32)
        MASK = sb("MASK", [P, NT])
        Cmat = sb("Cmat", [P, ET])
        REPI = sb("REPI", [P, 1], i32)
        FR = sb("FR", [P, CW]); LR = sb("LR", [P, CW])
        ZH = sb("ZH", [P, 512], f16)
        sc = sb("sc", [P, 8])
        small = sb("small", [P, 14, G])
        SS1, SD1, R1, SS2, SD2, R2, RM, SS3, SD3, R3, NDD, EM, CS, RW = (small[:, n, :] for n in range(14))
        RV, RS, RT, NB = (sb(name, [P, 4 * G]) for name in ("RV", "RS", "RT", "NB"))
        ST = sb("ST", [P, 4, G, 6])
        MV = sb("MV", [P, 4, G, 2])
        MVS, MV2, MV3, MVD = (MV[:, n, :, :] for n in range(4))
        acc = ctx.enter_context(nc.psum_tensor("acc", [P, 2, 512], f32))
        pX = ctx.enter_context(nc.psum_tensor("pX", [P, 1024], f32))
        pY = ctx.enter_context(nc.psum_tensor("pY", [P, 1024], f32))
        pZ = ctx.enter_context(nc.psum_tensor("pZ", [P, 1024], f32))
        pW = acc[:, :, :].rearrange("p a c -> p (a c)")

        EQF, M, WAT, AT2 = 6, 7, 8, 9

        def tiles(t):
            return t[:, 0:G * D].rearrange("p (k f) -> p k f", k=G)

        pXt, pYt, pZt, pWt = tiles(pX), tiles(pY), tiles(pZ), tiles(pW)

        kt = WK[0:ET, 0, 0:4 * P].rearrange("t (a e) -> t a e", a=4)
        kti = WK[0:ET, 1, 0:4 * P].bitcast(i32).rearrange("t (a e) -> t a e", a=4)
        wk_a, wk_b = WK[:, 2, :], WK[:, 3, :]
        PD, TD, PS_, TS_ = (WK[:, 4, n * ET:(n + 1) * ET] for n in range(4))
        KP, KS = WK[:, 3, 256:256 + ET], WK[:, 3, 384:384 + ET]
        RR = RCD[:, :]
        LK = WK[:, 6, 0:2 * ET].rearrange("p (t c) -> p t c", c=2)
        ones_t = WK[:, 6, 2 * ET:2 * ET + NT]
        rt = WK[0:1, 6, 0:6 * D].rearrange("a (r f) -> a r f", r=6)
        rest = WK[0:1, 6, 5 * D:6 * D]
        parts = WK[0:1, 2, 512:512 + 3 * D // 2].bitcast(bf16).rearrange("a (r f) -> a r f", r=3)
        GM, GP = WK[:, 7, 0:D + 1], WK[:, 7, 256:256 + D]
        iota_i = WK[:, 5, 0:NT].bitcast(i32)
        iota_h = WK[:, 5, NT:NT + NT // 2].bitcast(f16)
        OHP = WK[:, 10, :].bitcast(f16)[:, 0:4 * P].rearrange("p (a b c) -> p a b c", a=2, b=2)
        OHT = WK[:, 11, :].bitcast(f16)[:, 0:4 * NT].rearrange("p (a b c) -> p a b c", a=2, b=2)
        deg = WK[:, 7, 0:NT]; degout = WK[:, 8, 0:NT]
        cum = WK[:, 7, NT:2 * NT]; posn = WK[:, 8, NT:2 * NT]
        tabs = WK[:, 9, 0:2 * NT].rearrange("p (t c) -> p t c", c=2)
        tri = WK[:, 6, 0:P]

        carried = sem("waits_carried")
        consts = sem("constants_made")
        s_keys, s_wts, s_w32 = sem("keys_loaded"), sem("weights_loaded"), sem("previous_keys_loaded")
        vlink, glink = sem("vector_link"), sem("gpsimd_link")

        def marks(name, n):
            s_ = sem(name)
            return [Mark(s_, m + 1) for m in range(n)]

        (zeros, keys_f, idx_ready, comp_ready, lk_diag, cmask0, hist_out, rowtot, tab_ready, ns_in, ns_ready,
         bn_v1, bn_t1, bn_done1, gr, gr_p, bn_v2, bn_t2, bn_done2) = marks("vector_events", 19)
        (comp_mm, keys_T, lk_mm, rowoff, bn_b1, gr_mm, gr_q, bn_b2) = marks("tensor_events", 8)
        (ns_sq, bn_a1, bn_a2) = marks("scalar_events", 3)
        (cmask, mask1) = marks("gpsimd_events", 2)
        oh, ohmm = step("onehots_built"), step("onehots_counted", 1)
        zgroup = sem("zero_group_stored")
        tab_stored = sem("lookup_stored")
        rk_l, eq_built = [sem("rowkeys0"), sem("rowkeys1")], step("eq_built", 1)
        p1 = {k: step("p1_" + k, 1 if k in ("mm", "xm") else 0) for k in
              ("mm", "sq", "sqrt", "r", "s", "sq2", "sqrt2", "r2", "rm", "x2", "xm", "gram")}
        p1_x, p1_st = [sem("nodes_x0"), sem("nodes_x1")], [sem("p1_stored0"), sem("p1_stored1")]
        ag = {k: step("agg_" + k) for k in ("eqf", "m", "mmT", "aT", "mmP", "p", "cnt")}
        ag_st = [sem("agg_stored0"), sem("agg_stored1")]
        bd_l, bd_mm, bd_r, bd_sc = sem("boundary_rows_loaded"), sem("boundary_product"), sem("boundary_rows_ready"), sem("boundary_scattered")
        edge_sems, counted = {}, {}

        def edge_steps(*names):
            out_ = {}
            for k in names:
                if k not in edge_sems:
                    edge_sems[k], counted[k] = sem("edges_" + k), 0
                out_[k] = Step(edge_sems[k], 1 if k in ("raw", "y", "s", "eaT", "T", "z") else 0, counted[k])
                counted[k] += EG
            return out_

        xs = edge_steps("ix", "T", "aT", "mm", "raw", "ys")
        lk = edge_steps("ix")
        s1 = edge_steps("ix", "c", "rc", "nd", "y", "sq", "sqrt", "r", "x1")
        s2 = edge_steps("ix", "a", "a2", "s", "bn", "ag", "sqrt", "r", "x2", "keep", "eaT", "eaTc", "xT", "xTc", "z1", "zc", "sq", "stat", "em")
        d1 = edge_steps("ix", "T", "aT", "mm", "c", "rc", "nd", "y", "sq", "sqrt", "r", "x1", "a", "s", "bn", "ag", "sqrt2", "r2", "x2")
        s4 = edge_steps("ix", "cp", "T", "aT", "mm", "z")
        h1 = edge_steps("v1", "v", "exp", "t", "s1")
        s5 = edge_steps("v1", "v", "exp", "t", "s1", "s", "bn", "ag", "rw")
        d3 = edge_steps("v1", "v", "exp", "t", "s", "bn", "ag", "u", "u2", "bn2", "ag2", "o")
        lk_use = step("lookup_used", 1)
        gathered = [sem("gathered0"), sem("gathered1")]
        s2_ea = [sem("edge_features0"), sem("edge_features1")]
        bn_v, bn_t, bn_done, bn_b, bn_a = (bn_v1, bn_v2), (bn_t1, bn_t2), (bn_done1, bn_done2), (bn_b1, bn_b2), (bn_a1, bn_a2)
        d1_p, d1_st = sem("d1_sums"), sem("d1_stored")
        d2 = {k: step("d2_" + k, 1 if k in ("z", "T") else 0) for k in ("T", "aT", "mm", "z", "sq", "stat", "em")}
        d2_x, d2_p, d2_st = [sem("d2_x0"), sem("d2_x1")], [sem("d2_p0"), sem("d2_p1")], [sem("d2_stored0"), sem("d2_stored1")]
        p2 = {k: step("p2_" + k, 1 if k in ("t", "o") else 0) for k in ("T", "xT", "exp", "t", "bn", "ag", "u", "bn2", "ag2", "o")}
        for k in ("mm", "s"):
            p2[k] = Step(p1[k].sem, p1[k].lead, NG + 1)
        CHAIN = 4 + 3 * NEWTON
        inv = Chain(sem("inverse_roots"), CHAIN)
        p2_x, p2_st = [sem("p2_x0"), sem("p2_x1")], [sem("p2_stored0"), sem("p2_stored1")]
        d3_l = sem("d3_loaded")
        fin = sem("outputs_scattered")
        bias_st, bias_l = sem("bias_parts_stored"), sem("bias_parts_loaded")

        block = ctx.enter_context(nc.Block())

        def wait(eng, st, value):
            eng.wait_ge(st.sem if isinstance(st, (Step, Chain)) else st, value)

        def hold(eng):
            eng.sem_inc(carried, 1)

        def over(t):
            return t.unsqueeze(1).broadcast_to([P, G, D])

        def span(q):
            return bass.ds(q * G, G)

        @block.sync
        def _(sp):
            sp.dma_start(kti[:, 0, :], dst1[1:1 + EPAD].rearrange("(t p) -> t p", p=P)).then_inc(s_keys, 16)
            sp.dma_start(kti[:, 1, :], dst1[0:EPAD].rearrange("(t p) -> t p", p=P)).then_inc(s_keys, 16)
            sp.dma_start(kti[:, 2, :], src.rearrange("(t p) -> t p", p=P)).then_inc(s_keys, 16)
            sp.dma_start(kt[:, 3, :], weight.rearrange("(t p) -> t p", p=P)).then_inc(s_keys, 16)
            for to, of in ((wk_a[:, 0:D], W_conv_T), (wk_a[:, D:2 * D], W_aggr[0:D, :]), (wM, W_aggr[D:2 * D, :]),
                           (wL, W_l1), (w1a, W1[0:D, :]), (w1b, W1[D:2 * D, :]), (w2a, W2[0:D, :]),
                           (w2b, W2[D:2 * D, :]), (w3, W3_T)):
                sp.dma_start(to[:, :] if to.shape[1] == D else to, of).then_inc(s_wts, 16)
            sp.dma_start(blB[:, :], b_l1.rearrange("(a n) -> a n", a=1).broadcast_to([P, D])).then_inc(s_wts, 16)
            sp.dma_start(b3B[:, :], b3.rearrange("(a n) -> a n", a=1).broadcast_to([P, D])).then_inc(s_wts, 16)
            for n, r in enumerate((b1, g1, be1, b2, g2, be2, b_aggr)):
                sp.dma_start(rows[:, n, :], r.rearrange("(a n) -> a n", a=1)).then_inc(s_wts, 16)
            sp.dma_start(bconv[:, :], b_conv.rearrange("(n a) -> n a", a=1)).then_inc(s_wts, 16)

            def p1_load(q, u):
                wait(sp, p1["mm"], p1["mm"].prev2(q))
                sp.dma_start(WK[:, u, :], xT[bass.ds(q, 1), :, :].rearrange("a p c -> p (a c)")).then_inc(p1_x[u], 16)

            def p1_store(q, u):
                wait(sp, p1["x2"], p1["x2"].done(q))
                sp.dma_start(x2_dram[bass.ds(q, 1), :, :].rearrange("a p c -> p (a c)"), WK[:, 4 + u, :]).then_inc(p1_st[u], 16)

            def table_view(n, q, width):
                return table[n].rearrange("(t p) w -> p t w", p=P)[:, span(q), 0:width]

            def agg_store(n, q, i, u, width):
                a = n * EG + q
                wait(sp, ag["p"], ag["p"].done(a))
                sp.dma_start(table_view(n, q, width), PT[:, u, :, 0:width]).then_inc(ag_st[u], 16)

            def boundary(n, width):
                half = (n + 1) * EG // 2 * 16
                sp.wait_ge(ag_st[0], half)
                sp.wait_ge(ag_st[1], half)
                if n:
                    sp.wait_ge(bd_sc, 16 * n)
                t = table[n].rearrange("(t p) w -> t p w", p=P)
                sp.dma_start(FR[0:ET, 0:width], t[:, 0, :]).then_inc(bd_l, 16)
                sp.dma_start(LR[0:ET, 0:width], t[:, P - 1, :]).then_inc(bd_l, 16)

            def load_bias(n):
                sp.dma_start(parts_dram[n:n + 1, :, :], parts).then_inc(bias_st, 16)
                sp.wait_ge(bias_st, 16 * (n + 1))
                sp.dma_start(bias3[0:3, :], parts_dram[n, :, :]).then_inc(bias_l, 16)

            comp_ready.passed(sp)
            load_bias(0)
            zeros.passed(sp)
            for n in (0, 1):
                sp.dma_start(x2_dram[NG + n, :, :].rearrange("p (k f) -> p k f", k=G), XM[:, :, 0:D]).then_inc(zgroup, 16)
            sp.wait_ge(zgroup, 32)
            tab_ready.passed(sp)
            sp.dma_start(lookup_dram.rearrange("(p t) c -> p t c", p=P), tabs).then_inc(tab_stored, 16)
            sp.wait_ge(tab_stored, 16)
            p1_load(0, 0)
            sp.dma_start(WK[:, 1, :], xT[1, :, :]).then_inc(p1_x[1], 16)
            with sp.Fori(0, EG // 2) as i:
                for u in (0, 1):
                    q = i * 2 + u
                    wait(sp, eq_built, eq_built.prev2(q))
                    sp.dma_start(WK[:, 10 + u, :].bitcast(i32),
                                 dst1[bass.ds(q * (G * P) + 1, G * P)].rearrange("(a n) -> a n", a=1).broadcast_to([P, G * P]))\
                        .then_inc(rk_l[u], 16)
                    p1_load(q + 2, u)
                    p1_store(q, u)
            with sp.Fori(0, EG // 2) as i:
                for u in (0, 1):
                    q = i * 2 + u
                    p1_load(q + (EG + 2), u)
                    p1_store(q + EG, u)
                    agg_store(0, q, i, u, CW)
            boundary(0, CW)
            with sp.Fori(0, EG // 2) as i:
                for u in (0, 1):
                    q = i * 2 + u
                    p1_load(q + (2 * EG + 2), u)
                    p1_store(q + 2 * EG, u)
                    agg_store(1, q, i, u, D)
            boundary(1, D)
            with sp.Fori(0, EG // 2) as i:
                for u in (0, 1):
                    q = i * 2 + u
                    wait(sp, s2["eaT"], s2["eaT"].prev2(q))
                    sp.dma_start(scratch(10 + u), edge_attr.rearrange("(t p) f -> p t f", p=P)[:, span(q), :]).then_inc(s2_ea[u], 16)
                    p1_load(q + (3 * EG + 2), u)
                    p1_store(q + 3 * EG, u)
            sp.wait_ge(bd_sc, 32)
            wait(sp, p1["gram"], p1["gram"].prev(NG))
            for u in (0, 1):
                sp.wait_ge(p1_x[u], 16 * (NG // 2 + 1))
            with sp.Fori(0, EG // 2) as i:
                for u in (0, 1):
                    q = i * 2 + u
                    wait(sp, d1["s"], d1["s"].prev(q))
                    sp.dma_start(XM[:, :, :], table_view(0, q, CW)).then_inc(d1_p, 16)
                    sp.dma_start(scratch(1), table_view(1, q, D)).then_inc(d1_p, 16)
                    agg_store(2, q, i, u, D)
                    wait(sp, d1["x2"], d1["x2"].done(q))
                    sp.dma_start(xd_dram[bass.ds(q, 1), :, :].rearrange("a p c -> p (a c)"), WK[:, 3, :]).then_inc(d1_st, 16)
            boundary(2, D)
            sp.wait_ge(d1_st, 16 * EG)
            sp.wait_ge(bd_sc, 48)
            with sp.Fori(0, EG // 2) as i:
                for u in (0, 1):
                    q = i * 2 + u
                    wait(sp, d2["T"], d2["T"].prev2(q))
                    sp.dma_start(WK[:, u, :], xd_dram[bass.ds(q, 1), :, :].rearrange("a p c -> p (a c)")).then_inc(d2_x[u], 16)
                    wait(sp, d2["z"], d2["z"].prev2(q))
                    sp.dma_start(scratch(3 + u), table_view(2, q, D)).then_inc(d2_p[u], 16)
                    wait(sp, d2["z"], d2["z"].done(q))
                    sp.dma_start(zd_dram[bass.ds(q, 1), :, :].rearrange("a p c -> p (a c)"), WK[:, 5 if u == 0 else 10, :]).then_inc(d2_st[u], 16)

            def p2_load(q, u):
                wait(sp, p2["t"], p2["t"].prev2(q))
                sp.dma_start(WK[:, u, :], x2_dram[bass.ds(q, 1), :, :].rearrange("a p c -> p (a c)")).then_inc(p2_x[u], 16)

            def p2_store(q, u):
                wait(sp, p2["o"], p2["o"].done(q))
                sp.dma_start(out.rearrange("(p t) f -> p t f", p=P)[:, span(q), :], GS[:, u, :, 0:D]).then_inc(p2_st[u], 16)

            sp.wait_ge(p1_st[0], 16 * NG // 2)
            sp.wait_ge(p1_st[1], 16 * NG // 2)
            sp.wait_ge(d2_st[0], 16 * EG // 2)
            sp.wait_ge(d2_st[1], 16 * EG // 2)
            wait(sp, d2["stat"], d2["stat"].prev(EG))
            for u in (0, 1):
                sp.dma_start(WK[:, u, :], x2_dram[u, :, :]).then_inc(p2_x[u], 16)
            bn_done2.passed(sp)
            load_bias(1)
            with sp.Fori(0, EG // 2) as i:
                for u in (0, 1):
                    q = i * 2 + u
                    p2_load(q + 2, u)
                    agg_store(3, q, i, u, D)
                    p2_store(q, u)
            boundary(3, D)
            sp.wait_ge(bd_sc, 64)
            with sp.Fori(0, EG // 2) as i:
                for u in (0, 1):
                    q = i * 2 + u
                    wait(sp, d3["u2"], d3["u2"].prev(q))
                    sp.dma_start(WK[:, 6, :], xd_dram[bass.ds(q, 1), :, :].rearrange("a p c -> p (a c)")).then_inc(d3_l, 16)
                    sp.dma_start(WK[:, 7, :], zd_dram[bass.ds(q, 1), :, :].rearrange("a p c -> p (a c)")).then_inc(d3_l, 16)
                    sp.dma_start(scratch(8), table_view(3, q, D)).then_inc(d3_l, 16)
                    for n in range(3):
                        r = q * 3 + (EG + n)
                        v = (u + n) % 2
                        p2_load(r + 2, v)
                        p2_store(r, v)
            sp.wait_ge(p2_st[0], 16 * NG // 2)
            sp.wait_ge(p2_st[1], 16 * NG // 2)
            sp.wait_ge(p2_x[0], 16 * (NG // 2 + 1))
            sp.wait_ge(p2_x[1], 16 * (NG // 2 + 1))
            sp.wait_ge(fin, 16 * ET)

        @block.gpsimd
        def _(pool):
            pool.memset(ident[:, :], 0.0).then_inc(glink, 1)
            pool.memset(tri, 1.0).then_inc(glink, 1)
            pool.iota(iota_i, [[1, NT]], base=0, channel_multiplier=0).then_inc(consts, 1)
            pool.iota(sc[:, 0:1].bitcast(i32), [[0, 1]], base=P, channel_multiplier=P).then_inc(consts, 1)
            pool.wait_ge(glink, 2)
            pool.affine_select(out=ident[:, :], in_=ident[:, :], compare_op=ALU.not_equal, fill=1.0,
                               base=0, pattern=[[-1, P]], channel_multiplier=1).then_inc(consts, 1)
            pool.affine_select(out=tri, in_=tri, compare_op=ALU.is_gt, fill=0.0,
                               base=0, pattern=[[1, P]], channel_multiplier=-1).then_inc(consts, 1)

            def gather_group(q, u, ix, index, rows_of, width):
                hold(pool)
                pool.tensor_copy(IX[:, u, :], index[:, span(q)]).then_inc(ix.sem, 1)
                wait(pool, ix, ix.done(q))
                hold(pool)
                for k in range(G):
                    pool.indirect_dma_start(GS[:, u, k, 0:width], None, rows_of,
                                            bass.IndirectOffsetOnAxis(ap=IX[:, u, k:k + 1], axis=0)).then_inc(gathered[u], 16)

            idx_ready.passed(pool)
            with pool.Fori(0, EG // 2) as i:
                for u in (0, 1):
                    q = i * 2 + u
                    wait(pool, xs["raw"], xs["raw"].prev2(q))
                    gather_group(q, u, xs["ix"], SRCI, x, D)
            cmask0.passed(pool)
            pool.affine_select(out=Cmat[0:ET, :], in_=Cmat[0:ET, :], compare_op=ALU.is_gt, fill=0.0,
                               base=0, pattern=[[-1, ET]], channel_multiplier=1).then_inc(cmask.sem, 1)
            tab_ready.passed(pool)
            pool.affine_select(out=MASK[:, :], in_=MASK[:, :], compare_op=ALU.is_gt, fill=0.0,
                               base=NODES, pattern=[[-1, NT]], channel_multiplier=-NT).then_inc(mask1.sem, 1)
            pool.wait_ge(tab_stored, 16)
            with pool.Fori(0, EG // 2) as i:
                for u in (0, 1):
                    q = i * 2 + u
                    wait(pool, lk_use, lk_use.prev2(q))
                    gather_group(q, u, lk["ix"], SRCI, lookup_dram, 2)

            def scatter_boundary(n, width):
                pool.wait_ge(bd_r, n + 1)
                pool.indirect_dma_start(table[n], bass.IndirectOffsetOnAxis(ap=REPI[0:ET, 0:1], axis=0), LR[0:ET, 0:width], None,
                                        bounds_check=EPAD - 1, oob_is_err=False).then_inc(bd_sc, 16)
                pool.wait_ge(bd_sc, 16 * (n + 1))

            ns_ready.passed(pool)
            scatter_boundary(0, CW)
            with pool.Fori(0, EG // 2) as i:
                for u in (0, 1):
                    q = i * 2 + u
                    wait(pool, s1["y"], s1["y"].prev2(q))
                    gather_group(q, u, s1["ix"], POSI, table[0], CW)
            scatter_boundary(1, D)
            with pool.Fori(0, EG // 2) as i:
                for u in (0, 1):
                    q = i * 2 + u
                    wait(pool, s2["s"], s2["s"].prev2(q))
                    gather_group(q, u, s2["ix"], POSI, table[1], D)
            wait(pool, s2["s"], s2["s"].prev(EG))
            with pool.Fori(0, EG // 2) as i:
                for u in (0, 1):
                    q = i * 2 + u
                    wait(pool, d1["T"], d1["T"].prev2(q))
                    gather_group(q, u, d1["ix"], DSTI, x, D)
            scatter_boundary(2, D)
            wait(pool, d1["T"], d1["T"].prev(EG))
            with pool.Fori(0, EG // 2) as i:
                for u in (0, 1):
                    q = i * 2 + u
                    wait(pool, s4["z"], s4["z"].prev2(q))
                    gather_group(q, u, s4["ix"], POSI, table[2], D)

            wait(pool, s4["z"], s4["z"].prev(EG))
            bn_done2.passed(pool)
            with pool.Fori(0, EG // 2) as i:
                for u in (0, 1):
                    q = i * 2 + u
                    wait(pool, s5["s1"], s5["s1"].prev(q))
                    pool.tensor_tensor(scratch(9), Z[:, span(q), :], over(bn2B[:, 0, :]), ALU.mult).then_inc(s5["v1"].sem, 1)
                    wait(pool, s5["v1"], s5["v1"].done(q))
                    pool.tensor_tensor(scratch(9), scratch(9), over(bn2B[:, 1, :]), ALU.add).then_inc(s5["v"].sem, 1)
            scatter_boundary(3, D)
            with pool.Fori(0, EG // 2) as i:
                for u in (0, 1):
                    q = i * 2 + u
                    wait(pool, d3_l, q * 48 + 48)
                    pool.tensor_tensor(scratch(7), scratch(7), over(bn2B[:, 0, :]), ALU.mult).then_inc(d3["v1"].sem, 1)
                    wait(pool, d3["v1"], d3["v1"].done(q))
                    pool.tensor_tensor(scratch(7), scratch(7), over(bn2B[:, 1, :]), ALU.add).then_inc(d3["v"].sem, 1)
                    wait(pool, d3["u"], d3["u"].done(q))
                    pool.tensor_tensor(XM[:, :, 0:D], XM[:, :, 0:D], scratch(8), ALU.add).then_inc(d3["u2"].sem, 1)
            pool.wait_ge(p2_st[0], 16 * NG // 2)
            pool.wait_ge(p2_st[1], 16 * NG // 2)
            wait(pool, d3["o"], d3["o"].prev(EG))
            for t in range(ET):
                pool.indirect_dma_start(out, bass.IndirectOffsetOnAxis(ap=OUTI[:, t:t + 1], axis=0), YS[:, t, :], None,
                                        bounds_check=NODES - 1, oob_is_err=False).then_inc(fin, 16)
            pool.wait_ge(fin, 16 * ET)

        @block.tensor
        def _(pe):
            mm = pe.matmul

            def bias_first(to):
                for a, b in ((0, 4), (4, G)):
                    mm(to[:, a * D:b * D].rearrange("p (k f) -> p k f", f=D), ones3[0:3, :],
                       bias3[0:3, :].unsqueeze(1).broadcast_to([3, b - a, D]), start=True, stop=False, skip_group_check=True)

            for st in (ohmm, p1["mm"], s2["eaT"], xs["T"], d2["T"]):
                pe.sem_inc(st.sem, 1)
            pe.wait_ge(s_wts, 16 * 19)
            mm(pX[:, 0:D], wk_a[:, 0:D], wk_a[:, D:2 * D], start=True, stop=True)
            mm(pY[0:1, 0:D], bconv[:, 0:1], wk_a[:, D:2 * D], start=True, stop=True).then_inc(comp_mm.sem, 1)
            pe.wait_ge(consts, 4)
            keys_f.passed(pe)
            for a in range(4):
                last = pe.transpose(pZ[:, a * ET:(a + 1) * ET], kt[:, a, :], ident[0:ET, 0:ET])
            last.then_inc(keys_T.sem, 1)
            lk_diag.passed(pe)
            mm(pY[0:ET, 512:512 + ET], ones[0:ET, 0:ET], wk_b[0:ET, 0:ET], start=True, stop=True).then_inc(lk_mm.sem, 1)

            comp_ready.passed(pe)
            zeros.passed(pe)
            pe.wait_ge(bias_l, 16)
            for a in (0, 1):
                mm(acc[:, a, 0:NT], ZH[:, 0:P], ZH[:, 0:NT], start=True, stop=False, skip_group_check=True)
            with pe.Fori(0, EG // 2) as i:
                for u in (0, 1):
                    q = i * 2 + u
                    for k in range(G):
                        t = q * G + k
                        v = (u * G + k) % 2
                        wait(pe, oh, oh.done(t))
                        mm(acc[:, 0, 0:NT], OHP[:, v, 0, :], OHT[:, v, 0, :], start=False, stop=False, skip_group_check=True)
                        mm(acc[:, 1, 0:NT], OHP[:, v, 1, :], OHT[:, v, 1, :], start=False, stop=False, skip_group_check=True)\
                            .then_inc(ohmm.sem, 1)
                    wait(pe, gathered[u], i * (16 * G) + (0 * 8 * G * EG + 16 * G))
                    wait(pe, xs["aT"], xs["aT"].prev(q))
                    for k in range(G):
                        last = pe.transpose(pYt[:, k, :], GS[:, u, k, 0:D], ident[:, :])
                    last.then_inc(xs["T"].sem, 1)
                    wait(pe, xs["ys"], xs["ys"].prev(q))
                    wait(pe, xs["aT"], xs["aT"].done(q))
                    bias_first(pZ)
                    for k in range(G):
                        last = mm(pZt[:, k, :], scratch(WAT)[:, k, :], wM[:, :], start=False, stop=True, skip_group_check=True)
                    last.then_inc(xs["mm"].sem, 1)
            for a in (0, 1):
                last = mm(acc[:, a, 0:NT], ZH[:, 0:P], ZH[:, 0:NT], start=False, stop=True, skip_group_check=True)
            last.then_inc(ohmm.sem, 1)
            rowtot.passed(pe)
            mm(pY[:, 0:1], tri, cum[:, NT - 1:NT], start=True, stop=True).then_inc(rowoff.sem, 1)

            def p1_mm(q, h, u):
                wait(pe, p1_x[u], h * 16 + 16)
                wait(pe, p1["s"], p1["s"].prev(q))
                bias_first(pX)
                for k in range(G):
                    last = mm(pXt[:, k, :], WK[:, u, k * P:(k + 1) * P], wM[:, :], start=False, stop=True, skip_group_check=True)
                last.then_inc(p1["mm"].sem, 1)

            def p1_gram(q):
                wait(pe, p1["xm"], p1["xm"].done(q))
                for k in range(G):
                    last = mm(acc[:, 0, 0:D + 1], XM[:, k, 0:D], XM[:, k, 0:D + 1], start=False, stop=False, skip_group_check=True)
                last.then_inc(p1["gram"].sem, 1)

            def p1_next(n, q, i, u):
                p1_mm(q + (n * EG + 1), i + (n * (EG // 2) + u), 1 - u)

            def p1_group(n, q, i, u):
                p1_next(n, q, i, u)
                p1_gram(q + n * EG)

            def agg_sums(n, q):
                a = q + n * EG
                wait(pe, ag["eqf"], ag["eqf"].done(a))
                wait(pe, ag["aT"], ag["aT"].prev(a))
                wait(pe, ag["m"], ag["m"].done(a))
                for k in range(G):
                    last = mm(pYt[:, k, :], scratch(M)[:, k, :], scratch(EQF)[:, k, :], start=True, stop=True)
                last.then_inc(ag["mmT"].sem, 1)

            def agg_product(n, q, w):
                a = q + n * EG
                wait(pe, ag["p"], ag["p"].prev(a))
                wait(pe, ag["aT"], ag["aT"].done(a))
                for k in range(G):
                    last = mm(pZt[:, k, :], scratch(WAT)[:, k, :], w[:, :], start=True, stop=True)
                last.then_inc(ag["mmP"].sem, 1)

            def agg(n, q, w):
                agg_sums(n, q)
                agg_product(n, q, w)

            def boundary(n, width):
                pe.wait_ge(bd_l, 32 * (n + 1))
                if n == 0:
                    cmask.passed(pe)
                wait(pe, ag["p"], ag["p"].prev((n + 1) * EG))
                mm(pZ[0:ET, 0:width], Cmat[0:ET, :], FR[0:ET, 0:width], start=True, stop=True).then_inc(bd_mm, 1)

            hist_out.passed(pe)
            mm(acc[:, 0, 0:D + 1], ZH[:, 0:P], ZH[:, 0:D + 1], start=True, stop=False, skip_group_check=True)
            mm(acc[0:1, 1, 0:2 * D], ZH[:, 0:1], ZH[:, 0:2 * D], start=True, stop=False, skip_group_check=True)
            p1_mm(0, 0, 0)
            with pe.Fori(0, EG // 2) as i:
                for u in (0, 1):
                    p1_group(0, i * 2 + u, i, u)
            with pe.Fori(0, EG // 2) as i:
                for u in (0, 1):
                    q = i * 2 + u
                    p1_next(1, q, i, u)
                    agg_sums(0, q)
                    p1_gram(q + EG)
                    agg_product(0, q, wA)
            boundary(0, CW)
            with pe.Fori(0, EG // 2) as i:
                for u in (0, 1):
                    q = i * 2 + u
                    p1_group(2, q, i, u)
                    agg(1, q, wL)
            boundary(1, D)
            with pe.Fori(0, EG // 2) as i:
                for u in (0, 1):
                    q = i * 2 + u
                    p1_next(3, q, i, u)
                    wait(pe, s2_ea[u], i * 16 + 16)
                    wait(pe, s2["xTc"], s2["xTc"].prev(q))
                    for k in range(G):
                        last = pe.transpose(pYt[:, k, :], scratch(10 + u)[:, k, :], ident[:, :])
                    last.then_inc(s2["eaT"].sem, 1)
                    p1_gram(q + 3 * EG)
                    wait(pe, s2["eaTc"], s2["eaTc"].done(q))
                    wait(pe, s2["x2"], s2["x2"].done(q))
                    for k in range(G):
                        last = pe.transpose(pYt[:, k, :], scratch(M)[:, k, :], ident[:, :])
                    last.then_inc(s2["xT"].sem, 1)
                    wait(pe, s2["sq"], s2["sq"].prev(q))
                    wait(pe, s2["xTc"], s2["xTc"].done(q))
                    for k in range(G):
                        mm(pZt[:, k, :], scratch(WAT)[:, k, :], w1a[:, :], start=True, stop=False)
                        last = mm(pZt[:, k, :], scratch(AT2)[:, k, :], w1b[:, :], start=False, stop=True)
                    last.then_inc(s2["z1"].sem, 1)
                    wait(pe, s2["em"], s2["em"].done(q))
                    wait(pe, s2["sq"], s2["sq"].done(q))
                    hold(pe)
                    for k in range(G):
                        mm(acc[0:1, 1, 0:D], EM[:, k:k + 1], Z[:, bass.ds(q * G + k, 1), :].rearrange("p a f -> p (a f)"), start=False, stop=False, skip_group_check=True)
                        last = mm(acc[0:1, 1, D:2 * D], EM[:, k:k + 1], scratch(EQF)[:, k, :], start=False, stop=False, skip_group_check=True)
                    last.then_inc(s2["stat"].sem, 1)
            bn_t[0].passed(pe)
            mm(pX[:, 0:2 * D], ones[0:1, :], bnrow[0:1, :, :].rearrange("a b c -> a (b c)"), start=True, stop=True).then_inc(bn_b[0].sem, 1)
            bn_done[0].passed(pe)
            mm(acc[0:1, 1, 0:2 * D], ZH[:, 0:1], ZH[:, 0:2 * D], start=True, stop=False, skip_group_check=True)
            with pe.Fori(0, EG // 2) as i:
                for u in (0, 1):
                    q = i * 2 + u
                    wait(pe, gathered[u], i * (16 * G) + (4 * 8 * G * EG + 16 * G))
                    wait(pe, d1["y"], d1["y"].prev(q))
                    for k in range(G):
                        last = pe.transpose(pXt[:, k, :], GS[:, u, k, 0:D], ident[:, :])
                    last.then_inc(d1["T"].sem, 1)
                    agg(2, q, w2b)
                    wait(pe, d1["aT"], d1["aT"].done(q))
                    bias_first(pX)
                    for k in range(G):
                        last = mm(pXt[:, k, :], scratch(2)[:, k, :], wM[:, :], start=False, stop=True, skip_group_check=True)
                    last.then_inc(d1["mm"].sem, 1)
            boundary(2, D)
            pe.wait_ge(bd_r, 3)
            with pe.Fori(0, EG // 2) as i:
                for u in (0, 1):
                    q = i * 2 + u
                    wait(pe, d2_x[u], i * 16 + 16)
                    wait(pe, d2["z"], d2["z"].prev(q))
                    for k in range(G):
                        last = pe.transpose(pXt[:, k, :], scratch(u)[:, k, :], ident[:, :])
                    last.then_inc(d2["T"].sem, 1)
                    wait(pe, s4["aT"], s4["aT"].prev(q))
                    wait(pe, s4["cp"], s4["cp"].done(q))
                    for k in range(G):
                        last = pe.transpose(pYt[:, k, :], scratch(M)[:, k, :], ident[:, :])
                    last.then_inc(s4["T"].sem, 1)
                    wait(pe, d2["aT"], d2["aT"].done(q))
                    for k in range(G):
                        last = mm(pXt[:, k, :], scratch(2)[:, k, :], w2a[:, :], start=True, stop=True)
                    last.then_inc(d2["mm"].sem, 1)
                    wait(pe, s4["z"], s4["z"].prev(q))
                    wait(pe, s4["aT"], s4["aT"].done(q))
                    for k in range(G):
                        last = mm(pZt[:, k, :], scratch(WAT)[:, k, :], w2a[:, :], start=True, stop=True)
                    last.then_inc(s4["mm"].sem, 1)
                    wait(pe, d2["em"], d2["em"].done(q))
                    wait(pe, d2["sq"], d2["sq"].done(q))
                    for k in range(G):
                        mm(acc[0:1, 1, 0:D], EM[:, k:k + 1], scratch(5 if u == 0 else 10)[:, k, :], start=False, stop=False, skip_group_check=True)
                        last = mm(acc[0:1, 1, D:2 * D], EM[:, k:k + 1], scratch(EQF)[:, k, :], start=False, stop=False, skip_group_check=True)
                    last.then_inc(d2["stat"].sem, 1)
            gr.passed(pe)
            mm(pX[:, 0:D], GM[:, 0:D], w2a[:, :], start=True, stop=True)
            mm(pX[0:1, 512:512 + D], GM[:, D:D + 1], w2a[:, :], start=True, stop=True).then_inc(gr_mm.sem, 1)
            gr_p.passed(pe)
            mm(pY[0:1, 0:D], ones[:, 0:1], GP, start=True, stop=True).then_inc(gr_q.sem, 1)
            bn_t[1].passed(pe)
            mm(pX[:, 0:2 * D], ones[0:1, :], bnrow[0:1, :, :].rearrange("a b c -> a (b c)"), start=True, stop=True).then_inc(bn_b[0].sem, 1)
            bn_done[1].passed(pe)

            def p2_transpose(q, h, u):
                wait(pe, p2_x[u], h * 16 + 16)
                wait(pe, p2["xT"], p2["xT"].prev(q))
                for k in range(G):
                    last = pe.transpose(pXt[:, k, :], scratch(u)[:, k, :], ident[:, :])
                last.then_inc(p2["T"].sem, 1)

            def p2_product(q):
                wait(pe, p2["s"], p2["s"].prev(q))
                wait(pe, p2["xT"], p2["xT"].done(q))
                bias_first(pW)
                for k in range(G):
                    last = mm(pWt[:, k, :], scratch(2)[:, k, :], w2s[:, :], start=False, stop=True, skip_group_check=True)
                last.then_inc(p2["mm"].sem, 1)

            def p2_group(q, h, u):
                p2_product(q + 1)
                p2_transpose(q + 2, h, u)

            pe.wait_ge(bias_l, 32)
            p2_transpose(0, 0, 0)
            p2_product(0)
            p2_transpose(1, 0, 1)
            with pe.Fori(0, EG // 2) as i:
                for u in (0, 1):
                    q = i * 2 + u
                    p2_group(q, i + 1, u)
                    agg(3, q, w3)
            boundary(3, D)
            with pe.Fori(0, EG // 2) as i:
                for u in (0, 1):
                    q = i * 2 + u
                    for n in range(3):
                        r = (q * 3) + (EG + n)
                        p2_group(r, i * 3 + (EG // 2 + (3 * u + n) // 2 + 1), (u + n) % 2)

        @block.scalar
        def _(act):
            A = act.activation

            def square_sums(src_t, junk, ss, st):
                for k in range(G):
                    last = A(junk[:, k, 0:D], src_t[:, k, :], ACT.Square, accum_out=ss[:, k:k + 1])
                last.then_inc(st.sem, 1)

            def p1_first(q, u):
                wait(act, p1["xm"], p1["xm"].prev2(q))
                wait(act, p1["mm"], p1["mm"].done(q))
                hold(act)
                square_sums(pXt, scratch(2 + u), SS1, p1["sq"])
                wait(act, p1["sq"], p1["sq"].done(q))
                wait(act, p1["r"], p1["r"].prev(q))
                hold(act)
                A(SD1, SS1, ACT.Sqrt, bias=eps_ln[:, 0:1], scale=1.0 / D).then_inc(p1["sqrt"].sem, 1)

            def p1_second(q, u):
                wait(act, p1["gram"], p1["gram"].prev(q))
                wait(act, p1["s"], p1["s"].done(q))
                hold(act)
                square_sums(scratch(2 + u), XM, SS2, p1["sq2"])
                wait(act, p1["sq2"], p1["sq2"].done(q))
                wait(act, p1["r2"], p1["r2"].prev(q))
                hold(act)
                A(SD2, SS2, ACT.Sqrt, bias=eps_ln[:, 0:1], scale=1.0 / D).then_inc(p1["sqrt2"].sem, 1)

            def agg_eq(n, q):
                a = q + n * EG
                wait(act, ag["mmT"], ag["mmT"].prev(a))
                hold(act)
                A(scratch(EQF), EQ[:, span(q), :], ACT.Copy).then_inc(ag["eqf"].sem, 1)

            def agg_sums(n, q):
                a = q + n * EG
                wait(act, ag["mmP"], ag["mmP"].prev(a))
                wait(act, ag["mmT"], ag["mmT"].done(a))
                hold(act)
                A(scratch(WAT), pYt, ACT.Copy).then_inc(ag["aT"].sem, 1)

            def agg_rows(n, q, i, u):
                a = q + n * EG
                wait(act, ag_st[u], (i + n * (EG // 2)) * 16)
                wait(act, ag["mmP"], ag["mmP"].done(a))
                if n == 0:
                    wait(act, ag["cnt"], ag["cnt"].done(a))
                hold(act)
                A(PT[:, u, :, 0:D], pZt, ACT.Copy).then_inc(ag["p"].sem, 1)

            def agg(n, q, i, u):
                agg_sums(n, q)
                agg_rows(n, q, i, u)

            for st in (xs["raw"], p2["o"]):
                act.sem_inc(st.sem, 1)
            with act.Fori(0, EG // 2) as i:
                for u in (0, 1):
                    q = i * 2 + u
                    wait(act, xs["mm"], xs["mm"].prev(q))
                    wait(act, xs["T"], xs["T"].done(q))
                    hold(act)
                    A(scratch(WAT), pYt, ACT.Copy).then_inc(xs["aT"].sem, 1)
                    wait(act, gathered[u], i * (16 * G) + (0 * 8 * G * EG + 16 * G))
                    hold(act)
                    A(Z[:, span(q), :], GS[:, u, :, 0:D], ACT.Copy).then_inc(xs["raw"].sem, 1)
                    wait(act, xs["mm"], xs["mm"].done(q))
                    hold(act)
                    A(YS[:, span(q), :], pZt, ACT.Copy).then_inc(xs["ys"].sem, 1)
            comp_ready.passed(act)
            act.wait_ge(tab_stored, 16)
            p1_first(0, 0)
            with act.Fori(0, EG // 2) as i:
                for u in (0, 1):
                    q = i * 2 + u
                    p1_second(q, u)
                    p1_first(q + 1, 1 - u)
            ns_in.passed(act)
            A(NS[:, :], RR, ACT.Sqrt).then_inc(ns_sq.sem, 1)
            ns_ready.passed(act)
            with act.Fori(0, EG // 2) as i:
                for u in (0, 1):
                    q = i * 2 + u
                    agg_eq(0, q)
                    p1_second(q + EG, u)
                    agg_sums(0, q)
                    p1_first(q + (EG + 1), 1 - u)
                    agg_rows(0, q, i, u)
            with act.Fori(0, EG // 2) as i:
                for u in (0, 1):
                    q = i * 2 + u
                    p1_second(q + 2 * EG, u)
                    agg_eq(1, q)
                    wait(act, s1["y"], s1["y"].prev(q))
                    wait(act, s1["rc"], s1["rc"].done(q))
                    hold(act)
                    A(ND[:, span(q)], RC[:, span(q)], ACT.Sqrt).then_inc(s1["nd"].sem, 1)
                    p1_first(q + (2 * EG + 1), 1 - u)
                    wait(act, ag["mmT"], ag["mmT"].prev(q + EG))
                    wait(act, s1["y"], s1["y"].done(q))
                    hold(act)
                    for k in range(G):
                        last = A(scratch(M)[:, k, :], YS[:, bass.ds(q * G + k, 1), :].rearrange("p a f -> p (a f)"), ACT.Square, accum_out=SS3[:, k:k + 1])
                    last.then_inc(s1["sq"].sem, 1)
                    wait(act, s1["r"], s1["r"].prev(q))
                    wait(act, s1["sq"], s1["sq"].done(q))
                    hold(act)
                    A(SD3, SS3, ACT.Sqrt, bias=eps_ln[:, 0:1], scale=1.0 / D).then_inc(s1["sqrt"].sem, 1)
                    agg(1, q, i, u)
            with act.Fori(0, EG // 2) as i:
                for u in (0, 1):
                    q = i * 2 + u
                    p1_second(q + 3 * EG, u)
                    wait(act, s2["r"], s2["r"].prev(q))
                    wait(act, s2["ag"], s2["ag"].done(q))
                    hold(act)
                    A(SD3, MVS[:, :, 1], ACT.Sqrt, bias=eps_ln[:, 0:1], scale=1.0).then_inc(s2["sqrt"].sem, 1)
                    wait(act, s2["z1"], s2["z1"].prev(q))
                    wait(act, s2["eaT"], s2["eaT"].done(q))
                    hold(act)
                    A(scratch(AT2), pYt, ACT.Copy).then_inc(s2["eaTc"].sem, 1)
                    p1_first(q + (3 * EG + 1), 1 - u)
                    wait(act, s2["x2"], s2["x2"].done(q))
                    hold(act)
                    A(YS[:, span(q), :], scratch(M), ACT.Copy).then_inc(s2["keep"].sem, 1)
                    wait(act, s2["xT"], s2["xT"].done(q))
                    hold(act)
                    A(scratch(WAT), pYt, ACT.Copy).then_inc(s2["xTc"].sem, 1)
                    wait(act, s2["z1"], s2["z1"].done(q))
                    wait(act, s2["stat"], s2["stat"].prev(q))
                    hold(act)
                    A(Z[:, span(q), :], pZt, ACT.Copy).then_inc(s2["zc"].sem, 1)
                    A(scratch(EQF), pZt, ACT.Square).then_inc(s2["sq"].sem, 1)
            bn_v[0].passed(act)
            A(rt[:, 3, :], rt[:, 2, :], ACT.Sqrt).then_inc(bn_a[0].sem, 1)
            bn_done[0].passed(act)
            with act.Fori(0, EG // 2) as i:
                for u in (0, 1):
                    q = i * 2 + u
                    agg_eq(2, q)
                    wait(act, h1["s1"], h1["s1"].prev(q))
                    wait(act, h1["v"], h1["v"].done(q))
                    hold(act)
                    A(scratch(10), scratch(9), ACT.Exp).then_inc(h1["exp"].sem, 1)
                    wait(act, d1["mm"], d1["mm"].prev(q))
                    wait(act, d1["T"], d1["T"].done(q))
                    hold(act)
                    A(scratch(2), pXt, ACT.Copy).then_inc(d1["aT"].sem, 1)
                    agg(2, q, i, u)
                    wait(act, d1["x1"], d1["x1"].prev(q))
                    wait(act, d1["rc"], d1["rc"].done(q))
                    hold(act)
                    A(NDD, RCD[:, span(q)], ACT.Sqrt).then_inc(d1["nd"].sem, 1)
                    wait(act, d1["y"], d1["y"].done(q))
                    hold(act)
                    square_sums(scratch(4), scratch(5), SS3, d1["sq"])
                    wait(act, d1["sq"], d1["sq"].done(q))
                    hold(act)
                    A(SD3, SS3, ACT.Sqrt, bias=eps_ln[:, 0:1], scale=1.0 / D).then_inc(d1["sqrt"].sem, 1)
                    wait(act, d1["r2"], d1["r2"].prev(q))
                    wait(act, d1["ag"], d1["ag"].done(q))
                    hold(act)
                    A(SD2, MVS[:, :, 1], ACT.Sqrt, bias=eps_ln[:, 0:1], scale=1.0).then_inc(d1["sqrt2"].sem, 1)
            with act.Fori(0, EG // 2) as i:
                for u in (0, 1):
                    q = i * 2 + u
                    wait(act, s4["T"], s4["T"].prev(q))
                    hold(act)
                    A(scratch(M), YS[:, span(q), :], ACT.Copy).then_inc(s4["cp"].sem, 1)
                    wait(act, d2["mm"], d2["mm"].prev(q))
                    wait(act, d2["T"], d2["T"].done(q))
                    hold(act)
                    A(scratch(2), pXt, ACT.Copy).then_inc(d2["aT"].sem, 1)
                    wait(act, s4["mm"], s4["mm"].prev(q))
                    wait(act, s4["T"], s4["T"].done(q))
                    hold(act)
                    A(scratch(WAT), pYt, ACT.Copy).then_inc(s4["aT"].sem, 1)
                    wait(act, d2["stat"], d2["stat"].prev(q))
                    wait(act, d2["z"], d2["z"].done(q))
                    hold(act)
                    A(scratch(EQF), scratch(5 if u == 0 else 10), ACT.Square).then_inc(d2["sq"].sem, 1)
            bn_v[1].passed(act)
            A(rt[:, 3, :], rt[:, 2, :], ACT.Sqrt).then_inc(bn_a[0].sem, 1)
            bn_done[1].passed(act)

            def p2_copy(q):
                wait(act, p2["mm"], p2["mm"].prev(q))
                wait(act, p2["T"], p2["T"].done(q))
                hold(act)
                A(scratch(2), pXt, ACT.Copy).then_inc(p2["xT"].sem, 1)

            def p2_exp(q):
                wait(act, p2["t"], p2["t"].prev(q))
                wait(act, p2["mm"], p2["mm"].done(q))
                hold(act)
                A(scratch(3), pWt, ACT.Exp).then_inc(p2["exp"].sem, 1)

            def p2_out(q, h, u):
                wait(act, p2_st[u], h * 16)
                wait(act, inv, inv.done(q + 1))
                hold(act)
                for k in range(G):
                    last = A(GS[:, u, k, 0:D], scratch(10 + u)[:, k, :], ACT.Identity, bias=NB[:, 2 * G + k:2 * G + k + 1],
                             scale=RS[:, 2 * G + k:2 * G + k + 1])
                last.then_inc(p2["o"].sem, 1)

            p2_copy(0)
            p2_exp(0)
            p2_copy(1)
            with act.Fori(0, EG // 2) as i:
                for u in (0, 1):
                    q = i * 2 + u
                    p2_exp(q + 1)
                    agg_eq(3, q)
                    wait(act, s5["s"], s5["s"].prev(q))
                    wait(act, s5["v"], s5["v"].done(q))
                    hold(act)
                    A(XM[:, :, 0:D], scratch(9), ACT.Exp).then_inc(s5["exp"].sem, 1)
                    p2_copy(q + 2)
                    p2_out(q, i, u)
                    agg(3, q, i, u)
            with act.Fori(0, EG // 2) as i:
                for u in (0, 1):
                    q = i * 2 + u
                    for n in range(3):
                        r = (q * 3) + (EG + n)
                        p2_exp(r + 1)
                        p2_copy(r + 2)
                        if n == 0:
                            wait(act, d3["u"], d3["u"].prev(q))
                            wait(act, d3["v"], d3["v"].done(q))
                            hold(act)
                            A(scratch(9), scratch(7), ACT.Exp).then_inc(d3["exp"].sem, 1)
                        if n == 2:
                            wait(act, inv, inv.done(r))
                            hold(act)
                            for k in range(G):
                                last = A(YS[:, bass.ds(q * G + k, 1), :].rearrange("p a f -> p (a f)"), XM[:, k, 0:D], ACT.Identity,
                                         bias=NB[:, 3 * G + k:3 * G + k + 1], scale=RS[:, 3 * G + k:3 * G + k + 1])
                            last.then_inc(d3["o"].sem, 1)
                        p2_out(r, i * 3 + (EG // 2 + (3 * u + n) // 2), (u + n) % 2)

        @block.vector
        def _(dve):
            chain = [0]

            def link(ins):
                chain[0] += 1
                ins.then_inc(vlink, 1)
                dve.wait_ge(vlink, chain[0])

            ts, tt, stt = dve.tensor_scalar, dve.tensor_tensor, dve.scalar_tensor_tensor

            def row(t, q, k):
                return t[:, bass.ds(q * G + k, 1), :].rearrange("p a f -> p (a f)")

            def col(t, q, k):
                return t[:, bass.ds(q * G + k, 1)]

            for st in (lk_use, eq_built, p1["xm"], s1["y"], s2["s"], s4["z"], d2["z"], p2["t"]):
                dve.sem_inc(st.sem, 1)
            dve.memset(ones[:, :], 1.0)
            dve.memset(ones3[:, :], 1.0)
            dve.memset(eps_ln[:, :], LN_EPS)
            dve.memset(ZH[:, :], 0.0)
            dve.memset(PT[:, :, :, :], 0.0)
            dve.memset(ones_t, 1.0)
            dve.memset(Cmat[:, :], 0.0)
            dve.memset(XM[:, :, :], 0.0).then_inc(zeros.sem, 1)
            zeros.passed(dve)
            dve.wait_ge(s_keys, 64)
            dve.tensor_copy(kt[:, 0:3, :], kti[:, 0:3, :]).then_inc(keys_f.sem, 1)
            dve.wait_ge(consts, 4)
            dve.tensor_copy(iota_h, iota_i)
            dve.tensor_copy(sc[:, 1:2], sc[:, 0:1].bitcast(i32))
            keys_T.passed(dve)
            dve.tensor_copy(KD[:, :], pZ[:, 0:ET])
            dve.tensor_copy(KP, pZ[:, ET:2 * ET])
            dve.tensor_copy(KS, pZ[:, 2 * ET:3 * ET])
            link(dve.tensor_copy(WE[:, :], pZ[:, 3 * ET:4 * ET]))
            dve.tensor_copy(SRCI[:, :], KS)
            dve.tensor_copy(DSTI[:, :], KD[:, :]).then_inc(idx_ready.sem, 1)
            for key, p_, t_ in ((KD[:, :], PD, TD), (KS, PS_, TS_)):
                link(ts(p_, key, -(NT - 1) / 2.0, 1.0 / NT, ALU.add, ALU.mult))
                link(ts(p_, p_, ROUND, None, ALU.add))
                link(ts(p_, p_, -ROUND, None, ALU.add))
                link(stt(out=t_, in0=p_, scalar=-float(NT), in1=key, op0=ALU.mult, op1=ALU.add))
            link(ts(REAL[:, :], KD[:, :], float(NODES), None, ALU.is_lt))
            link(tt(REP[:, :], KD[:, :], KP, ALU.not_equal))
            link(tt(REP[:, :], REP[:, :], REAL[:, :], ALU.mult))
            link(ts(RC[:, :], REP[:, :], -NOWHERE, NOWHERE, ALU.mult, ALU.add))
            link(tt(RC[:, :], RC[:, :], KD[:, :], ALU.add))
            dve.tensor_copy(OUTI[:, :], RC[:, :])
            dve.wait_ge(s_wts, 16 * 19)

            def split(row_):
                link(dve.tensor_copy(parts[:, 0, :], row_))
                link(tt(rest, row_, parts[:, 0, :], ALU.subtract))
                link(dve.tensor_copy(parts[:, 1, :], rest))
                link(tt(rest, rest, parts[:, 1, :], ALU.subtract))
                link(dve.tensor_copy(parts[:, 2, :], rest))

            def centre(w, rows_, scratch_col):
                link(dve.tensor_reduce(scratch_col, w, axis=AX.X, op=ALU.add))
                link(ts(scratch_col, scratch_col, 1.0 / D, None, ALU.mult))
                link(ts(w, w, scratch_col, None, ALU.subtract))

            link(tt(wM[:, :], wM[:, :], ident[:, :], ALU.add))
            centre(wM[:, :], P, sc[:, 2:3])
            comp_mm.passed(dve)
            link(dve.tensor_copy(wA[:, :], pX[:, 0:D]))
            centre(wA[:, :], P, sc[:, 2:3])
            link(tt(b0row, pY[0:1, 0:D], rows[:, 6, :], ALU.add))
            centre(b0row, 1, sc[0:1, 2:3])
            link(ts(cB[:, :], blB[:, :], 0.0, None, ALU.max))
            centre(cB[:, :], P, sc[:, 2:3])
            split(b0row)
            dve.sem_inc(comp_ready.sem, 1)
            link(ts(wk_b[0:ET, 0:ET], ident[0:ET, 0:ET], kt[:, 0, P - 1:P], None, ALU.mult))
            dve.sem_inc(lk_diag.sem, 1)
            lk_mm.passed(dve)
            ts(Cmat[0:ET, :], pY[0:ET, 512:512 + ET], kt[:, 0, 0:1], None, ALU.is_equal).then_inc(cmask0.sem, 1)
            link(ts(wk_a[0:ET, 0:P], kt[:, 0, :], kt[:, 0, P - 1:P], None, ALU.is_equal))
            link(dve.tensor_reduce(sc[0:ET, 2:3], wk_a[0:ET, 0:P], axis=AX.X, op=ALU.add))
            link(ts(sc[0:ET, 3:4], sc[0:ET, 2:3], float(P), None, ALU.is_ge))
            link(ts(sc[0:ET, 4:5], kt[:, 1, 0:1], kt[:, 0, P - 1:P], None, ALU.is_equal))
            link(tt(sc[0:ET, 3:4], sc[0:ET, 3:4], sc[0:ET, 4:5], ALU.mult))
            link(tt(sc[0:ET, 1:2], sc[0:ET, 1:2], sc[0:ET, 2:3], ALU.subtract))
            link(stt(out=sc[0:ET, 1:2], in0=sc[0:ET, 3:4], scalar=NOWHERE, in1=sc[0:ET, 1:2], op0=ALU.mult, op1=ALU.add))
            link(dve.tensor_copy(REPI[0:ET, :], sc[0:ET, 1:2]))

            with dve.Fori(0, EG // 2) as i:
                for u in (0, 1):
                    q = i * 2 + u
                    for k in range(G):
                        t = q * G + k
                        v = (u * G + k) % 2
                        wait(dve, ohmm, ohmm.prev2(t))
                        ts(OHP[:, v, 0, :], iota_h[:, 0:P], PD[:, bass.ds(t, 1)], None, ALU.is_equal)
                        ts(OHT[:, v, 0, :], iota_h[:, 0:NT], TD[:, bass.ds(t, 1)], None, ALU.is_equal)
                        ts(OHP[:, v, 1, :], iota_h[:, 0:P], PS_[:, bass.ds(t, 1)], None, ALU.is_equal)
                        ts(OHT[:, v, 1, :], iota_h[:, 0:NT], TS_[:, bass.ds(t, 1)], None, ALU.is_equal).then_inc(oh.sem, 1)
            wait(dve, ohmm, ohmm.prev(ET + 1))
            wait(dve, xs["ys"], xs["ys"].prev(EG))
            dve.tensor_copy(degout, acc[:, 1, 0:NT])
            link(dve.tensor_copy(deg, acc[:, 0, 0:NT]))
            dve.sem_inc(hist_out.sem, 1)
            link(dve.tensor_tensor_scan(cum, ones_t, deg, 0.0, ALU.mult, ALU.add))
            dve.sem_inc(rowtot.sem, 1)
            rowoff.passed(dve)
            link(dve.tensor_copy(sc[:, 5:6], pY[:, 0:1]))
            link(tt(posn, cum, deg, ALU.subtract))
            link(ts(posn, posn, sc[:, 5:6], None, ALU.add))
            link(ts(MASK[:, :], deg, 0.0, None, ALU.is_equal))
            link(ts(cum, posn, -1.0, float(ZERO_ROW), ALU.mult, ALU.add))
            link(tt(cum, cum, MASK[:, :], ALU.mult))
            dve.tensor_copy(tabs[:, :, 0], degout)
            link(tt(tabs[:, :, 1], posn, cum, ALU.add))
            dve.sem_inc(tab_ready.sem, 1)
            mask1.passed(dve)

            def invert(st, q, r, sd, after):
                wait(dve, after, after.done(q))
                dve.reciprocal(r, sd).then_inc(st.sem, 1)

            def p1_first(q, u):
                wait(dve, p1["s"], p1["s"].prev(q))
                invert(p1["r"], q, R1, SD1, p1["sqrt"])
                wait(dve, p1["r"], p1["r"].done(q))
                for k in range(G):
                    last = stt(out=scratch(2 + u)[:, k, :], in0=pXt[:, k, :], scalar=R1[:, k:k + 1], in1=cB[:, :],
                               op0=ALU.mult, op1=ALU.add)
                last.then_inc(p1["s"].sem, 1)

            def p1_second(q, h, u):
                wait(dve, p1["xm"], p1["xm"].prev(q))
                invert(p1["r2"], q, R2, SD2, p1["sqrt2"])
                wait(dve, p1_st[u], h * 16)
                wait(dve, p1["r2"], p1["r2"].done(q))
                tt(RM, R2, MASK[:, span(q)], ALU.mult).then_inc(p1["rm"].sem, 1)
                for k in range(G):
                    last = ts(scratch(4 + u)[:, k, :], scratch(2 + u)[:, k, :], R2[:, k:k + 1], None, ALU.mult)
                last.then_inc(p1["x2"].sem, 1)
                wait(dve, p1["rm"], p1["rm"].done(q))
                hold(dve)
                dve.tensor_copy(XM[:, :, D], MASK[:, span(q)])
                for k in range(G):
                    last = ts(XM[:, k, 0:D], scratch(2 + u)[:, k, :], RM[:, k:k + 1], None, ALU.mult)
                last.then_inc(p1["xm"].sem, 1)

            def p1_this(n, q, i, u):
                p1_second(q + n * EG, i + n * (EG // 2), u)

            def p1_next(n, q, u):
                p1_first(q + (n * EG + 1), 1 - u)

            def p1_group(n, q, i, u):
                p1_this(n, q, i, u)
                p1_next(n, q, u)

            def boundary(n, width):
                dve.wait_ge(bd_mm, n + 1)
                tt(LR[0:ET, 0:width], LR[0:ET, 0:width], pZ[0:ET, 0:width], ALU.add).then_inc(bd_r, 1)

            p1_first(0, 0)
            with dve.Fori(0, EG // 2) as i:
                for u in (0, 1):
                    q = i * 2 + u
                    wait(dve, gathered[u], i * (16 * G) + (1 * 8 * G * EG + 16 * G))
                    hold(dve)
                    dve.tensor_copy(LK[:, span(q), :], GS[:, u, :, 0:2]).then_inc(lk_use.sem, 1)
                    wait(dve, rk_l[u], i * 16 + 16)
                    for k in range(G):
                        last = ts(row(EQ, q, k), WK[:, 10 + u, k * P:(k + 1) * P].bitcast(i32), col(KD, q, k), None, ALU.is_equal)
                    last.then_inc(eq_built.sem, 1)
                    p1_group(0, q, i, u)
            wait(dve, eq_built, eq_built.prev(EG))
            wait(dve, lk_use, lk_use.prev(EG))
            dve.memset(EQ[:, ET - 1, LASTROWS:P], 0.0)
            dve.tensor_copy(POSI[:, :], LK[:, :, 1])
            link(ts(RR, LK[:, :, 0], 1.0, None, ALU.max))
            link(dve.reciprocal(RR, RR))
            dve.sem_inc(ns_in.sem, 1)
            ns_sq.passed(dve)
            dve.sem_inc(ns_ready.sem, 1)
            with dve.Fori(0, EG // 2) as i:
                for u in (0, 1):
                    q = i * 2 + u
                    wait(dve, ag["mmT"], ag["mmT"].prev(q))
                    for k in range(G):
                        last = ts(scratch(M)[:, k, :], row(Z, q, k), col(NS, q, k), None, ALU.mult)
                    last.then_inc(ag["m"].sem, 1)
                    wait(dve, ag_st[u], i * 16)
                    wait(dve, ag["eqf"], ag["eqf"].done(q))
                    dve.tensor_reduce(PT[:, u, :, D], scratch(EQF), axis=AX.X, op=ALU.add).then_inc(ag["cnt"].sem, 1)
                    p1_group(1, q, i, u)
            boundary(0, CW)
            with dve.Fori(0, EG // 2) as i:
                for u in (0, 1):
                    q = i * 2 + u
                    wait(dve, gathered[u], i * (16 * G) + (2 * 8 * G * EG + 16 * G))
                    ts(CS, GS[:, u, :, D], 1.0, None, ALU.max).then_inc(s1["c"].sem, 1)
                    wait(dve, s1["c"], s1["c"].done(q))
                    hold(dve)
                    dve.reciprocal(RC[:, span(q)], CS).then_inc(s1["rc"].sem, 1)
                    p1_this(2, q, i, u)
                    wait(dve, s1["nd"], s1["nd"].done(q))
                    for k in range(G):
                        last = stt(out=row(YS, q, k), in0=GS[:, u, k, 0:D], scalar=col(ND, q, k), in1=row(YS, q, k),
                                   op0=ALU.mult, op1=ALU.add)
                    last.then_inc(s1["y"].sem, 1)
                    p1_next(2, q, u)
                    wait(dve, ag["m"], ag["m"].prev(q + EG))
                    invert(s1["r"], q, R3, SD3, s1["sqrt"])
                    wait(dve, s1["r"], s1["r"].done(q))
                    for k in range(G):
                        last = ts(row(YS, q, k), row(YS, q, k), R3[:, k:k + 1], None, ALU.mult)
                    last.then_inc(s1["x1"].sem, 1)
                    wait(dve, s1["x1"], s1["x1"].done(q))
                    for k in range(G):
                        last = ts(scratch(M)[:, k, :], row(YS, q, k), col(NS, q, k), None, ALU.mult)
                    last.then_inc(ag["m"].sem, 1)
            boundary(1, D)

            def stats(st_bn, st_ag, q, rows_, n):
                for k in range(G):
                    last = dve.bn_stats(ST[:, n, k, :], rows_(k))
                last.then_inc(st_bn.sem, 1)
                wait(dve, st_bn, st_bn.done(q))
                hold(dve)
                for k in range(G):
                    last = dve.bn_aggr(MV[:, n, k, :], ST[:, n, k, :])
                last.then_inc(st_ag.sem, 1)

            def inverse_roots(c, a, b, *after):
                cols = slice(a * G, b * G)
                mv = MV[:, :, :, :].rearrange("p n k c -> p (n k) c")
                v, y, t = RV[:, cols], RS[:, cols], RT[:, cols]
                bits = y.bitcast(i32)
                n = [0]

                def then(ins):
                    n[0] += 1
                    ins.then_inc(inv.sem, 1)
                    wait(dve, inv, inv.at(c, n[0]))

                for st, value in after:
                    wait(dve, st, value)
                then(ts(v, mv[:, cols, 1], LN_EPS, None, ALU.add))
                then(ts(bits, v.bitcast(i32), 1, None, ALU.logical_shift_right))
                then(ts(bits, bits, -1.0, SEED, ALU.mult, ALU.add))
                for _ in range(NEWTON):
                    then(tt(t, y, y, ALU.mult))
                    then(stt(out=t, in0=t, scalar=-0.5, in1=v, op0=ALU.mult, op1=ALU.mult))
                    then(stt(out=y, in0=t, scalar=1.5, in1=y, op0=ALU.add, op1=ALU.mult))
                then(stt(out=NB[:, cols], in0=mv[:, cols, 0], scalar=-1.0, in1=y, op0=ALU.mult, op1=ALU.mult))

            def norm(out_, rows_, mean, r, st):
                for k in range(G):
                    last = ts(out_[:, k, :], rows_(k), mean[:, k, 0:1], r[:, k:k + 1], ALU.subtract, ALU.mult)
                last.then_inc(st.sem, 1)

            with dve.Fori(0, EG // 2) as i:
                for u in (0, 1):
                    q = i * 2 + u
                    wait(dve, gathered[u], i * (16 * G) + (3 * 8 * G * EG + 16 * G))
                    for k in range(G):
                        last = stt(out=GS[:, u, k, 0:D], in0=GS[:, u, k, 0:D], scalar=col(ND, q, k), in1=blB[:, :],
                                   op0=ALU.mult, op1=ALU.add)
                    last.then_inc(s2["a"].sem, 1)
                    wait(dve, s2["a"], s2["a"].done(q))
                    stt(out=GS[:, u, :, 0:D], in0=GS[:, u, :, 0:D], scalar=0.0, in1=YS[:, span(q), :],
                        op0=ALU.max, op1=ALU.add).then_inc(s2["a2"].sem, 1)
                    wait(dve, s2["a2"], s2["a2"].done(q))
                    hold(dve)
                    stats(s2["bn"], s2["ag"], q, lambda k: GS[:, u, k, 0:D], 0)
                    p1_this(3, q, i, u)
                    invert(s2["r"], q, R3, SD3, s2["sqrt"])
                    wait(dve, s2["keep"], s2["keep"].prev(q))
                    wait(dve, s2["xT"], s2["xT"].prev(q))
                    wait(dve, s2["r"], s2["r"].done(q))
                    norm(scratch(M), lambda k: GS[:, u, k, 0:D], MVS, R3, s2["x2"])
                    wait(dve, s2["stat"], s2["stat"].prev(q))
                    wait(dve, s2["x2"], s2["x2"].done(q))
                    hold(dve)
                    dve.tensor_copy(EM, REAL[:, span(q)]).then_inc(s2["em"].sem, 1)
                    dve.sem_inc(s2["s"].sem, 1)
                    p1_next(3, q, u)

            def batch_norm(n, sums, count, b, gamma, beta, to):
                link(ts(rt[:, 0:2, :], sums, 1.0 / count, None, ALU.mult))
                link(tt(rt[:, 2, :], rt[:, 0, :], rt[:, 0, :], ALU.mult))
                link(tt(rt[:, 2, :], rt[:, 1, :], rt[:, 2, :], ALU.subtract))
                link(ts(rt[:, 2, :], rt[:, 2, :], 0.0, BN_EPS, ALU.max, ALU.add))
                dve.sem_inc(bn_v[0].sem, 1)
                bn_a[n - 1].passed(dve)
                link(dve.reciprocal(rt[:, 4, :], rt[:, 3, :]))
                link(tt(bnrow[:, 0, :], rt[:, 4, :], gamma, ALU.mult))
                link(tt(rt[:, 0, :], rt[:, 0, :], b, ALU.add))
                link(tt(rt[:, 0, :], b, rt[:, 0, :], ALU.subtract))
                link(tt(rt[:, 0, :], rt[:, 0, :], bnrow[:, 0, :], ALU.mult))
                link(tt(bnrow[:, 1, :], rt[:, 0, :], beta, ALU.add))
                dve.sem_inc(bn_t[0].sem, 1)
                bn_b[n - 1].passed(dve)
                link(dve.tensor_copy(to.rearrange("p a f -> p (a f)"), pX[:, 0:2 * D]))

            wait(dve, s2["stat"], s2["stat"].prev(EG))
            wait(dve, p1["s"], p1["s"].prev(NG + 1))
            batch_norm(1, acc[0:1, 1, 0:2 * D].rearrange("a (r f) -> a r f", r=2), EDGES, rows[:, 0, :], rows[:, 1, :], rows[:, 2, :], bn1B[:, :, :])
            dve.sem_inc(bn_done[0].sem, 1)
            with dve.Fori(0, EG // 2) as i:
                for u in (0, 1):
                    q = i * 2 + u
                    wait(dve, h1["s1"], h1["s1"].prev(q))
                    tt(scratch(9), Z[:, span(q), :], over(bn1B[:, 0, :]), ALU.mult).then_inc(h1["v1"].sem, 1)
                    wait(dve, h1["v1"], h1["v1"].done(q))
                    tt(scratch(9), scratch(9), over(bn1B[:, 1, :]), ALU.add).then_inc(h1["v"].sem, 1)
                    wait(dve, h1["exp"], h1["exp"].done(q))
                    ts(scratch(10), scratch(10), 1.0, -1.0, ALU.min, ALU.add).then_inc(h1["t"].sem, 1)
                    wait(dve, ag["mmT"], ag["mmT"].prev(q + 2 * EG))
                    wait(dve, h1["t"], h1["t"].done(q))
                    stt(out=scratch(M), in0=scratch(9), scalar=0.0, in1=scratch(10), op0=ALU.max, op1=ALU.add).then_inc(h1["s1"].sem, 1)
                    wait(dve, h1["s1"], h1["s1"].done(q))
                    dve.sem_inc(ag["m"].sem, 1)
                    wait(dve, d1_p, q * 32 + 32)
                    ts(CS, XM[:, :, D], 1.0, None, ALU.max).then_inc(d1["c"].sem, 1)
                    wait(dve, d1["c"], d1["c"].done(q))
                    hold(dve)
                    dve.reciprocal(RCD[:, span(q)], CS).then_inc(d1["rc"].sem, 1)
                    wait(dve, d1["nd"], d1["nd"].done(q))
                    wait(dve, d1["x2"], d1["x2"].prev(q))
                    wait(dve, d1["mm"], d1["mm"].done(q))
                    for k in range(G):
                        last = stt(out=scratch(4)[:, k, :], in0=XM[:, k, 0:D], scalar=NDD[:, k:k + 1], in1=pXt[:, k, :], op0=ALU.mult, op1=ALU.add)
                    last.then_inc(d1["y"].sem, 1)
                    for k in range(G):
                        last = stt(out=scratch(1)[:, k, :], in0=scratch(1)[:, k, :], scalar=NDD[:, k:k + 1], in1=blB[:, :], op0=ALU.mult, op1=ALU.add)
                    last.then_inc(d1["a"].sem, 1)
                    invert(d1["r"], q, R3, SD3, d1["sqrt"])
                    wait(dve, d1["r"], d1["r"].done(q))
                    for k in range(G):
                        last = ts(scratch(4)[:, k, :], scratch(4)[:, k, :], R3[:, k:k + 1], None, ALU.mult)
                    last.then_inc(d1["x1"].sem, 1)
                    wait(dve, d1["x1"], d1["x1"].done(q))
                    stt(out=scratch(4), in0=scratch(1), scalar=0.0, in1=scratch(4), op0=ALU.max, op1=ALU.add).then_inc(d1["s"].sem, 1)
                    wait(dve, d1["s"], d1["s"].done(q))
                    stats(d1["bn"], d1["ag"], q, lambda k: scratch(4)[:, k, :], 0)
                    invert(d1["r2"], q, R2, SD2, d1["sqrt2"])
                    wait(dve, d1_st, q * 16)
                    wait(dve, d1["r2"], d1["r2"].done(q))
                    norm(scratch(3), lambda k: scratch(4)[:, k, :], MVS, R2, d1["x2"])
            boundary(2, D)
            with dve.Fori(0, EG // 2) as i:
                for u in (0, 1):
                    q = i * 2 + u
                    zslot = scratch(5 if u == 0 else 10)
                    wait(dve, d2_p[u], i * 16 + 16)
                    wait(dve, d2_st[u], i * 16)
                    wait(dve, d2["mm"], d2["mm"].done(q))
                    for k in range(G):
                        last = stt(out=zslot[:, k, :], in0=scratch(3 + u)[:, k, :], scalar=col(RCD, q, k), in1=pXt[:, k, :], op0=ALU.mult, op1=ALU.add)
                    last.then_inc(d2["z"].sem, 1)
                    wait(dve, d2["stat"], d2["stat"].prev(q))
                    hold(dve)
                    dve.tensor_copy(EM, REP[:, span(q)]).then_inc(d2["em"].sem, 1)
                    wait(dve, gathered[u], i * (16 * G) + (5 * 8 * G * EG + 16 * G))
                    wait(dve, s4["mm"], s4["mm"].done(q))
                    for k in range(G):
                        last = stt(out=row(Z, q, k), in0=GS[:, u, k, 0:D], scalar=col(RC, q, k), in1=pZt[:, k, :], op0=ALU.mult, op1=ALU.add)
                    last.then_inc(s4["z"].sem, 1)
            wait(dve, p1["gram"], p1["gram"].prev(NG))
            wait(dve, s4["T"], s4["T"].prev(EG))
            link(dve.tensor_copy(GM, acc[:, 0, 0:D + 1]))
            dve.sem_inc(gr.sem, 1)
            gr_mm.passed(dve)
            link(tt(GP, pX[:, 0:D], w2a[:, :], ALU.mult))
            dve.sem_inc(gr_p.sem, 1)
            gr_q.passed(dve)
            wait(dve, d2["stat"], d2["stat"].prev(EG))
            link(dve.tensor_copy(rt[:, 0:2, :], acc[0:1, 1, 0:2 * D].rearrange("a (r f) -> a r f", r=2)))
            link(tt(rt[:, 0, :], rt[:, 0, :], pX[0:1, 512:512 + D], ALU.add))
            link(tt(rt[:, 1, :], rt[:, 1, :], pY[0:1, 0:D], ALU.add))
            batch_norm(2, rt[:, 0:2, :], NODES, rows[:, 3, :], rows[:, 4, :], rows[:, 5, :], bn2B[:, :, :])
            link(tt(w2s[:, :], w2a[:, :], bn2B[:, 0, :], ALU.mult))
            split(bnrow[:, 1, :])
            dve.sem_inc(bn_done[0].sem, 1)

            def p2_first(q, u):
                wait(dve, p2["exp"], p2["exp"].done(q))
                stt(out=scratch(3), in0=scratch(3), scalar=1.0, in1=scratch(u), op0=ALU.min, op1=ALU.add).then_inc(p2["t"].sem, 1)
                wait(dve, p2["t"], p2["t"].done(q))
                stt(out=scratch(4 + u), in0=pWt, scalar=0.0, in1=scratch(3), op0=ALU.max, op1=ALU.add).then_inc(p2["s"].sem, 1)
                wait(dve, p2["s"], p2["s"].done(q))
                stats(p2["bn"], p2["ag"], q, lambda k: scratch(4 + u)[:, k, :], 1)

            def p2_last(q, u):
                wait(dve, p2["o"], p2["o"].prev2(q))
                for k in range(G):
                    last = stt(out=scratch(10 + u)[:, k, :], in0=scratch(4 + u)[:, k, :], scalar=RS[:, G + k:G + k + 1], in1=b3B[:, :],
                               op0=ALU.mult, op1=ALU.add)
                last.then_inc(p2["u"].sem, 1)
                wait(dve, p2["u"], p2["u"].done(q))
                stats(p2["bn2"], p2["ag2"], q, lambda k: scratch(10 + u)[:, k, :], 2)

            def p2_roots(q, a, b, *after):
                inverse_roots(q + 1, a, b, (p2["ag2"], p2["ag2"].done(q)), (p2["ag"], p2["ag"].done(q + 1)),
                              (p2["o"], p2["o"].prev(q)), (p2["u"], p2["u"].done(q)), *after)

            p2_first(0, 0)
            inverse_roots(0, 1, 2, (p2["ag"], p2["ag"].done(0)))
            with dve.Fori(0, EG // 2) as i:
                for u in (0, 1):
                    q = i * 2 + u
                    p2_last(q, u)
                    p2_first(q + 1, 1 - u)
                    wait(dve, s5["exp"], s5["exp"].done(q))
                    stt(out=XM[:, :, 0:D], in0=XM[:, :, 0:D], scalar=1.0, in1=YS[:, span(q), :], op0=ALU.min, op1=ALU.add).then_inc(s5["t"].sem, 1)
                    wait(dve, s5["t"], s5["t"].done(q))
                    stt(out=XM[:, :, 0:D], in0=scratch(9), scalar=0.0, in1=XM[:, :, 0:D], op0=ALU.max, op1=ALU.add).then_inc(s5["s1"].sem, 1)
                    wait(dve, s5["s1"], s5["s1"].done(q))
                    stats(s5["bn"], s5["ag"], q, lambda k: XM[:, k, 0:D], 0)
                    p2_roots(q, 0, 3, (s5["ag"], s5["ag"].done(q)))
                    tt(RW, RS[:, 0:G], WE[:, span(q)], ALU.mult).then_inc(s5["rw"].sem, 1)
                    wait(dve, ag["mmT"], ag["mmT"].prev(q + 3 * EG))
                    wait(dve, s5["rw"], s5["rw"].done(q))
                    norm(scratch(M), lambda k: XM[:, k, 0:D], MVS, RW, ag["m"])
                    wait(dve, ag["m"], ag["m"].done(q + 3 * EG))
                    dve.sem_inc(s5["s"].sem, 1)
            boundary(3, D)
            with dve.Fori(0, EG // 2) as i:
                for u in (0, 1):
                    q = i * 2 + u
                    r = q * 3 + EG
                    p2_last(r, u)
                    p2_first(r + 1, 1 - u)
                    wait(dve, d3["exp"], d3["exp"].done(q))
                    stt(out=scratch(9), in0=scratch(9), scalar=1.0, in1=scratch(6), op0=ALU.min, op1=ALU.add).then_inc(d3["t"].sem, 1)
                    wait(dve, d3["t"], d3["t"].done(q))
                    stt(out=scratch(9), in0=scratch(7), scalar=0.0, in1=scratch(9), op0=ALU.max, op1=ALU.add).then_inc(d3["s"].sem, 1)
                    wait(dve, d3["s"], d3["s"].done(q))
                    stats(d3["bn"], d3["ag"], q, lambda k: scratch(9)[:, k, :], 0)
                    p2_roots(r, 0, 3, (d3["ag"], d3["ag"].done(q)))
                    wait(dve, d3["o"], d3["o"].prev(q))
                    for k in range(G):
                        last = stt(out=XM[:, k, 0:D], in0=scratch(9)[:, k, :], scalar=RS[:, k:k + 1], in1=b3B[:, :], op0=ALU.mult, op1=ALU.add)
                    last.then_inc(d3["u"].sem, 1)
                    p2_last(r + 1, 1 - u)
                    p2_first(r + 2, u)
                    wait(dve, d3["u2"], d3["u2"].done(q))
                    stats(d3["bn2"], d3["ag2"], q, lambda k: XM[:, k, 0:D], 3)
                    p2_roots(r + 1, 1, 4, (d3["ag2"], d3["ag2"].done(q)))
                    p2_last(r + 2, u)
                    p2_first(r + 3, 1 - u)
                    p2_roots(r + 2, 1, 3)



def kernel(x, src, dst, edge_attr_128, edge_weight, L0_gnn_W_conv, L0_gnn_b_conv, L0_gnn_W_aggr, L0_gnn_b_aggr,
           L1_gnn_weight, L1_gnn_bias, L2_gnn_u, L2_gnn_W1, L2_gnn_b1, L2_gnn_g1, L2_gnn_be1, L2_gnn_W2, L2_gnn_b2,
           L2_gnn_g2, L2_gnn_be2, L3_gnn_W, L3_gnn_b):
    from concourse import bacc
    from concourse.bass_utils import run_bass_kernel_spmd

    x = np.asarray(x)
    src, dst, ea, w = (np.asarray(a) for a in (src, dst, edge_attr_128, edge_weight))
    xp = np.zeros((NPAD, D), x.dtype)
    xp[:NODES] = x
    xT = np.zeros((NG + 2, D, G * P), x.dtype)
    xT[:NG] = xp.reshape(P, NG, G, D).transpose(1, 3, 2, 0).reshape(NG, D, G * P)
    dst1 = np.full((EPAD + 1,), NPAD - 1, dst.dtype)
    dst1[0] = -1
    dst1[1:EDGES + 1] = dst
    srcp = np.full((EPAD,), NPAD - 1, src.dtype)
    srcp[:EDGES] = src
    wp = np.zeros((EPAD,), w.dtype)
    wp[:EDGES] = w
    eap = np.zeros((EPAD, D), ea.dtype)
    eap[:EDGES] = ea
    ins = dict(x=xp, xT=xT, edge_attr=eap, dst1=dst1, src=srcp, weight=wp,
               W_conv_T=np.ascontiguousarray(np.asarray(L0_gnn_W_conv).T), b_conv=L0_gnn_b_conv, W_aggr=L0_gnn_W_aggr,
               b_aggr=L0_gnn_b_aggr, W_l1=L1_gnn_weight, b_l1=L1_gnn_bias, W1=L2_gnn_W1, b1=L2_gnn_b1, g1=L2_gnn_g1,
               be1=L2_gnn_be1, W2=L2_gnn_W2, b2=L2_gnn_b2, g2=L2_gnn_g2, be2=L2_gnn_be2,
               W3_T=np.ascontiguousarray(np.asarray(L3_gnn_W).T), b3=L3_gnn_b)
    ins = {k: np.ascontiguousarray(np.asarray(v)) for k, v in ins.items()}
    nc = bacc.Bacc("TRN2", target_bir_lowering=False, num_devices=1)
    aps = {k: nc.dram_tensor("in_" + k, v.shape, mybir.dt.from_np(v.dtype), kind="ExternalInput").ap() for k, v in ins.items()}
    out = nc.dram_tensor("out", (NPAD, D), mybir.dt.float32, kind="ExternalOutput").ap()
    build(nc, out=out, **aps)
    r = run_bass_kernel_spmd(nc, [{"in_" + k: v for k, v in ins.items()}], core_ids=[0])
    return r.results[0]["out"][:NODES]
```

```python
import numpy as np
import concourse.bass as bass
from concourse import mybir
from contextlib import ExitStack

P = 128
D = 128
G = 7
NODES, EDGES = 50000, 12500
NT = 392
NG = NT // G
NPAD = P * NT
ET = 98
EG = ET // G
EPAD = ET * P
LASTROWS = EDGES - (ET - 1) * P
CW = 132
ZERO_ROW = EPAD - 1
NOWHERE = 100000.0
LN_EPS, BN_EPS = 1e-5, 1e-4
SEED = float(0x5F3759DF)
NEWTON = 3
ROUND = float(3 << 22)


class Step:

    def __init__(self, sem, lead=0, base=0):
        self.sem, self.lead, self.base = sem, lead, base

    def done(self, q):
        return q + (1 + self.lead + self.base)

    def prev(self, q):
        return q + (self.lead + self.base)

    def prev2(self, q):
        return q + (self.lead + self.base - 1)


class Mark:

    def __init__(self, sem, at):
        self.sem, self.at = sem, at

    def passed(self, eng):
        eng.wait_ge(self.sem, self.at)


class Chain:

    def __init__(self, sem, per, base=0):
        self.sem, self.per, self.base = sem, per, base

    def at(self, q, j):
        return q * self.per + (self.base * self.per + j)

    def done(self, q):
        return self.at(q, self.per)

    def prev(self, q):
        return self.at(q, 0)


def build(nc, x, xT, edge_attr, dst1, src, weight, W_conv_T, b_conv, W_aggr, b_aggr, W_l1, b_l1,
          W1, b1, g1, be1, W2, b2, g2, be2, W3_T, b3, out):
    f32, i32, f16, bf16 = mybir.dt.float32, mybir.dt.int32, mybir.dt.float16, mybir.dt.bfloat16
    ALU = mybir.AluOpType
    ACT = mybir.ActivationFunctionType
    AX = mybir.AxisListType

    ctx = ExitStack()
    with ctx:
        def sb(name, shape, dt=f32):
            return ctx.enter_context(nc.sbuf_tensor(name, shape, dt))

        def sem(name):
            return ctx.enter_context(nc.semaphore(name))

        def step(name, lead=0):
            return Step(sem(name), lead)

        def dram(name, shape, dt=f32):
            return nc.dram_tensor(name, shape, dt, kind="Internal").ap()

        def scratch(i):
            return WK[:, i, :].rearrange("p (k f) -> p k f", k=G)

        x2_dram = dram("x2_dram", (NG + 4, P, G * D))
        parts_dram = dram("parts_dram", (2, 3, D), bf16)
        lookup_dram = dram("lookup_dram", (NPAD, 2))
        table = [dram("sums0", (EPAD, CW))] + [dram(f"sums{n}", (EPAD, D)) for n in (1, 2, 3)]
        xd_dram = dram("xd_dram", (EG, P, G * D))
        zd_dram = dram("zd_dram", (EG, P, G * D))

        YS = sb("YS", [P, ET, D])
        Z = sb("Z", [P, ET, D])
        EQ = sb("EQ", [P, ET, P], bf16)
        WK = sb("WK", [P, 12, G * D])
        XM = sb("XM", [P, G, CW])
        PT = sb("PT", [P, 2, G, CW])
        GS = sb("GS", [P, 2, G, CW])
        ident = sb("ident", [P, P])
        ones = sb("ones", [P, P])
        wM = sb("wM", [P, D]); wA = sb("wA", [P, D]); wL = sb("wL", [P, D])
        w1a = sb("w1a", [P, D]); w1b = sb("w1b", [P, D])
        w2a = sb("w2a", [P, D]); w2b = sb("w2b", [P, D]); w2s = sb("w2s", [P, D])
        w3 = sb("w3", [P, D])
        blB = sb("blB", [P, D]); cB = sb("cB", [P, D]); b3B = sb("b3B", [P, D])
        bn1B = sb("bn1B", [P, 2, D]); bn2B = sb("bn2B", [P, 2, D])
        bias3 = sb("bias3", [3, D], bf16)
        ones3 = sb("ones3", [3, P], bf16)
        rows = sb("rows", [1, 7, D])
        bnrow = sb("bnrow", [1, 2, D])
        b0row = bnrow[:, 1, :]
        bconv = sb("bconv", [P, 1])
        eps_ln = sb("eps_ln", [P, 1])
        KD = sb("KD", [P, ET]); WE = sb("WE", [P, ET])
        NS = sb("NS", [P, ET]); ND = sb("ND", [P, ET]); RC = sb("RC", [P, ET]); RCD = sb("RCD", [P, ET])
        REP = sb("REP", [P, ET]); REAL = sb("REAL", [P, ET])
        SRCI = sb("SRCI", [P, ET], i32); DSTI = sb("DSTI", [P, ET], i32)
        POSI = sb("POSI", [P, ET], i32); OUTI = sb("OUTI", [P, ET], i32)
        IX = sb("IX", [P, 2, G], i32)
        MASK = sb("MASK", [P, NT])
        Cmat = sb("Cmat", [P, ET])
        REPI = sb("REPI", [P, 1], i32)
        FR = sb("FR", [P, CW]); LR = sb("LR", [P, CW])
        ZH = sb("ZH", [P, 512], f16)
        sc = sb("sc", [P, 8])
        small = sb("small", [P, 14, G])
        SS1, SD1, R1, SS2, SD2, R2, RM, SS3, SD3, R3, NDD, EM, CS, RW = (small[:, n, :] for n in range(14))
        RV, RS, RT, NB = (sb(name, [P, 4 * G]) for name in ("RV", "RS", "RT", "NB"))
        ST = sb("ST", [P, 4, G, 6])
        MV = sb("MV", [P, 4, G, 2])
        MVS = MV[:, 0, :, :]
        acc = ctx.enter_context(nc.psum_tensor("acc", [P, 2, 512], f32))
        pX = ctx.enter_context(nc.psum_tensor("pX", [P, 1024], f32))
        pY = ctx.enter_context(nc.psum_tensor("pY", [P, 1024], f32))
        pZ = ctx.enter_context(nc.psum_tensor("pZ", [P, 1024], f32))
        pW = acc[:, :, :].rearrange("p a c -> p (a c)")

        EQF, M, WAT, AT2 = 6, 7, 8, 9

        def tiles(t):
            return t[:, 0:G * D].rearrange("p (k f) -> p k f", k=G)

        pXt, pYt, pZt, pWt = tiles(pX), tiles(pY), tiles(pZ), tiles(pW)

        kt = WK[0:ET, 0, 0:4 * P].rearrange("t (a e) -> t a e", a=4)
        kti = WK[0:ET, 1, 0:4 * P].bitcast(i32).rearrange("t (a e) -> t a e", a=4)
        wk_a, wk_b = WK[:, 2, :], WK[:, 3, :]
        PD, TD, PS_, TS_ = (WK[:, 4, n * ET:(n + 1) * ET] for n in range(4))
        KP, KS = WK[:, 3, 256:256 + ET], WK[:, 3, 384:384 + ET]
        RR = RCD[:, :]
        LK = WK[:, 6, 0:2 * ET].rearrange("p (t c) -> p t c", c=2)
        ones_t = WK[:, 6, 2 * ET:2 * ET + NT]
        rt = WK[0:1, 6, 0:6 * D].rearrange("a (r f) -> a r f", r=6)
        rest = WK[0:1, 6, 5 * D:6 * D]
        parts = WK[0:1, 2, 512:512 + 3 * D // 2].bitcast(bf16).rearrange("a (r f) -> a r f", r=3)
        GM, GP = WK[:, 7, 0:D + 1], WK[:, 7, 256:256 + D]
        iota_i = WK[:, 5, 0:NT].bitcast(i32)
        iota_h = WK[:, 5, NT:NT + NT // 2].bitcast(f16)
        OHP = WK[:, 10, :].bitcast(f16)[:, 0:4 * P].rearrange("p (a b c) -> p a b c", a=2, b=2)
        OHT = WK[:, 11, :].bitcast(f16)[:, 0:4 * NT].rearrange("p (a b c) -> p a b c", a=2, b=2)
        deg = WK[:, 7, 0:NT]; degout = WK[:, 8, 0:NT]
        cum = WK[:, 7, NT:2 * NT]; posn = WK[:, 8, NT:2 * NT]
        tabs = WK[:, 9, 0:2 * NT].rearrange("p (t c) -> p t c", c=2)
        tri = WK[:, 6, 0:P]

        carried = sem("waits_carried")
        consts = sem("constants_made")
        s_keys, s_wts = sem("keys_loaded"), sem("weights_loaded")
        vlink, glink = sem("vector_link"), sem("gpsimd_link")

        def marks(name, n):
            s_ = sem(name)
            return [Mark(s_, m + 1) for m in range(n)]

        (zeros, keys_f, idx_ready, comp_ready, lk_diag, cmask0, hist_out, rowtot, tab_ready, ns_in, ns_ready,
         bn_v1, bn_t1, bn_done1, gr, gr_p, bn_v2, bn_t2, bn_done2) = marks("vector_events", 19)
        (comp_mm, keys_T, lk_mm, rowoff, bn_b1, gr_mm, gr_q, bn_b2) = marks("tensor_events", 8)
        (ns_sq, bn_a1, bn_a2) = marks("scalar_events", 3)
        (cmask, mask1) = marks("gpsimd_events", 2)
        oh, ohmm = step("onehots_built"), step("onehots_counted", 1)
        zgroup = sem("zero_group_stored")
        tab_stored = sem("lookup_stored")
        rk_l, eq_built = [sem("rowkeys0"), sem("rowkeys1")], step("eq_built", 1)
        p1 = {k: step("p1_" + k, 1 if k in ("mm", "xm") else 0) for k in
              ("mm", "sq", "sqrt", "r", "s", "sq2", "sqrt2", "r2", "rm", "x2", "xm", "gram")}
        p1_x, p1_st = [sem("nodes_x0"), sem("nodes_x1")], [sem("p1_stored0"), sem("p1_stored1")]
        ag = {k: step("agg_" + k) for k in ("eqf", "m", "mmT", "aT", "mmP", "p", "cnt")}
        ag_st = [sem("agg_stored0"), sem("agg_stored1")]
        bd_l, bd_mm, bd_r, bd_sc = sem("boundary_rows_loaded"), sem("boundary_product"), sem("boundary_rows_ready"), sem("boundary_scattered")
        edge_sems, counted = {}, {}

        def edge_steps(*names):
            out_ = {}
            for k in names:
                if k not in edge_sems:
                    edge_sems[k], counted[k] = sem("edges_" + k), 0
                out_[k] = Step(edge_sems[k], 1 if k in ("raw", "y", "s", "eaT", "T", "z") else 0, counted[k])
                counted[k] += EG
            return out_

        xs = edge_steps("ix", "T", "aT", "mm", "raw", "ys")
        lk = edge_steps("ix")
        s1 = edge_steps("ix", "c", "rc", "nd", "y", "sq", "sqrt", "r", "rw", "x1")
        s2 = edge_steps("ix", "a", "a2", "s", "bn", "ag", "sqrt", "r", "x2", "keep", "eaT", "eaTc", "xT", "xTc", "z1", "zc", "sq", "stat", "em")
        d1 = edge_steps("ix", "T", "aT", "mm", "c", "rc", "nd", "y", "sq", "sqrt", "r", "x1", "a", "s", "bn", "ag", "sqrt2", "r2", "x2")
        s4 = edge_steps("ix", "cp", "T", "aT", "mm", "z")
        h1 = edge_steps("v1", "v", "exp", "t", "s1")
        s5 = edge_steps("v1", "v", "exp", "t", "s1", "s", "bn", "ag", "rw")
        d3 = edge_steps("v1", "v", "exp", "t", "s", "bn", "ag", "u", "u2", "bn2", "ag2", "o")
        lk_use = step("lookup_used", 1)
        gathered = [sem("gathered0"), sem("gathered1")]
        s2_ea = [sem("edge_features0"), sem("edge_features1")]
        bn_v, bn_t, bn_done, bn_b, bn_a = (bn_v1, bn_v2), (bn_t1, bn_t2), (bn_done1, bn_done2), (bn_b1, bn_b2), (bn_a1, bn_a2)
        d1_p, d1_st = sem("d1_sums"), sem("d1_stored")
        d2 = {k: step("d2_" + k, 1 if k in ("z", "T") else 0) for k in ("T", "aT", "mm", "z", "sq", "stat", "em")}
        d2_x, d2_p, d2_st = [sem("d2_x0"), sem("d2_x1")], [sem("d2_p0"), sem("d2_p1")], [sem("d2_stored0"), sem("d2_stored1")]
        p2 = {k: step("p2_" + k, 1 if k in ("t", "o") else 0) for k in ("T", "xT", "neg", "exp", "t", "bn", "ag", "u", "sq", "o")}
        for k in ("mm", "s"):
            p2[k] = Step(p1[k].sem, p1[k].lead, NG + 1)
        CHAIN = 7 + 3 * NEWTON
        inv = Chain(sem("inverse_roots"), CHAIN)
        p2_x, p2_st = [sem("p2_x0"), sem("p2_x1")], [sem("p2_stored0"), sem("p2_stored1")]
        d3_l = sem("d3_loaded")
        fin = sem("outputs_scattered")
        bias_st, bias_l = sem("bias_parts_stored"), sem("bias_parts_loaded")

        block = ctx.enter_context(nc.Block())

        def wait(eng, st, value):
            eng.wait_ge(st.sem if isinstance(st, (Step, Chain)) else st, value)

        def hold(eng):
            eng.sem_inc(carried, 1)

        def over(t):
            return t.unsqueeze(1).broadcast_to([P, G, D])

        def span(q):
            return bass.ds(q * G, G)

        def each_group(eng, body):
            with eng.Fori(0, EG // 2 - 1) as i:
                for u in (0, 1):
                    body(i * 2 + u, i, u, True)
            for u in (0, 1):
                body(EG - 2 + u, EG // 2 - 1, u, u == 0)

        @block.sync
        def _(sp):
            sp.dma_start(kti[:, 0, :], dst1[1:1 + EPAD].rearrange("(t p) -> t p", p=P)).then_inc(s_keys, 16)
            sp.dma_start(kti[:, 1, :], dst1[0:EPAD].rearrange("(t p) -> t p", p=P)).then_inc(s_keys, 16)
            sp.dma_start(kti[:, 2, :], src.rearrange("(t p) -> t p", p=P)).then_inc(s_keys, 16)
            sp.dma_start(kt[:, 3, :], weight.rearrange("(t p) -> t p", p=P)).then_inc(s_keys, 16)
            for to, of in ((wk_a[:, 0:D], W_conv_T), (wk_a[:, D:2 * D], W_aggr[0:D, :]), (wM, W_aggr[D:2 * D, :]),
                           (wL, W_l1), (w1a, W1[0:D, :]), (w1b, W1[D:2 * D, :]), (w2a, W2[0:D, :]),
                           (w2b, W2[D:2 * D, :]), (w3, W3_T)):
                sp.dma_start(to[:, :] if to.shape[1] == D else to, of).then_inc(s_wts, 16)
            sp.dma_start(blB[:, :], b_l1.rearrange("(a n) -> a n", a=1).broadcast_to([P, D])).then_inc(s_wts, 16)
            sp.dma_start(b3B[:, :], b3.rearrange("(a n) -> a n", a=1).broadcast_to([P, D])).then_inc(s_wts, 16)
            for n, r in enumerate((b1, g1, be1, b2, g2, be2, b_aggr)):
                sp.dma_start(rows[:, n, :], r.rearrange("(a n) -> a n", a=1)).then_inc(s_wts, 16)
            sp.dma_start(bconv[:, :], b_conv.rearrange("(n a) -> n a", a=1)).then_inc(s_wts, 16)

            def p1_load(q, u):
                wait(sp, p1["mm"], p1["mm"].prev2(q))
                sp.dma_start(WK[:, u, :], xT[bass.ds(q, 1), :, :].rearrange("a p c -> p (a c)")).then_inc(p1_x[u], 16)

            def p1_store(q, u):
                wait(sp, p1["x2"], p1["x2"].done(q))
                sp.dma_start(x2_dram[bass.ds(q, 1), :, :].rearrange("a p c -> p (a c)"), WK[:, 4 + u, :]).then_inc(p1_st[u], 16)

            def table_view(n, q, width):
                return table[n].rearrange("(t p) w -> p t w", p=P)[:, span(q), 0:width]

            def agg_store(n, q, i, u, width):
                a = n * EG + q
                wait(sp, ag["p"], ag["p"].done(a))
                sp.dma_start(table_view(n, q, width), PT[:, u, :, 0:width]).then_inc(ag_st[u], 16)

            def boundary(n, width):
                half = (n + 1) * EG // 2 * 16
                sp.wait_ge(ag_st[0], half)
                sp.wait_ge(ag_st[1], half)
                if n:
                    sp.wait_ge(bd_sc, 16 * n)
                t = table[n].rearrange("(t p) w -> t p w", p=P)
                sp.dma_start(FR[0:ET, 0:width], t[:, 0, :]).then_inc(bd_l, 16)
                sp.dma_start(LR[0:ET, 0:width], t[:, P - 1, :]).then_inc(bd_l, 16)

            def load_bias(n):
                sp.dma_start(parts_dram[n:n + 1, :, :], parts).then_inc(bias_st, 16)
                sp.wait_ge(bias_st, 16 * (n + 1))
                sp.dma_start(bias3[0:3, :], parts_dram[n, :, :]).then_inc(bias_l, 16)

            comp_ready.passed(sp)
            load_bias(0)
            zeros.passed(sp)
            for n in range(4):
                sp.dma_start(x2_dram[NG + n, :, :].rearrange("p (k f) -> p k f", k=G), XM[:, :, 0:D]).then_inc(zgroup, 16)
            sp.wait_ge(zgroup, 64)
            tab_ready.passed(sp)
            sp.dma_start(lookup_dram.rearrange("(p t) c -> p t c", p=P), tabs).then_inc(tab_stored, 16)
            sp.wait_ge(tab_stored, 16)
            def keys_load(q, u):
                wait(sp, eq_built, eq_built.prev2(q))
                sp.dma_start(WK[:, 10 + u, :].bitcast(i32),
                             dst1[bass.ds(q * (G * P) + 1, G * P)].rearrange("(a n) -> a n", a=1).broadcast_to([P, G * P]))\
                    .then_inc(rk_l[u], 16)

            def loop_b(q, i, u, more):
                if more:
                    keys_load(q + 1, 1 - u)
                p1_load(q + 2, u)
                p1_store(q, u)

            keys_load(0, 0)
            for u in (0, 1):
                sp.dma_start(WK[:, u, :], xT[u, :, :]).then_inc(p1_x[u], 16)
            each_group(sp, loop_b)
            with sp.Fori(0, EG // 2) as i:
                for u in (0, 1):
                    q = i * 2 + u
                    p1_load(q + (EG + 2), u)
                    p1_store(q + EG, u)
                    agg_store(0, q, i, u, CW)
            boundary(0, CW)
            with sp.Fori(0, EG // 2) as i:
                for u in (0, 1):
                    q = i * 2 + u
                    p1_load(q + (2 * EG + 2), u)
                    p1_store(q + 2 * EG, u)
                    agg_store(1, q, i, u, D)
            boundary(1, D)
            with sp.Fori(0, EG // 2) as i:
                for u in (0, 1):
                    q = i * 2 + u
                    wait(sp, s2["eaT"], s2["eaT"].prev2(q))
                    sp.dma_start(scratch(10 + u), edge_attr.rearrange("(t p) f -> p t f", p=P)[:, span(q), :]).then_inc(s2_ea[u], 16)
                    p1_load(q + (3 * EG + 2), u)
                    p1_store(q + 3 * EG, u)
            sp.wait_ge(bd_sc, 32)
            wait(sp, p1["gram"], p1["gram"].prev(NG))
            for u in (0, 1):
                sp.wait_ge(p1_x[u], 16 * (NG // 2 + 1))
            def d1_load(q):
                wait(sp, d1["s"], d1["s"].prev(q))
                sp.dma_start(XM[:, :, :], table_view(0, q, CW)).then_inc(d1_p, 16)
                sp.dma_start(scratch(1), table_view(1, q, D)).then_inc(d1_p, 16)

            def loop_f(q, i, u, more):
                agg_store(2, q, i, u, D)
                if more:
                    d1_load(q + 1)
                wait(sp, d1["x2"], d1["x2"].done(q))
                sp.dma_start(xd_dram[bass.ds(q, 1), :, :].rearrange("a p c -> p (a c)"), WK[:, 3, :]).then_inc(d1_st, 16)

            d1_load(0)
            each_group(sp, loop_f)
            boundary(2, D)
            sp.wait_ge(d1_st, 16 * EG)
            sp.wait_ge(bd_sc, 48)
            def d2_load(q, u):
                wait(sp, d2["T"], d2["T"].prev2(q))
                sp.dma_start(WK[:, u, :], xd_dram[bass.ds(q, 1), :, :].rearrange("a p c -> p (a c)")).then_inc(d2_x[u], 16)
                wait(sp, d2["z"], d2["z"].prev2(q))
                sp.dma_start(scratch(3 + u), table_view(2, q, D)).then_inc(d2_p[u], 16)

            def loop_g(q, i, u, more):
                if more:
                    d2_load(q + 1, 1 - u)
                wait(sp, d2["z"], d2["z"].done(q))
                sp.dma_start(zd_dram[bass.ds(q, 1), :, :].rearrange("a p c -> p (a c)"), WK[:, 5 if u == 0 else 10, :]).then_inc(d2_st[u], 16)

            d2_load(0, 0)
            each_group(sp, loop_g)

            def p2_load(q, u):
                wait(sp, p2["t"], p2["t"].prev2(q))
                sp.dma_start(WK[:, u, :], x2_dram[bass.ds(q, 1), :, :].rearrange("a p c -> p (a c)")).then_inc(p2_x[u], 16)

            def p2_store(q, u):
                wait(sp, p2["o"], p2["o"].done(q))
                sp.dma_start(out.rearrange("(p t) f -> p t f", p=P)[:, span(q), :], GS[:, u, :, 0:D]).then_inc(p2_st[u], 16)

            sp.wait_ge(p1_st[0], 16 * NG // 2)
            sp.wait_ge(p1_st[1], 16 * NG // 2)
            sp.wait_ge(d2_st[0], 16 * EG // 2)
            sp.wait_ge(d2_st[1], 16 * EG // 2)
            wait(sp, d2["stat"], d2["stat"].prev(EG))
            for u in (0, 1):
                sp.dma_start(WK[:, u, :], x2_dram[u, :, :]).then_inc(p2_x[u], 16)
            bn_done2.passed(sp)
            load_bias(1)
            wait(sp, p2["t"], p2["t"].done(0))
            sp.dma_start(WK[:, 0, :], x2_dram[2, :, :]).then_inc(p2_x[0], 16)
            def loop_h(q, i, u, more):
                if more:
                    p2_load(q + 4, u)
                agg_store(3, q, i, u, D)
                if more:
                    p2_store(q + 1, 1 - u)

            p2_load(3, 1)
            p2_store(0, 0)
            each_group(sp, loop_h)
            boundary(3, D)
            sp.wait_ge(bd_sc, 64)
            def d3_load(q):
                wait(sp, d3["u2"], d3["u2"].prev(q))
                sp.dma_start(WK[:, 6, :], xd_dram[bass.ds(q, 1), :, :].rearrange("a p c -> p (a c)")).then_inc(d3_l, 16)
                sp.dma_start(WK[:, 7, :], zd_dram[bass.ds(q, 1), :, :].rearrange("a p c -> p (a c)")).then_inc(d3_l, 16)
                sp.dma_start(scratch(8), table_view(3, q, D)).then_inc(d3_l, 16)

            def loop_i(q, i, u, more):
                for n in range(3):
                    r, v = q * 3 + (EG + n), (u + n) % 2
                    if n == 2 and more:
                        d3_load(q + 1)
                    p2_load(r + 4, v)
                    p2_store(r, v)

            p2_load(EG + 3, 1)
            d3_load(0)
            each_group(sp, loop_i)
            sp.wait_ge(p2_st[0], 16 * NG // 2)
            sp.wait_ge(p2_st[1], 16 * NG // 2)
            sp.wait_ge(p2_x[0], 16 * (NG // 2 + 2))
            sp.wait_ge(p2_x[1], 16 * (NG // 2 + 2))
            sp.wait_ge(fin, 16 * ET)

        @block.gpsimd
        def _(pool):
            pool.memset(ident[:, :], 0.0).then_inc(glink, 1)
            pool.memset(tri, 1.0).then_inc(glink, 1)
            pool.iota(iota_i, [[1, NT]], base=0, channel_multiplier=0).then_inc(consts, 1)
            pool.iota(sc[:, 0:1].bitcast(i32), [[0, 1]], base=P, channel_multiplier=P).then_inc(consts, 1)
            pool.wait_ge(glink, 2)
            pool.affine_select(out=ident[:, :], in_=ident[:, :], compare_op=ALU.not_equal, fill=1.0,
                               base=0, pattern=[[-1, P]], channel_multiplier=1).then_inc(consts, 1)
            pool.affine_select(out=tri, in_=tri, compare_op=ALU.is_gt, fill=0.0,
                               base=0, pattern=[[1, P]], channel_multiplier=-1).then_inc(consts, 1)

            def gather_group(q, u, ix, index, rows_of, width):
                hold(pool)
                pool.tensor_copy(IX[:, u, :], index[:, span(q)]).then_inc(ix.sem, 1)
                wait(pool, ix, ix.done(q))
                hold(pool)
                for k in range(G):
                    pool.indirect_dma_start(GS[:, u, k, 0:width], None, rows_of,
                                            bass.IndirectOffsetOnAxis(ap=IX[:, u, k:k + 1], axis=0)).then_inc(gathered[u], 16)

            idx_ready.passed(pool)
            with pool.Fori(0, EG // 2) as i:
                for u in (0, 1):
                    q = i * 2 + u
                    wait(pool, xs["raw"], xs["raw"].prev2(q))
                    wait(pool, xs["T"], xs["T"].prev2(q))
                    gather_group(q, u, xs["ix"], SRCI, x, D)
            cmask0.passed(pool)
            pool.affine_select(out=Cmat[0:ET, :], in_=Cmat[0:ET, :], compare_op=ALU.is_gt, fill=0.0,
                               base=0, pattern=[[-1, ET]], channel_multiplier=1).then_inc(cmask.sem, 1)
            tab_ready.passed(pool)
            pool.affine_select(out=MASK[:, :], in_=MASK[:, :], compare_op=ALU.is_gt, fill=0.0,
                               base=NODES, pattern=[[-1, NT]], channel_multiplier=-NT).then_inc(mask1.sem, 1)
            pool.wait_ge(tab_stored, 16)
            with pool.Fori(0, EG // 2) as i:
                for u in (0, 1):
                    q = i * 2 + u
                    wait(pool, lk_use, lk_use.prev2(q))
                    gather_group(q, u, lk["ix"], SRCI, lookup_dram, 2)

            def scatter_boundary(n, width):
                pool.wait_ge(bd_r, n + 1)
                pool.indirect_dma_start(table[n], bass.IndirectOffsetOnAxis(ap=REPI[0:ET, 0:1], axis=0), LR[0:ET, 0:width], None,
                                        bounds_check=EPAD - 1, oob_is_err=False).then_inc(bd_sc, 16)
                pool.wait_ge(bd_sc, 16 * (n + 1))

            ns_ready.passed(pool)
            scatter_boundary(0, CW)
            with pool.Fori(0, EG // 2) as i:
                for u in (0, 1):
                    q = i * 2 + u
                    wait(pool, s1["y"], s1["y"].prev2(q))
                    gather_group(q, u, s1["ix"], POSI, table[0], CW)
            scatter_boundary(1, D)
            with pool.Fori(0, EG // 2) as i:
                for u in (0, 1):
                    q = i * 2 + u
                    wait(pool, s2["s"], s2["s"].prev2(q))
                    gather_group(q, u, s2["ix"], POSI, table[1], D)
            wait(pool, s2["s"], s2["s"].prev(EG))
            with pool.Fori(0, EG // 2) as i:
                for u in (0, 1):
                    q = i * 2 + u
                    wait(pool, d1["T"], d1["T"].prev2(q))
                    gather_group(q, u, d1["ix"], DSTI, x, D)
                    bn_done1.passed(pool)
                    wait(pool, h1["s1"], h1["s1"].prev(q))
                    pool.tensor_tensor(scratch(9), Z[:, span(q), :], over(bn1B[:, 0, :]), ALU.mult).then_inc(h1["v1"].sem, 1)
                    wait(pool, h1["v1"], h1["v1"].done(q))
                    pool.tensor_tensor(scratch(9), scratch(9), over(bn1B[:, 1, :]), ALU.add).then_inc(h1["v"].sem, 1)
            scatter_boundary(2, D)
            wait(pool, d1["T"], d1["T"].prev(EG))
            with pool.Fori(0, EG // 2) as i:
                for u in (0, 1):
                    q = i * 2 + u
                    wait(pool, s4["z"], s4["z"].prev2(q))
                    gather_group(q, u, s4["ix"], POSI, table[2], D)

            def p2_add(q, u):
                wait(pool, p2["exp"], p2["exp"].done(q))
                pool.tensor_tensor(scratch(3), scratch(3), scratch(u), ALU.add).then_inc(p2["t"].sem, 1)

            wait(pool, s4["z"], s4["z"].prev(EG))
            pool.sem_inc(p2["t"].sem, 1)
            bn_done2.passed(pool)
            p2_add(0, 0)
            p2_add(1, 1)
            with pool.Fori(0, EG // 2) as i:
                for u in (0, 1):
                    q = i * 2 + u
                    wait(pool, s5["s1"], s5["s1"].prev(q))
                    pool.tensor_tensor(scratch(9), Z[:, span(q), :], over(bn2B[:, 0, :]), ALU.mult).then_inc(s5["v1"].sem, 1)
                    wait(pool, s5["v1"], s5["v1"].done(q))
                    pool.tensor_tensor(scratch(9), scratch(9), over(bn2B[:, 1, :]), ALU.add).then_inc(s5["v"].sem, 1)
                    p2_add(q + 2, u)
            scatter_boundary(3, D)
            with pool.Fori(0, EG // 2) as i:
                for u in (0, 1):
                    q = i * 2 + u
                    r = q * 3 + EG
                    wait(pool, d3_l, q * 48 + 48)
                    pool.tensor_tensor(scratch(7), scratch(7), over(bn2B[:, 0, :]), ALU.mult).then_inc(d3["v1"].sem, 1)
                    wait(pool, d3["v1"], d3["v1"].done(q))
                    pool.tensor_tensor(scratch(7), scratch(7), over(bn2B[:, 1, :]), ALU.add).then_inc(d3["v"].sem, 1)
                    p2_add(r + 2, u)
                    p2_add(r + 3, 1 - u)
                    wait(pool, d3["u"], d3["u"].done(q))
                    pool.tensor_tensor(XM[:, :, 0:D], XM[:, :, 0:D], scratch(8), ALU.add).then_inc(d3["u2"].sem, 1)
                    p2_add(r + 4, u)
            pool.wait_ge(p2_st[0], 16 * NG // 2)
            pool.wait_ge(p2_st[1], 16 * NG // 2)
            wait(pool, d3["o"], d3["o"].prev(EG))
            for t in range(ET):
                pool.indirect_dma_start(out, bass.IndirectOffsetOnAxis(ap=OUTI[:, t:t + 1], axis=0), YS[:, t, :], None,
                                        bounds_check=NODES - 1, oob_is_err=False).then_inc(fin, 16)
            pool.wait_ge(fin, 16 * ET)

        @block.tensor
        def _(pe):
            mm = pe.matmul

            def bias_first(to):
                for a, b in ((0, 4), (4, G)):
                    mm(to[:, a * D:b * D].rearrange("p (k f) -> p k f", f=D), ones3[0:3, :],
                       bias3[0:3, :].unsqueeze(1).broadcast_to([3, b - a, D]), start=True, stop=False, skip_group_check=True)

            for st in (ohmm, p1["mm"], s2["eaT"], xs["T"], d2["T"]):
                pe.sem_inc(st.sem, 1)
            pe.wait_ge(s_wts, 16 * 19)
            mm(pX[:, 0:D], wk_a[:, 0:D], wk_a[:, D:2 * D], start=True, stop=True)
            mm(pY[0:1, 0:D], bconv[:, 0:1], wk_a[:, D:2 * D], start=True, stop=True).then_inc(comp_mm.sem, 1)
            pe.wait_ge(consts, 4)
            keys_f.passed(pe)
            for a in range(4):
                last = pe.transpose(pZ[:, a * ET:(a + 1) * ET], kt[:, a, :], ident[0:ET, 0:ET])
            last.then_inc(keys_T.sem, 1)
            lk_diag.passed(pe)
            mm(pY[0:ET, 512:512 + ET], ones[0:ET, 0:ET], wk_b[0:ET, 0:ET], start=True, stop=True).then_inc(lk_mm.sem, 1)

            cmask0.passed(pe)
            pe.wait_ge(bias_l, 16)
            for a in (0, 1):
                mm(acc[:, a, 0:NT], ZH[:, 0:P], ZH[:, 0:NT], start=True, stop=False, skip_group_check=True)
            with pe.Fori(0, EG // 2) as i:
                for u in (0, 1):
                    q = i * 2 + u
                    wait(pe, gathered[u], i * (16 * G) + (0 * 8 * G * EG + 16 * G))
                    wait(pe, xs["aT"], xs["aT"].prev(q))
                    for k in range(G):
                        last = pe.transpose(pYt[:, k, :], GS[:, u, k, 0:D], ident[:, :])
                    last.then_inc(xs["T"].sem, 1)
                    for k in range(G):
                        t = q * G + k
                        v = (u * G + k) % 2
                        wait(pe, oh, oh.done(t))
                        mm(acc[:, 0, 0:NT], OHP[:, v, 0, :], OHT[:, v, 0, :], start=False, stop=False, skip_group_check=True)
                        mm(acc[:, 1, 0:NT], OHP[:, v, 1, :], OHT[:, v, 1, :], start=False, stop=False, skip_group_check=True)\
                            .then_inc(ohmm.sem, 1)
                    wait(pe, xs["ys"], xs["ys"].prev(q))
                    wait(pe, xs["aT"], xs["aT"].done(q))
                    bias_first(pZ)
                    for k in range(G):
                        last = mm(pZt[:, k, :], scratch(WAT)[:, k, :], wM[:, :], start=False, stop=True, skip_group_check=True)
                    last.then_inc(xs["mm"].sem, 1)
            for a in (0, 1):
                last = mm(acc[:, a, 0:NT], ZH[:, 0:P], ZH[:, 0:NT], start=False, stop=True, skip_group_check=True)
            last.then_inc(ohmm.sem, 1)
            rowtot.passed(pe)
            mm(pY[:, 0:1], tri, cum[:, NT - 1:NT], start=True, stop=True).then_inc(rowoff.sem, 1)

            def p1_mm(q, h, u, to=pX, by_turns=False):
                wait(pe, p1_x[u], h * 16 + 16)
                wait(pe, p1["s"], p1["s"].prev2(q) if by_turns else p1["s"].prev(q))
                bias_first(to)
                for k in range(G):
                    last = mm(tiles(to)[:, k, :], WK[:, u, k * P:(k + 1) * P], wM[:, :], start=False, stop=True, skip_group_check=True)
                last.then_inc(p1["mm"].sem, 1)

            def p1_gram(q):
                wait(pe, p1["xm"], p1["xm"].done(q))
                for k in range(G):
                    last = mm(acc[:, 0, 0:D + 1], XM[:, k, 0:D], XM[:, k, 0:D + 1], start=False, stop=False, skip_group_check=True)
                last.then_inc(p1["gram"].sem, 1)

            def agg_sums(n, q):
                a = q + n * EG
                wait(pe, ag["eqf"], ag["eqf"].done(a))
                wait(pe, ag["aT"], ag["aT"].prev(a))
                wait(pe, ag["m"], ag["m"].done(a))
                for k in range(G):
                    last = mm(pYt[:, k, :], scratch(M)[:, k, :], scratch(EQF)[:, k, :], start=True, stop=True)
                last.then_inc(ag["mmT"].sem, 1)

            def agg_product(n, q, w):
                a = q + n * EG
                wait(pe, ag["p"], ag["p"].prev(a))
                wait(pe, ag["aT"], ag["aT"].done(a))
                for k in range(G):
                    last = mm(pZt[:, k, :], scratch(WAT)[:, k, :], w[:, :], start=True, stop=True)
                last.then_inc(ag["mmP"].sem, 1)

            def agg(n, q, w):
                agg_sums(n, q)
                agg_product(n, q, w)

            def boundary(n, width):
                pe.wait_ge(bd_l, 32 * (n + 1))
                if n == 0:
                    cmask.passed(pe)
                wait(pe, ag["p"], ag["p"].prev((n + 1) * EG))
                mm(pZ[0:ET, 0:width], Cmat[0:ET, :], FR[0:ET, 0:width], start=True, stop=True).then_inc(bd_mm, 1)

            hist_out.passed(pe)
            mm(acc[:, 0, 0:D + 1], ZH[:, 0:P], ZH[:, 0:D + 1], start=True, stop=False, skip_group_check=True)
            mm(acc[0:1, 1, 0:2 * D], ZH[:, 0:1], ZH[:, 0:2 * D], start=True, stop=False, skip_group_check=True)

            def loop_b(q, i, u, more):
                if more:
                    p1_mm(q + 2, i + 1, u, (pX, pY)[u], by_turns=True)
                p1_gram(q)

            p1_mm(0, 0, 0)
            tab_ready.passed(pe)
            p1_mm(1, 0, 1, pY, by_turns=True)
            each_group(pe, loop_b)
            def agg_and_p1(n, w):
                def body(q, i, u, more):
                    agg_sums(n, q)
                    if more:
                        p1_mm(q + ((n + 1) * EG + 2), i + ((n + 1) * (EG // 2) + 1), u)
                    agg_product(n, q, w)
                    if more:
                        p1_gram(q + ((n + 1) * EG + 1))
                p1_mm((n + 1) * EG + 1, (n + 1) * (EG // 2), 1)
                p1_gram((n + 1) * EG)
                each_group(pe, body)

            agg_and_p1(0, wA)
            boundary(0, CW)
            agg_and_p1(1, wL)
            boundary(1, D)
            def feature_transpose(q, h, u):
                wait(pe, s2_ea[u], h * 16 + 16)
                wait(pe, s2["xTc"], s2["xTc"].prev(q))
                for k in range(G):
                    last = pe.transpose(pYt[:, k, :], scratch(10 + u)[:, k, :], ident[:, :])
                last.then_inc(s2["eaT"].sem, 1)

            def loop_e(q, i, u, more):
                wait(pe, s2["eaTc"], s2["eaTc"].done(q))
                wait(pe, s2["x2"], s2["x2"].done(q))
                for k in range(G):
                    last = pe.transpose(pYt[:, k, :], scratch(M)[:, k, :], ident[:, :])
                last.then_inc(s2["xT"].sem, 1)
                if more:
                    p1_mm(q + (3 * EG + 2), i + (3 * (EG // 2) + 1), u)
                wait(pe, s2["sq"], s2["sq"].prev(q))
                wait(pe, s2["xTc"], s2["xTc"].done(q))
                for k in range(G):
                    mm(pZt[:, k, :], scratch(WAT)[:, k, :], w1a[:, :], start=True, stop=False)
                    last = mm(pZt[:, k, :], scratch(AT2)[:, k, :], w1b[:, :], start=False, stop=True)
                last.then_inc(s2["z1"].sem, 1)
                if more:
                    feature_transpose(q + 1, i + u, 1 - u)
                wait(pe, s2["em"], s2["em"].done(q))
                wait(pe, s2["sq"], s2["sq"].done(q))
                hold(pe)
                for k in range(G):
                    mm(acc[0:1, 1, 0:D], EM[:, k:k + 1], Z[:, bass.ds(q * G + k, 1), :].rearrange("p a f -> p (a f)"), start=False, stop=False, skip_group_check=True)
                    last = mm(acc[0:1, 1, D:2 * D], EM[:, k:k + 1], scratch(EQF)[:, k, :], start=False, stop=False, skip_group_check=True)
                last.then_inc(s2["stat"].sem, 1)
                if more:
                    p1_gram(q + (3 * EG + 1))

            p1_mm(3 * EG + 1, 3 * (EG // 2), 1)
            feature_transpose(0, 0, 0)
            p1_gram(3 * EG)
            each_group(pe, loop_e)
            bn_t[0].passed(pe)
            mm(pX[:, 0:2 * D], ones[0:1, :], bnrow[0:1, :, :].rearrange("a b c -> a (b c)"), start=True, stop=True).then_inc(bn_b[0].sem, 1)
            bn_done[0].passed(pe)
            mm(acc[0:1, 1, 0:2 * D], ZH[:, 0:1], ZH[:, 0:2 * D], start=True, stop=False, skip_group_check=True)
            def d1_transpose(q, i, u):
                wait(pe, gathered[u], i * (16 * G) + (4 * 8 * G * EG + 16 * G))
                wait(pe, d1["y"], d1["y"].prev(q))
                for k in range(G):
                    last = pe.transpose(pXt[:, k, :], GS[:, u, k, 0:D], ident[:, :])
                last.then_inc(d1["T"].sem, 1)

            def d1_product(q):
                wait(pe, d1["aT"], d1["aT"].done(q))
                bias_first(pX)
                for k in range(G):
                    last = mm(pXt[:, k, :], scratch(2)[:, k, :], wM[:, :], start=False, stop=True, skip_group_check=True)
                last.then_inc(d1["mm"].sem, 1)

            def loop_f(q, i, u, more):
                agg_sums(2, q)
                if more:
                    d1_transpose(q + 1, i + u, 1 - u)
                agg_product(2, q, w2b)
                if more:
                    d1_product(q + 1)

            d1_transpose(0, 0, 0)
            d1_product(0)
            each_group(pe, loop_f)
            boundary(2, D)
            pe.wait_ge(bd_r, 3)
            def g_transpose(q, h, u):
                wait(pe, d2_x[u], h * 16 + 16)
                wait(pe, d2["z"], d2["z"].prev(q))
                for k in range(G):
                    last = pe.transpose(pXt[:, k, :], scratch(u)[:, k, :], ident[:, :])
                last.then_inc(d2["T"].sem, 1)
                wait(pe, s4["aT"], s4["aT"].prev(q))
                wait(pe, s4["cp"], s4["cp"].done(q))
                for k in range(G):
                    last = pe.transpose(pYt[:, k, :], scratch(M)[:, k, :], ident[:, :])
                last.then_inc(s4["T"].sem, 1)

            def loop_g(q, i, u, more):
                wait(pe, d2["aT"], d2["aT"].done(q))
                for k in range(G):
                    last = mm(pXt[:, k, :], scratch(2)[:, k, :], w2a[:, :], start=True, stop=True)
                last.then_inc(d2["mm"].sem, 1)
                wait(pe, s4["z"], s4["z"].prev(q))
                wait(pe, s4["aT"], s4["aT"].done(q))
                for k in range(G):
                    last = mm(pZt[:, k, :], scratch(WAT)[:, k, :], w2a[:, :], start=True, stop=True)
                last.then_inc(s4["mm"].sem, 1)
                if more:
                    g_transpose(q + 1, i + u, 1 - u)
                wait(pe, d2["em"], d2["em"].done(q))
                wait(pe, d2["sq"], d2["sq"].done(q))
                for k in range(G):
                    mm(acc[0:1, 1, 0:D], EM[:, k:k + 1], scratch(5 if u == 0 else 10)[:, k, :], start=False, stop=False, skip_group_check=True)
                    last = mm(acc[0:1, 1, D:2 * D], EM[:, k:k + 1], scratch(EQF)[:, k, :], start=False, stop=False, skip_group_check=True)
                last.then_inc(d2["stat"].sem, 1)

            g_transpose(0, 0, 0)
            each_group(pe, loop_g)
            gr.passed(pe)
            mm(pX[:, 0:D], GM[:, 0:D], w2a[:, :], start=True, stop=True)
            mm(pX[0:1, 512:512 + D], GM[:, D:D + 1], w2a[:, :], start=True, stop=True).then_inc(gr_mm.sem, 1)
            gr_p.passed(pe)
            mm(pY[0:1, 0:D], ones[:, 0:1], GP, start=True, stop=True).then_inc(gr_q.sem, 1)
            bn_t[1].passed(pe)
            mm(pX[:, 0:2 * D], ones[0:1, :], bnrow[0:1, :, :].rearrange("a b c -> a (b c)"), start=True, stop=True).then_inc(bn_b[0].sem, 1)
            bn_done[1].passed(pe)

            def p2_transpose(q, h, u):
                wait(pe, p2_x[u], h * 16 + 16)
                wait(pe, p2["xT"], p2["xT"].prev(q))
                for k in range(G):
                    last = pe.transpose(pXt[:, k, :], scratch(u)[:, k, :], ident[:, :])
                last.then_inc(p2["T"].sem, 1)

            def p2_product(q):
                wait(pe, p2["s"], p2["s"].prev(q))
                wait(pe, p2["xT"], p2["xT"].done(q))
                bias_first(pW)
                for k in range(G):
                    last = mm(pWt[:, k, :], scratch(2)[:, k, :], w2s[:, :], start=False, stop=True, skip_group_check=True)
                last.then_inc(p2["mm"].sem, 1)

            def p2_group(q, h, u):
                p2_product(q + 2)
                p2_transpose(q + 3, h, u)

            p2_transpose(0, 0, 0)
            pe.wait_ge(bias_l, 32)
            p2_product(0)
            p2_transpose(1, 0, 1)
            p2_product(1)
            p2_transpose(2, 1, 0)
            def loop_h(q, i, u, more):
                agg_sums(3, q)
                if more:
                    p2_group(q + 1, i + 2, u)
                agg_product(3, q, w3)

            p2_group(0, 1, 1)
            each_group(pe, loop_h)
            boundary(3, D)
            with pe.Fori(0, EG // 2) as i:
                for u in (0, 1):
                    q = i * 2 + u
                    for n in range(3):
                        r = (q * 3) + (EG + n)
                        p2_group(r, i * 3 + (EG // 2 + (3 * u + n + 3) // 2), (u + n + 1) % 2)

        @block.scalar
        def _(act):
            A = act.activation

            def square_sums(src_t, junk, ss, st):
                for k in range(G):
                    last = A(junk[:, k, 0:D], src_t[:, k, :], ACT.Square, accum_out=ss[:, k:k + 1])
                last.then_inc(st.sem, 1)

            def p1_first(q, u, of=pX):
                wait(act, p1["xm"], p1["xm"].prev2(q))
                wait(act, p1["sqrt"], p1["sqrt"].prev(q))
                wait(act, p1["mm"], p1["mm"].done(q))
                hold(act)
                square_sums(tiles(of), scratch(2 + u), SS1, p1["sq"])
                wait(act, p1["sq"], p1["sq"].done(q))
                wait(act, p1["r"], p1["r"].prev(q))
                hold(act)
                A(SD1, SS1, ACT.Sqrt, bias=eps_ln[:, 0:1], scale=1.0 / D).then_inc(p1["sqrt"].sem, 1)

            def p1_second(q, u):
                wait(act, p1["gram"], p1["gram"].prev(q))
                wait(act, p1["sqrt2"], p1["sqrt2"].prev(q))
                wait(act, p1["s"], p1["s"].done(q))
                hold(act)
                square_sums(scratch(2 + u), XM, SS2, p1["sq2"])
                wait(act, p1["sq2"], p1["sq2"].done(q))
                wait(act, p1["r2"], p1["r2"].prev(q))
                hold(act)
                A(SD2, SS2, ACT.Sqrt, bias=eps_ln[:, 0:1], scale=1.0 / D).then_inc(p1["sqrt2"].sem, 1)

            def agg_eq(n, q):
                a = q + n * EG
                wait(act, ag["mmT"], ag["mmT"].prev(a))
                hold(act)
                A(scratch(EQF), EQ[:, span(q), :], ACT.Copy).then_inc(ag["eqf"].sem, 1)

            def agg_sums(n, q):
                a = q + n * EG
                wait(act, ag["mmP"], ag["mmP"].prev(a))
                wait(act, ag["mmT"], ag["mmT"].done(a))
                hold(act)
                A(scratch(WAT), pYt, ACT.Copy).then_inc(ag["aT"].sem, 1)

            def agg_rows(n, q, i, u):
                a = q + n * EG
                wait(act, ag_st[u], (i + n * (EG // 2)) * 16)
                wait(act, ag["mmP"], ag["mmP"].done(a))
                if n == 0:
                    wait(act, ag["cnt"], ag["cnt"].done(a))
                hold(act)
                A(PT[:, u, :, 0:D], pZt, ACT.Copy).then_inc(ag["p"].sem, 1)

            def agg(n, q, i, u):
                agg_sums(n, q)
                agg_rows(n, q, i, u)

            for st in (xs["raw"], p2["o"]):
                act.sem_inc(st.sem, 1)
            with act.Fori(0, EG // 2) as i:
                for u in (0, 1):
                    q = i * 2 + u
                    wait(act, gathered[u], i * (16 * G) + (0 * 8 * G * EG + 16 * G))
                    hold(act)
                    A(Z[:, span(q), :], GS[:, u, :, 0:D], ACT.Copy).then_inc(xs["raw"].sem, 1)
                    wait(act, xs["mm"], xs["mm"].prev(q))
                    wait(act, xs["T"], xs["T"].done(q))
                    hold(act)
                    A(scratch(WAT), pYt, ACT.Copy).then_inc(xs["aT"].sem, 1)
                    wait(act, xs["mm"], xs["mm"].done(q))
                    hold(act)
                    A(YS[:, span(q), :], pZt, ACT.Copy).then_inc(xs["ys"].sem, 1)
            comp_ready.passed(act)
            act.wait_ge(tab_stored, 16)
            p1_first(0, 0)
            with act.Fori(0, EG // 2) as i:
                for u in (0, 1):
                    q = i * 2 + u
                    p1_first(q + 1, 1 - u, (pY, pX)[u])
                    p1_second(q, u)
            ns_in.passed(act)
            A(NS[:, :], RR, ACT.Sqrt).then_inc(ns_sq.sem, 1)
            ns_ready.passed(act)
            def loop_c(q, i, u, more):
                if more:
                    p1_second(q + (EG + 1), 1 - u)
                agg_sums(0, q)
                if more:
                    wait(act, ag["cnt"], ag["cnt"].done(q))
                    agg_eq(0, q + 1)
                agg_rows(0, q, i, u)
                if more:
                    p1_first(q + (EG + 2), u)

            agg_eq(0, 0)
            p1_second(EG, 0)
            p1_first(EG + 1, 1)
            each_group(act, loop_c)

            def s1_degree(q):
                wait(act, s1["y"], s1["y"].prev(q))
                wait(act, s1["rc"], s1["rc"].done(q))
                hold(act)
                A(ND[:, span(q)], RC[:, span(q)], ACT.Sqrt).then_inc(s1["nd"].sem, 1)

            def s1_norm(q):
                wait(act, ag["mmT"], ag["mmT"].prev(q + EG))
                wait(act, s1["y"], s1["y"].done(q))
                hold(act)
                for k in range(G):
                    last = A(scratch(M)[:, k, :], YS[:, bass.ds(q * G + k, 1), :].rearrange("p a f -> p (a f)"), ACT.Square, accum_out=SS3[:, k:k + 1])
                last.then_inc(s1["sq"].sem, 1)
                wait(act, s1["r"], s1["r"].prev(q))
                wait(act, s1["sq"], s1["sq"].done(q))
                hold(act)
                A(SD3, SS3, ACT.Sqrt, bias=eps_ln[:, 0:1], scale=1.0 / D).then_inc(s1["sqrt"].sem, 1)

            def loop_d(q, i, u, more):
                if more:
                    p1_second(q + (2 * EG + 1), 1 - u)
                    s1_degree(q + 1)
                agg_sums(1, q)
                if more:
                    p1_first(q + (2 * EG + 2), u)
                agg_rows(1, q, i, u)
                if more:
                    agg_eq(1, q + 1)
                    s1_norm(q + 1)

            p1_second(2 * EG, 0)
            s1_degree(0)
            p1_first(2 * EG + 1, 1)
            agg_eq(1, 0)
            s1_norm(0)
            each_group(act, loop_d)
            def s2_first(q):
                wait(act, s2["r"], s2["r"].prev(q))
                wait(act, s2["ag"], s2["ag"].done(q))
                hold(act)
                A(SD3, MVS[:, :, 1], ACT.Sqrt, bias=eps_ln[:, 0:1], scale=1.0).then_inc(s2["sqrt"].sem, 1)
                wait(act, s2["z1"], s2["z1"].prev(q))
                wait(act, s2["eaT"], s2["eaT"].done(q))
                hold(act)
                A(scratch(AT2), pYt, ACT.Copy).then_inc(s2["eaTc"].sem, 1)

            def loop_e(q, i, u, more):
                wait(act, s2["x2"], s2["x2"].done(q))
                hold(act)
                A(YS[:, span(q), :], scratch(M), ACT.Copy).then_inc(s2["keep"].sem, 1)
                wait(act, s2["xT"], s2["xT"].done(q))
                hold(act)
                A(scratch(WAT), pYt, ACT.Copy).then_inc(s2["xTc"].sem, 1)
                if more:
                    p1_second(q + (3 * EG + 1), 1 - u)
                wait(act, s2["z1"], s2["z1"].done(q))
                wait(act, s2["stat"], s2["stat"].prev(q))
                hold(act)
                A(Z[:, span(q), :], pZt, ACT.Copy).then_inc(s2["zc"].sem, 1)
                A(scratch(EQF), pZt, ACT.Square).then_inc(s2["sq"].sem, 1)
                if more:
                    s2_first(q + 1)
                    p1_first(q + (3 * EG + 2), u)

            p1_second(3 * EG, 0)
            s2_first(0)
            p1_first(3 * EG + 1, 1)
            each_group(act, loop_e)
            bn_v[0].passed(act)
            A(rt[:, 3, :], rt[:, 2, :], ACT.Sqrt).then_inc(bn_a[0].sem, 1)
            bn_done[0].passed(act)
            def f_first(q):
                agg_eq(2, q)
                wait(act, h1["s1"], h1["s1"].prev(q))
                wait(act, h1["v"], h1["v"].done(q))
                hold(act)
                A(scratch(10), scratch(9), ACT.Exp).then_inc(h1["exp"].sem, 1)
                A(sc[:, 6:7], eps_ln[:, 0:1], ACT.Sqrt)

            def d1_copy(q):
                wait(act, d1["mm"], d1["mm"].prev(q))
                wait(act, d1["T"], d1["T"].done(q))
                hold(act)
                A(scratch(2), pXt, ACT.Copy).then_inc(d1["aT"].sem, 1)

            def loop_f(q, i, u, more):
                wait(act, d1["x1"], d1["x1"].prev(q))
                wait(act, d1["rc"], d1["rc"].done(q))
                hold(act)
                A(NDD, RCD[:, span(q)], ACT.Sqrt).then_inc(d1["nd"].sem, 1)
                wait(act, d1["y"], d1["y"].done(q))
                hold(act)
                square_sums(scratch(4), scratch(5), SS3, d1["sq"])
                wait(act, d1["sq"], d1["sq"].done(q))
                hold(act)
                A(SD3, SS3, ACT.Sqrt, bias=eps_ln[:, 0:1], scale=1.0 / D).then_inc(d1["sqrt"].sem, 1)
                agg_sums(2, q)
                if more:
                    d1_copy(q + 1)
                agg_rows(2, q, i, u)
                wait(act, d1["r2"], d1["r2"].prev(q))
                wait(act, d1["ag"], d1["ag"].done(q))
                hold(act)
                A(SD2, MVS[:, :, 1], ACT.Sqrt, bias=eps_ln[:, 0:1], scale=1.0).then_inc(d1["sqrt2"].sem, 1)
                if more:
                    f_first(q + 1)

            f_first(0)
            d1_copy(0)
            each_group(act, loop_f)
            def g_keep(q):
                wait(act, s4["T"], s4["T"].prev(q))
                hold(act)
                A(scratch(M), YS[:, span(q), :], ACT.Copy).then_inc(s4["cp"].sem, 1)

            def g_copy(q):
                wait(act, d2["mm"], d2["mm"].prev(q))
                wait(act, d2["T"], d2["T"].done(q))
                hold(act)
                A(scratch(2), pXt, ACT.Copy).then_inc(d2["aT"].sem, 1)
                wait(act, s4["mm"], s4["mm"].prev(q))
                wait(act, s4["T"], s4["T"].done(q))
                hold(act)
                A(scratch(WAT), pYt, ACT.Copy).then_inc(s4["aT"].sem, 1)

            def loop_g(q, i, u, more):
                if more:
                    g_keep(q + 1)
                wait(act, d2["stat"], d2["stat"].prev(q))
                wait(act, d2["z"], d2["z"].done(q))
                hold(act)
                A(scratch(EQF), scratch(5 if u == 0 else 10), ACT.Square).then_inc(d2["sq"].sem, 1)
                if more:
                    g_copy(q + 1)

            g_keep(0)
            g_copy(0)
            each_group(act, loop_g)
            bn_v[1].passed(act)
            A(rt[:, 3, :], rt[:, 2, :], ACT.Sqrt).then_inc(bn_a[0].sem, 1)
            bn_done[1].passed(act)

            def p2_copy(q):
                wait(act, p2["mm"], p2["mm"].prev(q))
                wait(act, p2["T"], p2["T"].done(q))
                hold(act)
                A(scratch(2), pXt, ACT.Copy).then_inc(p2["xT"].sem, 1)

            def p2_exp(q):
                wait(act, p2["s"], p2["s"].prev(q))
                wait(act, p2["mm"], p2["mm"].done(q))
                hold(act)
                A(scratch(3), pWt, ACT.Relu, scale=-1.0).then_inc(p2["neg"].sem, 1)
                wait(act, p2["neg"], p2["neg"].done(q))
                hold(act)
                A(scratch(3), scratch(3), ACT.Exp, scale=-1.0).then_inc(p2["exp"].sem, 1)

            def p2_square(q, h, u):
                wait(act, p2_st[u], h * 16)
                wait(act, inv, inv.done(q))
                wait(act, p2["u"], p2["u"].done(q))
                hold(act)
                for k in range(G):
                    last = A(GS[:, u, k, 0:D], scratch(10 + u)[:, k, :], ACT.Square, bias=NB[:, G + k:G + k + 1], scale=1.0,
                             accum_out=SS1[:, k:k + 1])
                last.then_inc(p2["sq"].sem, 1)

            def norm_rows(out_, rows_, n, st):
                for k in range(G):
                    last = A(out_(k), rows_(k), ACT.Identity, bias=NB[:, n * G + k:n * G + k + 1], scale=RS[:, n * G + k:n * G + k + 1])
                last.then_inc(st.sem, 1)

            def p2_out(q, u):
                wait(act, p2["sq"], p2["sq"].done(q))
                wait(act, inv, inv.done(q + 1))
                hold(act)
                norm_rows(lambda k: GS[:, u, k, 0:D], lambda k: scratch(10 + u)[:, k, :], 2, p2["o"])

            act.wait_ge(bias_st, 32)
            p2_copy(0)
            p2_exp(0)
            p2_copy(1)
            p2_exp(1)
            p2_copy(2)
            def s5_exp(q):
                wait(act, s5["s"], s5["s"].prev(q))
                wait(act, s5["v"], s5["v"].done(q))
                hold(act)
                A(XM[:, :, 0:D], scratch(9), ACT.Exp).then_inc(s5["exp"].sem, 1)

            def loop_h(q, i, u, more):
                if more:
                    s5_exp(q + 1)
                agg_sums(3, q)
                if more:
                    agg_eq(3, q + 1)
                    p2_square(q + 1, i + u, 1 - u)
                agg_rows(3, q, i, u)
                if more:
                    p2_exp(q + 3)
                    p2_copy(q + 4)
                    p2_out(q + 1, 1 - u)

            agg_eq(3, 0)
            s5_exp(0)
            p2_square(0, 0, 0)
            p2_exp(2)
            p2_copy(3)
            p2_out(0, 0)
            each_group(act, loop_h)
            def i_step(q, i, u, n, before=lambda: None, after=lambda: None):
                r, h, v = q * 3 + (EG + n), i * 3 + (EG // 2 + (3 * u + n) // 2), (u + n) % 2
                before()
                p2_square(r, h, v)
                p2_exp(r + 2)
                p2_copy(r + 3)
                after()
                p2_out(r, v)

            def d3_out(q):
                wait(act, inv, inv.done(q * 3 + (EG + 2) + 1))
                hold(act)
                norm_rows(lambda k: YS[:, bass.ds(q * G + k, 1), :].rearrange("p a f -> p (a f)"), lambda k: XM[:, k, 0:D], 3, d3["o"])

            def d3_exp(q):
                wait(act, d3["u"], d3["u"].prev(q))
                wait(act, d3["v"], d3["v"].done(q))
                hold(act)
                A(scratch(9), scratch(7), ACT.Exp).then_inc(d3["exp"].sem, 1)

            def loop_i(q, i, u, more):
                i_step(q, i, u, 2)
                if more:
                    i_step(q + 1, i + u, 1 - u, 0)
                    i_step(q + 1, i + u, 1 - u, 1, lambda: d3_exp(q + 1), lambda: d3_out(q))
                else:
                    d3_out(q)

            i_step(0, 0, 0, 0)
            i_step(0, 0, 0, 1, lambda: d3_exp(0))
            each_group(act, loop_i)

        @block.vector
        def _(dve):
            chain = [0]

            def link(ins):
                chain[0] += 1
                ins.then_inc(vlink, 1)
                dve.wait_ge(vlink, chain[0])

            ts, tt, stt = dve.tensor_scalar, dve.tensor_tensor, dve.scalar_tensor_tensor

            def row(t, q, k):
                return t[:, bass.ds(q * G + k, 1), :].rearrange("p a f -> p (a f)")

            def col(t, q, k):
                return t[:, bass.ds(q * G + k, 1)]

            for st in (lk_use, eq_built, p1["xm"], s1["y"], s2["s"], s4["z"], d2["z"]):
                dve.sem_inc(st.sem, 1)
            dve.memset(ones[:, :], 1.0)
            dve.memset(ones3[:, :], 1.0)
            dve.memset(MV[:, :, :, :], 0.0)
            dve.memset(eps_ln[:, :], LN_EPS)
            dve.memset(ZH[:, :], 0.0)
            dve.memset(PT[:, :, :, :], 0.0)
            dve.memset(ones_t, 1.0)
            dve.memset(Cmat[:, :], 0.0)
            dve.memset(XM[:, :, :], 0.0).then_inc(zeros.sem, 1)
            zeros.passed(dve)
            dve.wait_ge(s_keys, 64)
            dve.tensor_copy(kt[:, 0:3, :], kti[:, 0:3, :]).then_inc(keys_f.sem, 1)
            dve.wait_ge(consts, 4)
            dve.tensor_copy(iota_h, iota_i)
            dve.tensor_copy(sc[:, 1:2], sc[:, 0:1].bitcast(i32))
            keys_T.passed(dve)
            dve.tensor_copy(KD[:, :], pZ[:, 0:ET])
            dve.tensor_copy(KP, pZ[:, ET:2 * ET])
            dve.tensor_copy(KS, pZ[:, 2 * ET:3 * ET])
            link(dve.tensor_copy(WE[:, :], pZ[:, 3 * ET:4 * ET]))
            dve.tensor_copy(SRCI[:, :], KS)
            dve.tensor_copy(DSTI[:, :], KD[:, :]).then_inc(idx_ready.sem, 1)
            for key, p_, t_ in ((KD[:, :], PD, TD), (KS, PS_, TS_)):
                link(ts(p_, key, -(NT - 1) / 2.0, 1.0 / NT, ALU.add, ALU.mult))
                link(ts(p_, p_, ROUND, None, ALU.add))
                link(ts(p_, p_, -ROUND, None, ALU.add))
                link(stt(out=t_, in0=p_, scalar=-float(NT), in1=key, op0=ALU.mult, op1=ALU.add))
            link(ts(REAL[:, :], KD[:, :], float(NODES), None, ALU.is_lt))
            link(tt(REP[:, :], KD[:, :], KP, ALU.not_equal))
            link(tt(REP[:, :], REP[:, :], REAL[:, :], ALU.mult))
            link(ts(RC[:, :], REP[:, :], -NOWHERE, NOWHERE, ALU.mult, ALU.add))
            link(tt(RC[:, :], RC[:, :], KD[:, :], ALU.add))
            dve.tensor_copy(OUTI[:, :], RC[:, :])
            dve.wait_ge(s_wts, 16 * 19)

            def split(row_):
                link(dve.tensor_copy(parts[:, 0, :], row_))
                link(tt(rest, row_, parts[:, 0, :], ALU.subtract))
                link(dve.tensor_copy(parts[:, 1, :], rest))
                link(tt(rest, rest, parts[:, 1, :], ALU.subtract))
                link(dve.tensor_copy(parts[:, 2, :], rest))

            def centre(w, rows_, scratch_col):
                link(dve.tensor_reduce(scratch_col, w, axis=AX.X, op=ALU.add))
                link(ts(scratch_col, scratch_col, 1.0 / D, None, ALU.mult))
                link(ts(w, w, scratch_col, None, ALU.subtract))

            link(tt(wM[:, :], wM[:, :], ident[:, :], ALU.add))
            centre(wM[:, :], P, sc[:, 2:3])
            comp_mm.passed(dve)
            link(dve.tensor_copy(wA[:, :], pX[:, 0:D]))
            centre(wA[:, :], P, sc[:, 2:3])
            link(tt(b0row, pY[0:1, 0:D], rows[:, 6, :], ALU.add))
            centre(b0row, 1, sc[0:1, 2:3])
            link(ts(cB[:, :], blB[:, :], 0.0, None, ALU.max))
            centre(cB[:, :], P, sc[:, 2:3])
            centre(b3B[:, :], P, sc[:, 2:3])
            split(b0row)
            dve.sem_inc(comp_ready.sem, 1)
            link(ts(wk_b[0:ET, 0:ET], ident[0:ET, 0:ET], kt[:, 0, P - 1:P], None, ALU.mult))
            dve.sem_inc(lk_diag.sem, 1)
            lk_mm.passed(dve)
            ts(Cmat[0:ET, :], pY[0:ET, 512:512 + ET], kt[:, 0, 0:1], None, ALU.is_equal).then_inc(cmask0.sem, 1)
            link(ts(wk_a[0:ET, 0:P], kt[:, 0, :], kt[:, 0, P - 1:P], None, ALU.is_equal))
            link(dve.tensor_reduce(sc[0:ET, 2:3], wk_a[0:ET, 0:P], axis=AX.X, op=ALU.add))
            link(ts(sc[0:ET, 3:4], sc[0:ET, 2:3], float(P), None, ALU.is_ge))
            link(ts(sc[0:ET, 4:5], kt[:, 1, 0:1], kt[:, 0, P - 1:P], None, ALU.is_equal))
            link(tt(sc[0:ET, 3:4], sc[0:ET, 3:4], sc[0:ET, 4:5], ALU.mult))
            link(tt(sc[0:ET, 1:2], sc[0:ET, 1:2], sc[0:ET, 2:3], ALU.subtract))
            link(stt(out=sc[0:ET, 1:2], in0=sc[0:ET, 3:4], scalar=NOWHERE, in1=sc[0:ET, 1:2], op0=ALU.mult, op1=ALU.add))
            link(dve.tensor_copy(REPI[0:ET, :], sc[0:ET, 1:2]))

            with dve.Fori(0, EG // 2) as i:
                for u in (0, 1):
                    q = i * 2 + u
                    for k in range(G):
                        t = q * G + k
                        v = (u * G + k) % 2
                        wait(dve, ohmm, ohmm.prev2(t))
                        ts(OHP[:, v, 0, :], iota_h[:, 0:P], PD[:, bass.ds(t, 1)], None, ALU.is_equal)
                        ts(OHT[:, v, 0, :], iota_h[:, 0:NT], TD[:, bass.ds(t, 1)], None, ALU.is_equal)
                        ts(OHP[:, v, 1, :], iota_h[:, 0:P], PS_[:, bass.ds(t, 1)], None, ALU.is_equal)
                        ts(OHT[:, v, 1, :], iota_h[:, 0:NT], TS_[:, bass.ds(t, 1)], None, ALU.is_equal).then_inc(oh.sem, 1)
            wait(dve, ohmm, ohmm.prev(ET + 1))
            wait(dve, xs["ys"], xs["ys"].prev(EG))
            dve.tensor_copy(degout, acc[:, 1, 0:NT])
            link(dve.tensor_copy(deg, acc[:, 0, 0:NT]))
            dve.sem_inc(hist_out.sem, 1)
            link(dve.tensor_tensor_scan(cum, ones_t, deg, 0.0, ALU.mult, ALU.add))
            dve.sem_inc(rowtot.sem, 1)
            rowoff.passed(dve)
            link(dve.tensor_copy(sc[:, 5:6], pY[:, 0:1]))
            link(tt(posn, cum, deg, ALU.subtract))
            link(ts(posn, posn, sc[:, 5:6], None, ALU.add))
            link(ts(MASK[:, :], deg, 0.0, None, ALU.is_equal))
            link(ts(cum, posn, -1.0, float(ZERO_ROW), ALU.mult, ALU.add))
            link(tt(cum, cum, MASK[:, :], ALU.mult))
            dve.tensor_copy(tabs[:, :, 0], degout)
            link(tt(tabs[:, :, 1], posn, cum, ALU.add))
            dve.sem_inc(tab_ready.sem, 1)
            mask1.passed(dve)

            def invert(st, q, r, sd, after):
                wait(dve, after, after.done(q))
                dve.reciprocal(r, sd).then_inc(st.sem, 1)

            def p1_first(q, u, of=pX):
                wait(dve, p1["s"], p1["s"].prev(q))
                invert(p1["r"], q, R1, SD1, p1["sqrt"])
                wait(dve, p1["r"], p1["r"].done(q))
                for k in range(G):
                    last = stt(out=scratch(2 + u)[:, k, :], in0=tiles(of)[:, k, :], scalar=R1[:, k:k + 1], in1=cB[:, :],
                               op0=ALU.mult, op1=ALU.add)
                last.then_inc(p1["s"].sem, 1)

            def p1_second(q, h, u):
                wait(dve, p1["xm"], p1["xm"].prev(q))
                invert(p1["r2"], q, R2, SD2, p1["sqrt2"])
                wait(dve, p1_st[u], h * 16)
                wait(dve, p1["r2"], p1["r2"].done(q))
                tt(RM, R2, MASK[:, span(q)], ALU.mult).then_inc(p1["rm"].sem, 1)
                for k in range(G):
                    last = ts(scratch(4 + u)[:, k, :], scratch(2 + u)[:, k, :], R2[:, k:k + 1], None, ALU.mult)
                last.then_inc(p1["x2"].sem, 1)
                wait(dve, p1["rm"], p1["rm"].done(q))
                hold(dve)
                dve.tensor_copy(XM[:, :, D], MASK[:, span(q)])
                for k in range(G):
                    last = ts(XM[:, k, 0:D], scratch(2 + u)[:, k, :], RM[:, k:k + 1], None, ALU.mult)
                last.then_inc(p1["xm"].sem, 1)

            def p1_this(n, q, i, u):
                p1_second(q + n * EG, i + n * (EG // 2), u)

            def p1_next(n, q, u):
                p1_first(q + (n * EG + 1), 1 - u)

            def boundary(n, width):
                dve.wait_ge(bd_mm, n + 1)
                tt(LR[0:ET, 0:width], LR[0:ET, 0:width], pZ[0:ET, 0:width], ALU.add).then_inc(bd_r, 1)

            p1_first(0, 0)
            with dve.Fori(0, EG // 2) as i:
                for u in (0, 1):
                    q = i * 2 + u
                    wait(dve, gathered[u], i * (16 * G) + (1 * 8 * G * EG + 16 * G))
                    hold(dve)
                    dve.tensor_copy(LK[:, span(q), :], GS[:, u, :, 0:2]).then_inc(lk_use.sem, 1)
                    wait(dve, rk_l[u], i * 16 + 16)
                    for k in range(G):
                        last = ts(row(EQ, q, k), WK[:, 10 + u, k * P:(k + 1) * P].bitcast(i32), col(KD, q, k), None, ALU.is_equal)
                    last.then_inc(eq_built.sem, 1)
                    p1_first(q + 1, 1 - u, (pY, pX)[u])
                    p1_this(0, q, i, u)
            wait(dve, eq_built, eq_built.prev(EG))
            wait(dve, lk_use, lk_use.prev(EG))
            dve.memset(EQ[:, ET - 1, LASTROWS:P], 0.0)
            dve.tensor_copy(POSI[:, :], LK[:, :, 1])
            link(ts(RR, LK[:, :, 0], 1.0, None, ALU.max))
            link(dve.reciprocal(RR, RR))
            dve.sem_inc(ns_in.sem, 1)
            ns_sq.passed(dve)
            dve.sem_inc(ns_ready.sem, 1)
            with dve.Fori(0, EG // 2) as i:
                for u in (0, 1):
                    q = i * 2 + u
                    p1_this(1, q, i, u)
                    wait(dve, ag["mmT"], ag["mmT"].prev(q))
                    for k in range(G):
                        last = ts(scratch(M)[:, k, :], row(Z, q, k), col(NS, q, k), None, ALU.mult)
                    last.then_inc(ag["m"].sem, 1)
                    wait(dve, ag_st[u], i * 16)
                    wait(dve, ag["eqf"], ag["eqf"].done(q))
                    dve.tensor_reduce(PT[:, u, :, D], scratch(EQF), axis=AX.X, op=ALU.add).then_inc(ag["cnt"].sem, 1)
                    p1_next(1, q, u)
            boundary(0, CW)
            with dve.Fori(0, EG // 2) as i:
                for u in (0, 1):
                    q = i * 2 + u
                    wait(dve, gathered[u], i * (16 * G) + (2 * 8 * G * EG + 16 * G))
                    ts(CS, GS[:, u, :, D], 1.0, None, ALU.max).then_inc(s1["c"].sem, 1)
                    wait(dve, s1["c"], s1["c"].done(q))
                    hold(dve)
                    dve.reciprocal(RC[:, span(q)], CS).then_inc(s1["rc"].sem, 1)
                    p1_this(2, q, i, u)
                    wait(dve, s1["nd"], s1["nd"].done(q))
                    for k in range(G):
                        last = stt(out=row(YS, q, k), in0=GS[:, u, k, 0:D], scalar=col(ND, q, k), in1=row(YS, q, k),
                                   op0=ALU.mult, op1=ALU.add)
                    last.then_inc(s1["y"].sem, 1)
                    p1_next(2, q, u)
                    wait(dve, ag["m"], ag["m"].prev(q + EG))
                    invert(s1["r"], q, R3, SD3, s1["sqrt"])
                    wait(dve, s1["r"], s1["r"].done(q))
                    tt(RW, R3, NS[:, span(q)], ALU.mult).then_inc(s1["rw"].sem, 1)
                    wait(dve, s1["rw"], s1["rw"].done(q))
                    for k in range(G):
                        last = ts(scratch(M)[:, k, :], row(YS, q, k), RW[:, k:k + 1], None, ALU.mult)
                    last.then_inc(ag["m"].sem, 1)
                    wait(dve, ag["m"], ag["m"].done(q + EG))
                    for k in range(G):
                        last = ts(row(YS, q, k), row(YS, q, k), R3[:, k:k + 1], None, ALU.mult)
                    last.then_inc(s1["x1"].sem, 1)
            boundary(1, D)

            def moments(st_bn, rows_, n):
                for k in range(G):
                    last = dve.bn_stats(ST[:, n, k, :], rows_(k))
                last.then_inc(st_bn.sem, 1)

            def mean_var(st_bn, st_ag, q, n):
                wait(dve, st_bn, st_bn.done(q))
                hold(dve)
                for k in range(G):
                    last = dve.bn_aggr(MV[:, n, k, :], ST[:, n, k, :])
                last.then_inc(st_ag.sem, 1)

            def stats(st_bn, st_ag, q, rows_, n):
                moments(st_bn, rows_, n)
                mean_var(st_bn, st_ag, q, n)

            def inverse_roots(c, a, b, *after):
                cols = slice(a * G, b * G)
                use = [slice(m * G, (m + 1) * G) for m in range(4)]
                mv = MV[:, :, :, :].rearrange("p n k c -> p (n k) c")
                v, y, t = RV[:, cols], RS[:, cols], RT[:, cols]
                bits = y.bitcast(i32)
                n = [0]

                def then(ins, last=False):
                    by = CHAIN - n[0] if last else 1
                    n[0] += by
                    ins.then_inc(inv.sem, by)
                    wait(dve, inv, inv.at(c, n[0]))

                def minus_mean(part):
                    return stt(out=NB[:, part], in0=mv[:, part, 0], scalar=-1.0, in1=RS[:, part], op0=ALU.mult, op1=ALU.mult)

                for st, value in after:
                    wait(dve, st, value)
                then(ts(v, mv[:, cols, 1], LN_EPS, None, ALU.add))
                if b > 2:
                    then(ts(RV[:, use[2]], SS1, 1.0 / D, LN_EPS, ALU.mult, ALU.add))
                then(ts(bits, v.bitcast(i32), 1, None, ALU.logical_shift_right))
                then(ts(bits, bits, -1.0, SEED, ALU.mult, ALU.add))
                for _ in range(NEWTON):
                    then(tt(t, y, y, ALU.mult))
                    then(stt(out=t, in0=t, scalar=-0.5, in1=v, op0=ALU.mult, op1=ALU.mult))
                    then(stt(out=y, in0=t, scalar=1.5, in1=y, op0=ALU.add, op1=ALU.mult))
                if b > 2:
                    then(tt(NB[:, use[2]], NB[:, use[1]], RS[:, use[2]], ALU.mult))
                if b > 3:
                    then(minus_mean(use[3]))
                then(minus_mean(slice(a * G, 2 * G)), last=True)

            def norm(out_, rows_, mean, r, st):
                for k in range(G):
                    last = ts(out_[:, k, :], rows_(k), mean[:, k, 0:1], r[:, k:k + 1], ALU.subtract, ALU.mult)
                last.then_inc(st.sem, 1)

            with dve.Fori(0, EG // 2) as i:
                for u in (0, 1):
                    q = i * 2 + u
                    wait(dve, gathered[u], i * (16 * G) + (3 * 8 * G * EG + 16 * G))
                    for k in range(G):
                        last = stt(out=GS[:, u, k, 0:D], in0=GS[:, u, k, 0:D], scalar=col(ND, q, k), in1=blB[:, :],
                                   op0=ALU.mult, op1=ALU.add)
                    last.then_inc(s2["a"].sem, 1)
                    wait(dve, s2["a"], s2["a"].done(q))
                    stt(out=GS[:, u, :, 0:D], in0=GS[:, u, :, 0:D], scalar=0.0, in1=YS[:, span(q), :],
                        op0=ALU.max, op1=ALU.add).then_inc(s2["a2"].sem, 1)
                    wait(dve, s2["a2"], s2["a2"].done(q))
                    hold(dve)
                    stats(s2["bn"], s2["ag"], q, lambda k: GS[:, u, k, 0:D], 0)
                    p1_this(3, q, i, u)
                    invert(s2["r"], q, R3, SD3, s2["sqrt"])
                    wait(dve, s2["keep"], s2["keep"].prev(q))
                    wait(dve, s2["xT"], s2["xT"].prev(q))
                    wait(dve, s2["r"], s2["r"].done(q))
                    norm(scratch(M), lambda k: GS[:, u, k, 0:D], MVS, R3, s2["x2"])
                    wait(dve, s2["stat"], s2["stat"].prev(q))
                    wait(dve, s2["x2"], s2["x2"].done(q))
                    hold(dve)
                    dve.tensor_copy(EM, REAL[:, span(q)]).then_inc(s2["em"].sem, 1)
                    dve.sem_inc(s2["s"].sem, 1)
                    p1_next(3, q, u)

            def batch_norm(n, sums, count, b, gamma, beta, to):
                link(ts(rt[:, 0:2, :], sums, 1.0 / count, None, ALU.mult))
                link(tt(rt[:, 2, :], rt[:, 0, :], rt[:, 0, :], ALU.mult))
                link(tt(rt[:, 2, :], rt[:, 1, :], rt[:, 2, :], ALU.subtract))
                link(ts(rt[:, 2, :], rt[:, 2, :], 0.0, BN_EPS, ALU.max, ALU.add))
                dve.sem_inc(bn_v[0].sem, 1)
                bn_a[n - 1].passed(dve)
                link(dve.reciprocal(rt[:, 4, :], rt[:, 3, :]))
                link(tt(bnrow[:, 0, :], rt[:, 4, :], gamma, ALU.mult))
                link(tt(rt[:, 0, :], rt[:, 0, :], b, ALU.add))
                link(tt(rt[:, 0, :], b, rt[:, 0, :], ALU.subtract))
                link(tt(rt[:, 0, :], rt[:, 0, :], bnrow[:, 0, :], ALU.mult))
                link(tt(bnrow[:, 1, :], rt[:, 0, :], beta, ALU.add))
                dve.sem_inc(bn_t[0].sem, 1)
                bn_b[n - 1].passed(dve)
                link(dve.tensor_copy(to.rearrange("p a f -> p (a f)"), pX[:, 0:2 * D]))

            wait(dve, s2["stat"], s2["stat"].prev(EG))
            wait(dve, p1["s"], p1["s"].prev(NG + 1))
            batch_norm(1, acc[0:1, 1, 0:2 * D].rearrange("a (r f) -> a r f", r=2), EDGES, rows[:, 0, :], rows[:, 1, :], rows[:, 2, :], bn1B[:, :, :])
            dve.sem_inc(bn_done[0].sem, 1)
            with dve.Fori(0, EG // 2) as i:
                for u in (0, 1):
                    q = i * 2 + u
                    wait(dve, h1["exp"], h1["exp"].done(q))
                    ts(scratch(10), scratch(10), 1.0, -1.0, ALU.min, ALU.add).then_inc(h1["t"].sem, 1)
                    wait(dve, ag["mmT"], ag["mmT"].prev(q + 2 * EG))
                    wait(dve, h1["t"], h1["t"].done(q))
                    stt(out=scratch(M), in0=scratch(9), scalar=0.0, in1=scratch(10), op0=ALU.max, op1=ALU.add).then_inc(h1["s1"].sem, 1)
                    wait(dve, h1["s1"], h1["s1"].done(q))
                    dve.sem_inc(ag["m"].sem, 1)
                    wait(dve, d1_p, q * 32 + 32)
                    ts(CS, XM[:, :, D], 1.0, None, ALU.max).then_inc(d1["c"].sem, 1)
                    wait(dve, d1["c"], d1["c"].done(q))
                    hold(dve)
                    dve.reciprocal(RCD[:, span(q)], CS).then_inc(d1["rc"].sem, 1)
                    wait(dve, d1["nd"], d1["nd"].done(q))
                    wait(dve, d1["x2"], d1["x2"].prev(q))
                    wait(dve, d1["mm"], d1["mm"].done(q))
                    for k in range(G):
                        last = stt(out=scratch(4)[:, k, :], in0=XM[:, k, 0:D], scalar=NDD[:, k:k + 1], in1=pXt[:, k, :], op0=ALU.mult, op1=ALU.add)
                    last.then_inc(d1["y"].sem, 1)
                    for k in range(G):
                        last = stt(out=scratch(1)[:, k, :], in0=scratch(1)[:, k, :], scalar=NDD[:, k:k + 1], in1=blB[:, :], op0=ALU.mult, op1=ALU.add)
                    last.then_inc(d1["a"].sem, 1)
                    invert(d1["r"], q, R3, SD3, d1["sqrt"])
                    wait(dve, d1["r"], d1["r"].done(q))
                    for k in range(G):
                        last = ts(scratch(4)[:, k, :], scratch(4)[:, k, :], R3[:, k:k + 1], None, ALU.mult)
                    last.then_inc(d1["x1"].sem, 1)
                    wait(dve, d1["x1"], d1["x1"].done(q))
                    stt(out=scratch(4), in0=scratch(1), scalar=0.0, in1=scratch(4), op0=ALU.max, op1=ALU.add).then_inc(d1["s"].sem, 1)
                    wait(dve, d1["s"], d1["s"].done(q))
                    stats(d1["bn"], d1["ag"], q, lambda k: scratch(4)[:, k, :], 0)
                    invert(d1["r2"], q, R2, SD2, d1["sqrt2"])
                    wait(dve, d1_st, q * 16)
                    wait(dve, d1["r2"], d1["r2"].done(q))
                    norm(scratch(3), lambda k: scratch(4)[:, k, :], MVS, R2, d1["x2"])
            boundary(2, D)
            with dve.Fori(0, EG // 2) as i:
                for u in (0, 1):
                    q = i * 2 + u
                    zslot = scratch(5 if u == 0 else 10)
                    wait(dve, d2_p[u], i * 16 + 16)
                    wait(dve, d2_st[u], i * 16)
                    wait(dve, d2["mm"], d2["mm"].done(q))
                    for k in range(G):
                        last = stt(out=zslot[:, k, :], in0=scratch(3 + u)[:, k, :], scalar=col(RCD, q, k), in1=pXt[:, k, :], op0=ALU.mult, op1=ALU.add)
                    last.then_inc(d2["z"].sem, 1)
                    wait(dve, d2["stat"], d2["stat"].prev(q))
                    hold(dve)
                    dve.tensor_copy(EM, REP[:, span(q)]).then_inc(d2["em"].sem, 1)
                    wait(dve, gathered[u], i * (16 * G) + (5 * 8 * G * EG + 16 * G))
                    wait(dve, s4["mm"], s4["mm"].done(q))
                    for k in range(G):
                        last = stt(out=row(Z, q, k), in0=GS[:, u, k, 0:D], scalar=col(RC, q, k), in1=pZt[:, k, :], op0=ALU.mult, op1=ALU.add)
                    last.then_inc(s4["z"].sem, 1)
            wait(dve, p1["gram"], p1["gram"].prev(NG))
            wait(dve, s4["T"], s4["T"].prev(EG))
            link(dve.tensor_copy(GM, acc[:, 0, 0:D + 1]))
            dve.sem_inc(gr.sem, 1)
            gr_mm.passed(dve)
            link(tt(GP, pX[:, 0:D], w2a[:, :], ALU.mult))
            dve.sem_inc(gr_p.sem, 1)
            gr_q.passed(dve)
            wait(dve, d2["stat"], d2["stat"].prev(EG))
            link(dve.tensor_copy(rt[:, 0:2, :], acc[0:1, 1, 0:2 * D].rearrange("a (r f) -> a r f", r=2)))
            link(tt(rt[:, 0, :], rt[:, 0, :], pX[0:1, 512:512 + D], ALU.add))
            link(tt(rt[:, 1, :], rt[:, 1, :], pY[0:1, 0:D], ALU.add))
            batch_norm(2, rt[:, 0:2, :], NODES, rows[:, 3, :], rows[:, 4, :], rows[:, 5, :], bn2B[:, :, :])
            link(tt(w2s[:, :], w2a[:, :], bn2B[:, 0, :], ALU.mult))
            split(bnrow[:, 1, :])
            dve.sem_inc(bn_done[0].sem, 1)

            def p2_first(q, u, beside=()):
                steps = list(beside) + [lambda: None] * 2
                wait(dve, p2["t"], p2["t"].done(q))
                stt(out=scratch(4 + u), in0=pWt, scalar=0.0, in1=scratch(3), op0=ALU.max, op1=ALU.add).then_inc(p2["s"].sem, 1)
                steps[0]()
                wait(dve, p2["s"], p2["s"].done(q))
                moments(p2["bn"], lambda k: scratch(4 + u)[:, k, :], 1)
                steps[1]()
                mean_var(p2["bn"], p2["ag"], q, 1)
                for step_ in steps[2:]:
                    step_()

            def p2_last(q, u):
                wait(dve, p2["o"], p2["o"].prev2(q))
                for k in range(G):
                    last = stt(out=scratch(10 + u)[:, k, :], in0=scratch(4 + u)[:, k, :], scalar=RS[:, G + k:G + k + 1], in1=b3B[:, :],
                               op0=ALU.mult, op1=ALU.add)
                last.then_inc(p2["u"].sem, 1)

            def p2_roots(q, a, b, *after):
                inverse_roots(q + 1, a, b, (p2["sq"], p2["sq"].done(q)), (p2["ag"], p2["ag"].done(q + 1)),
                              (p2["o"], p2["o"].prev(q)), (p2["u"], p2["u"].done(q)), *after)

            p2_first(0, 0)
            inverse_roots(0, 1, 2, (p2["ag"], p2["ag"].done(0)))
            with dve.Fori(0, EG // 2) as i:
                for u in (0, 1):
                    q = i * 2 + u
                    p2_last(q, u)

                    def elu_low():
                        wait(dve, s5["exp"], s5["exp"].done(q))
                        stt(out=XM[:, :, 0:D], in0=XM[:, :, 0:D], scalar=1.0, in1=YS[:, span(q), :], op0=ALU.min, op1=ALU.add).then_inc(s5["t"].sem, 1)

                    def elu_high():
                        wait(dve, s5["t"], s5["t"].done(q))
                        stt(out=XM[:, :, 0:D], in0=scratch(9), scalar=0.0, in1=XM[:, :, 0:D], op0=ALU.max, op1=ALU.add).then_inc(s5["s1"].sem, 1)

                    def elu_stats():
                        wait(dve, s5["s1"], s5["s1"].done(q))
                        stats(s5["bn"], s5["ag"], q, lambda k: XM[:, k, 0:D], 0)

                    p2_first(q + 1, 1 - u, (elu_low, elu_high, elu_stats))
                    p2_roots(q, 0, 3, (s5["ag"], s5["ag"].done(q)))
                    tt(RW, RS[:, 0:G], WE[:, span(q)], ALU.mult).then_inc(s5["rw"].sem, 1)
                    wait(dve, ag["mmT"], ag["mmT"].prev(q + 3 * EG))
                    wait(dve, s5["rw"], s5["rw"].done(q))
                    norm(scratch(M), lambda k: XM[:, k, 0:D], MVS, RW, ag["m"])
                    wait(dve, ag["m"], ag["m"].done(q + 3 * EG))
                    dve.sem_inc(s5["s"].sem, 1)
            boundary(3, D)
            with dve.Fori(0, EG // 2) as i:
                for u in (0, 1):
                    q = i * 2 + u
                    r = q * 3 + EG
                    p2_last(r, u)
                    p2_first(r + 1, 1 - u)
                    p2_roots(r, 1, 3)
                    p2_last(r + 1, 1 - u)

                    def elu_low():
                        wait(dve, d3["exp"], d3["exp"].done(q))
                        stt(out=scratch(9), in0=scratch(9), scalar=1.0, in1=scratch(6), op0=ALU.min, op1=ALU.add).then_inc(d3["t"].sem, 1)

                    def elu_high():
                        wait(dve, d3["t"], d3["t"].done(q))
                        stt(out=scratch(9), in0=scratch(7), scalar=0.0, in1=scratch(9), op0=ALU.max, op1=ALU.add).then_inc(d3["s"].sem, 1)

                    def elu_stats():
                        wait(dve, d3["s"], d3["s"].done(q))
                        stats(d3["bn"], d3["ag"], q, lambda k: scratch(9)[:, k, :], 0)

                    p2_first(r + 2, u, (elu_low, elu_high, elu_stats))
                    p2_roots(r + 1, 0, 3, (d3["ag"], d3["ag"].done(q)))
                    wait(dve, d3["o"], d3["o"].prev(q))
                    for k in range(G):
                        last = stt(out=XM[:, k, 0:D], in0=scratch(9)[:, k, :], scalar=RS[:, k:k + 1], in1=b3B[:, :], op0=ALU.mult, op1=ALU.add)
                    last.then_inc(d3["u"].sem, 1)
                    p2_last(r + 2, u)

                    def sum_moments():
                        wait(dve, d3["u2"], d3["u2"].done(q))
                        moments(d3["bn2"], lambda k: XM[:, k, 0:D], 3)

                    p2_first(r + 3, 1 - u, (lambda: None, sum_moments))
                    mean_var(d3["bn2"], d3["ag2"], q, 3)
                    p2_roots(r + 2, 1, 4, (d3["ag2"], d3["ag2"].done(q)))



def kernel(x, src, dst, edge_attr_128, edge_weight, L0_gnn_W_conv, L0_gnn_b_conv, L0_gnn_W_aggr, L0_gnn_b_aggr,
           L1_gnn_weight, L1_gnn_bias, L2_gnn_u, L2_gnn_W1, L2_gnn_b1, L2_gnn_g1, L2_gnn_be1, L2_gnn_W2, L2_gnn_b2,
           L2_gnn_g2, L2_gnn_be2, L3_gnn_W, L3_gnn_b):
    from concourse import bacc
    from concourse.bass_utils import run_bass_kernel_spmd

    x = np.asarray(x)
    src, dst, ea, w = (np.asarray(a) for a in (src, dst, edge_attr_128, edge_weight))
    xp = np.zeros((NPAD, D), x.dtype)
    xp[:NODES] = x
    xT = np.zeros((NG + 2, D, G * P), x.dtype)
    xT[:NG] = xp.reshape(P, NG, G, D).transpose(1, 3, 2, 0).reshape(NG, D, G * P)
    dst1 = np.full((EPAD + 1,), NPAD - 1, dst.dtype)
    dst1[0] = -1
    dst1[1:EDGES + 1] = dst
    srcp = np.full((EPAD,), NPAD - 1, src.dtype)
    srcp[:EDGES] = src
    wp = np.zeros((EPAD,), w.dtype)
    wp[:EDGES] = w
    eap = np.zeros((EPAD, D), ea.dtype)
    eap[:EDGES] = ea
    ins = dict(x=xp, xT=xT, edge_attr=eap, dst1=dst1, src=srcp, weight=wp,
               W_conv_T=np.ascontiguousarray(np.asarray(L0_gnn_W_conv).T), b_conv=L0_gnn_b_conv, W_aggr=L0_gnn_W_aggr,
               b_aggr=L0_gnn_b_aggr, W_l1=L1_gnn_weight, b_l1=L1_gnn_bias, W1=L2_gnn_W1, b1=L2_gnn_b1, g1=L2_gnn_g1,
               be1=L2_gnn_be1, W2=L2_gnn_W2, b2=L2_gnn_b2, g2=L2_gnn_g2, be2=L2_gnn_be2,
               W3_T=np.ascontiguousarray(np.asarray(L3_gnn_W).T), b3=L3_gnn_b)
    ins = {k: np.ascontiguousarray(np.asarray(v)) for k, v in ins.items()}
    nc = bacc.Bacc("TRN2", target_bir_lowering=False, num_devices=1)
    aps = {k: nc.dram_tensor("in_" + k, v.shape, mybir.dt.from_np(v.dtype), kind="ExternalInput").ap() for k, v in ins.items()}
    out = nc.dram_tensor("out", (NPAD, D), mybir.dt.float32, kind="ExternalOutput").ap()
    build(nc, out=out, **aps)
    r = run_bass_kernel_spmd(nc, [{"in_" + k: v for k, v in ins.items()}], core_ids=[0])
    return r.results[0]["out"][:NODES]
```
